# Optimizing a Trainium2 kernel written in Bass

```python
import numpy as np
import jax
import jax.numpy as jnp

def _softmax(x, axis=-1):
    return jax.nn.softmax(x, axis=axis)

def _gelu(x):
    return jax.nn.gelu(x, approximate=True)

def _silu(x):
    return jax.nn.silu(x)

def _sigmoid(x):
    return jax.nn.sigmoid(x)

def _layernorm(x, axis=-1, eps=1e-05):
    m = jnp.mean(x, axis=axis, keepdims=True)
    v = jnp.var(x, axis=axis, keepdims=True)
    return (x - m) / jnp.sqrt(v + eps)

def _scatter_add(tgt, idx, src, axis=0):
    return tgt.at[idx].add(src)

def _segment_sum(src, seg, n):
    return jax.ops.segment_sum(src, seg, n)
kernel_name = 'mk_gnn_resnorm_d4_gnn_r32_3aa79d'

def setup_inputs(seed: int=0):
    np.random.seed(seed)
    _w = jnp.asarray

    def _rec_inputs():
        import jax
        import jax.numpy as jnp
        _gk = jax.random.key(seed)
        x = -0.000256 + 0.5003 * jax.random.normal(jax.random.fold_in(_gk, 1), (3125, 64), jnp.float32)
        _s = jax.random.randint(jax.random.fold_in(_gk, 2), (50000,), 0, 3125, jnp.int32)
        _d = jax.random.randint(jax.random.fold_in(_gk, 3), (50000,), 0, 3125, jnp.int32)
        _loop = jnp.arange(3125, dtype=jnp.int32)
        src = jnp.concatenate([_s, _d, _loop])
        dst = jnp.concatenate([_d, _s, _loop])
        _o = jnp.argsort(dst, stable=True)
        src = src[_o]
        dst = dst[_o]
        edge_type_8 = jax.random.randint(jax.random.fold_in(_gk, 13), (103125,), 0, 8, jnp.int32)
        return (x, src, dst, edge_type_8)
    x, src, dst, edge_type_8 = _rec_inputs()

    def _L0_gnn_setup():
        import jax, jax.numpy as jnp
        import numpy as np
        C = 0.01
        EPS = 1e-06
        MIN_NORM = 1e-10
        N_NODES = 50000
        N_EDGES = 12500
        IN_FEAT = 64
        OUT_FEAT = 64
        NUM_RELS = 8
        NUM_HEADS = 4
        SQRT_C = np.sqrt(C).astype(np.float32)

        def project_to_ball(x, c=C):
            norm = jnp.maximum(jnp.linalg.norm(x, axis=-1, keepdims=True), MIN_NORM)
            maxnorm = (1.0 - 1e-05) / np.sqrt(c)
            return jnp.where(norm > maxnorm, x * (maxnorm / norm), x)

        def log_map_zero(x, c=C):
            norm = jnp.maximum(jnp.linalg.norm(x, axis=-1, keepdims=True), MIN_NORM)
            t = jnp.clip(np.sqrt(c) * norm, MIN_NORM, 1.0 - 1e-05)
            return jnp.arctanh(t) * x / t

        def exp_map_zero(v, c=C):
            norm = jnp.maximum(jnp.linalg.norm(v, axis=-1, keepdims=True), MIN_NORM)
            t = np.sqrt(c) * norm
            return jnp.tanh(t) * v / t

        def mobius_add(x, y, c=C):
            xy = jnp.sum(x * y, axis=-1, keepdims=True)
            x2 = jnp.sum(x * x, axis=-1, keepdims=True)
            y2 = jnp.sum(y * y, axis=-1, keepdims=True)
            num = (1.0 + 2.0 * c * xy + c * y2) * x + (1.0 - c * x2) * y
            den = 1.0 + 2.0 * c * xy + c ** 2 * x2 * y2
            return num / jnp.maximum(den, MIN_NORM)

        def leaky_relu(x, slope=0.2):
            return jnp.where(x > 0, x, slope * x)
        key = jax.random.key(seed)
        k1, k2, k3, k4, k5, k6, k7 = jax.random.split(key, 7)
        h = jax.random.normal(k1, (N_NODES, IN_FEAT), dtype=jnp.float32) * 0.5
        h = project_to_ball(h)
        rel_weight = jax.random.normal(k2, (NUM_RELS, NUM_HEADS, IN_FEAT, OUT_FEAT), dtype=jnp.float32) * 0.125
        attn_vec = jax.random.normal(k3, (NUM_RELS, NUM_HEADS, OUT_FEAT), dtype=jnp.float32) * 0.125
        rel_emb = jax.random.normal(k4, (NUM_RELS, IN_FEAT), dtype=jnp.float32) * 0.1
        src = jax.random.randint(k5, (N_EDGES,), 0, N_NODES, dtype=jnp.int32)
        dst = jax.random.randint(k6, (N_EDGES,), 0, N_NODES, dtype=jnp.int32)
        etype = jax.random.randint(k7, (N_EDGES,), 0, NUM_RELS, dtype=jnp.int32)
        return {'h_hyper': h, 'rel_weight': rel_weight, 'attn_vec': attn_vec, 'rel_emb': rel_emb, 'src': src, 'dst': dst, 'etype': etype}
    _L0_gnn_all = _L0_gnn_setup()
    _L0_gnn_in = {k: v for k, v in _L0_gnn_all.items() if k in ('rel_weight', 'attn_vec', 'rel_emb')}
    del _L0_gnn_all

    def _L1_gnn_setup():
        import jax, jax.numpy as jnp
        import numpy as np
        N_NODES = 3125
        N_EDGES = 100000
        D = 64
        key = jax.random.key(seed)
        k1, k2, k3, k4, k5 = jax.random.split(key, 5)
        x = jax.random.normal(k1, (N_NODES, D), dtype=jnp.float32)
        src = jax.random.randint(k2, (N_EDGES,), 0, N_NODES, dtype=jnp.int64)
        dst = jax.random.randint(k3, (N_EDGES,), 0, N_NODES, dtype=jnp.int64)
        W = jax.random.normal(k4, (D, D), dtype=jnp.float32) / np.sqrt(D)
        b = jax.random.normal(k5, (D,), dtype=jnp.float32) * 0.01
        return {'x': x, 'src': src, 'dst': dst, 'W': W, 'b': b}
    _L1_gnn_all = _L1_gnn_setup()
    _L1_gnn_in = {k: v for k, v in _L1_gnn_all.items() if k in ('W', 'b')}
    del _L1_gnn_all

    def _L2_gnn_setup():
        import jax, jax.numpy as jnp
        import numpy as np
        N_NODES = 3125
        N_EDGES = 1250000
        D_FEAT = 64
        UNITS = 64
        key = jax.random.key(seed)
        k1, k2, k3 = jax.random.split(key, 3)
        features = jax.random.normal(k1, (N_NODES, D_FEAT), dtype=jnp.float32)
        edge_index = jax.random.randint(k2, (2, N_EDGES), 0, N_NODES, dtype=jnp.int64)
        weight = jax.random.normal(k3, (D_FEAT, UNITS), dtype=jnp.float32) * (1.0 / np.sqrt(D_FEAT))
        bias = jnp.zeros((UNITS,), dtype=jnp.float32)
        return {'features': features, 'edge_index': edge_index, 'weight': weight, 'bias': bias}
    _L2_gnn_all = _L2_gnn_setup()
    _L2_gnn_in = {k: v for k, v in _L2_gnn_all.items() if k in ('weight', 'bias')}
    del _L2_gnn_all

    def _L3_gnn_setup():
        import jax, jax.numpy as jnp
        import numpy as np
        key = jax.random.key(seed)
        k1, k2, k3 = jax.random.split(key, 3)
        N_SRC, N_DST, E, D = (3125, 3125, 50000, 64)
        h = jax.random.normal(k1, (N_SRC, D), dtype=jnp.float32)
        src_idx = jax.random.randint(k2, (E,), 0, N_SRC, dtype=jnp.int32)
        dst_idx = jax.random.randint(k3, (E,), 0, N_DST, dtype=jnp.int32)
        return {'h': h, 'src_idx': src_idx, 'dst_idx': dst_idx, 'num_src': N_SRC, 'num_dst': N_DST}
    _L3_gnn_all = _L3_gnn_setup()
    _L3_gnn_in = {k: v for k, v in _L3_gnn_all.items() if k in ()}
    del _L3_gnn_all
    return {'x': x, 'src': src, 'dst': dst, 'edge_type_8': edge_type_8, 'L0_gnn_rel_weight': _L0_gnn_in['rel_weight'], 'L0_gnn_attn_vec': _L0_gnn_in['attn_vec'], 'L0_gnn_rel_emb': _L0_gnn_in['rel_emb'], 'L1_gnn_W': _L1_gnn_in['W'], 'L1_gnn_b': _L1_gnn_in['b'], 'L2_gnn_weight': _L2_gnn_in['weight'], 'L2_gnn_bias': _L2_gnn_in['bias']}

def reference(x, src, dst, edge_type_8, L0_gnn_rel_weight, L0_gnn_attn_vec, L0_gnn_rel_emb, L1_gnn_W, L1_gnn_b, L2_gnn_weight, L2_gnn_bias):
    import jax
    import jax.numpy as jnp

    def _L0_gnn_ref(h_hyper, rel_weight, attn_vec, rel_emb, src, dst, etype):
        import jax, jax.numpy as jnp
        import numpy as np
        C = 0.01
        EPS = 1e-06
        MIN_NORM = 1e-10
        N_NODES = 50000
        N_EDGES = 12500
        IN_FEAT = 64
        OUT_FEAT = 64
        NUM_RELS = 8
        NUM_HEADS = 4
        SQRT_C = np.sqrt(C).astype(np.float32)

        def project_to_ball(x, c=C):
            norm = jnp.maximum(jnp.linalg.norm(x, axis=-1, keepdims=True), MIN_NORM)
            maxnorm = (1.0 - 1e-05) / np.sqrt(c)
            return jnp.where(norm > maxnorm, x * (maxnorm / norm), x)

        def log_map_zero(x, c=C):
            norm = jnp.maximum(jnp.linalg.norm(x, axis=-1, keepdims=True), MIN_NORM)
            t = jnp.clip(np.sqrt(c) * norm, MIN_NORM, 1.0 - 1e-05)
            return jnp.arctanh(t) * x / t

        def exp_map_zero(v, c=C):
            norm = jnp.maximum(jnp.linalg.norm(v, axis=-1, keepdims=True), MIN_NORM)
            t = np.sqrt(c) * norm
            return jnp.tanh(t) * v / t

        def mobius_add(x, y, c=C):
            xy = jnp.sum(x * y, axis=-1, keepdims=True)
            x2 = jnp.sum(x * x, axis=-1, keepdims=True)
            y2 = jnp.sum(y * y, axis=-1, keepdims=True)
            num = (1.0 + 2.0 * c * xy + c * y2) * x + (1.0 - c * x2) * y
            den = 1.0 + 2.0 * c * xy + c ** 2 * x2 * y2
            return num / jnp.maximum(den, MIN_NORM)

        def leaky_relu(x, slope=0.2):
            return jnp.where(x > 0, x, slope * x)
        E = src.shape[0]
        N = h_hyper.shape[0]
        R, H, din, dh = rel_weight.shape
        h_t = log_map_zero(h_hyper)
        h_src_t = h_t[src]
        msg_t = jnp.zeros((E, H, dh), dtype=h_hyper.dtype)
        for r in range(R):
            xr = jnp.where((etype == r)[:, None], h_src_t, 0.0)
            msg_t = msg_t + jnp.einsum('ei,hio->eho', xr, rel_weight[r])
        msg_h = exp_map_zero(msg_t)
        diff = mobius_add(h_hyper[src], -h_hyper[dst])
        diff_t = log_map_zero(diff)
        av = attn_vec[etype]
        score = leaky_relu(jnp.einsum('ed,ehd->eh', diff_t, av))
        m = jax.ops.segment_max(score, dst, num_segments=N)
        ex = jnp.exp(score - m[dst])
        denom = jax.ops.segment_sum(ex, dst, num_segments=N)
        alpha = ex / denom[dst]
        nsq = jnp.sum(msg_h * msg_h, axis=-1)
        lam = 2.0 / (1.0 - C * nsq + EPS)
        w = alpha * lam
        num = jax.ops.segment_sum(w[..., None] * msg_h, dst, num_segments=N)
        den = jax.ops.segment_sum(w, dst, num_segments=N) + EPS
        mid = project_to_ball(num / den[..., None])
        agg_t = jnp.mean(log_map_zero(mid), axis=1)
        h_new = exp_map_zero(agg_t)
        return h_new

    def _L1_gnn_ref(x, src, dst, W, b):
        import jax, jax.numpy as jnp
        import numpy as np
        N_NODES = 3125
        N_EDGES = 100000
        D = 64
        n = x.shape[0]
        ones = jnp.ones_like(src, dtype=x.dtype)
        deg_out = jax.ops.segment_sum(ones, src, num_segments=n)
        deg_in = jax.ops.segment_sum(ones, dst, num_segments=n)
        norm_out = jnp.where(deg_out > 0, jax.lax.rsqrt(jnp.maximum(deg_out, 1.0)), 0.0)
        norm_in = jnp.where(deg_in > 0, jax.lax.rsqrt(jnp.maximum(deg_in, 1.0)), 0.0)
        h = x * norm_out[:, None] @ W
        msgs = jnp.take(h, src, axis=0)
        agg = jax.ops.segment_sum(msgs, dst, num_segments=n)
        return agg * norm_in[:, None] + b

    def _L2_gnn_ref(features, edge_index, weight, bias):
        import jax, jax.numpy as jnp
        import numpy as np
        N_NODES = 3125
        N_EDGES = 1250000
        D_FEAT = 64
        UNITS = 64
        num_nodes = features.shape[0]
        row = edge_index[0]
        col = edge_index[1]
        ones = jnp.ones(row.shape[0], dtype=features.dtype)
        degrees = jax.ops.segment_sum(ones, row, num_segments=num_nodes)
        deg_inv_sqrt = jnp.power(degrees, -0.5)
        deg_inv_sqrt = jnp.where(jnp.isfinite(deg_inv_sqrt), deg_inv_sqrt, 0.0)
        w = deg_inv_sqrt[row] * deg_inv_sqrt[col]
        msgs = features[col] * w[:, None]
        propagated = jax.ops.segment_sum(msgs, row, num_segments=num_nodes)
        h = propagated @ weight + bias
        return jax.nn.relu(h)

    def _L3_gnn_ref(h, src_idx, dst_idx, num_src, num_dst):
        import jax, jax.numpy as jnp
        import numpy as np
        ones = jnp.ones(src_idx.shape[0], dtype=h.dtype)
        out_deg = jnp.clip(jax.ops.segment_sum(ones, src_idx, num_segments=num_src), 1.0)
        in_deg = jnp.clip(jax.ops.segment_sum(ones, dst_idx, num_segments=num_dst), 1.0)
        norm_src = out_deg ** (-1.0)
        norm_dst = in_deg ** (-1.0)
        feat_src = h * norm_src[:, None]
        msgs = feat_src[src_idx]
        rst = jax.ops.segment_sum(msgs, dst_idx, num_segments=num_dst)
        return rst * norm_dst[:, None]
    edge_index = jnp.stack([src, dst])
    x = _layernorm(x + _L0_gnn_ref(x, L0_gnn_rel_weight, L0_gnn_attn_vec, L0_gnn_rel_emb, src, dst, edge_type_8), axis=-1)
    x = _layernorm(x + _L1_gnn_ref(x, src, dst, L1_gnn_W, L1_gnn_b), axis=-1)
    x = _layernorm(x + _L2_gnn_ref(x, edge_index, L2_gnn_weight, L2_gnn_bias), axis=-1)
    x = _layernorm(x + _L3_gnn_ref(x, src, dst, 3125, 3125), axis=-1)
    return x

_drawn_inputs = setup_inputs


def setup_inputs(seed=0):
    import zlib

    import numpy as np

    out = dict(_drawn_inputs(seed))
    spreads = {'L2_gnn_bias': (0.0, 0.1)}
    factors = {'L1_gnn_b': 4.939}
    for name, (base, spread) in spreads.items():
        noise = np.random.default_rng([zlib.crc32(name.encode()), seed]).standard_normal(out[name].shape)
        drawn = base * np.exp(spread * noise) if base else spread * noise
        out[name] = jnp.asarray(drawn.astype(out[name].dtype))
    for name, factor in factors.items():
        out[name] = (out[name] * factor).astype(out[name].dtype)
    return out
```

```python
from contextlib import ExitStack

import concourse.bass as bass
from concourse import mybir

P = 128
F32 = mybir.dt.float32
F16 = mybir.dt.float16
BF16 = mybir.dt.bfloat16
I32 = mybir.dt.int32
ALU = mybir.AluOpType
ACT = mybir.ActivationFunctionType
X = mybir.AxisListType.X

N, D = 3125, 64
E = 103125
R, H = 8, 4
NT = -(-N // P)
FULL = N // P
REST = N - FULL * P
NP = NT * P

PAIR = 2 * P
PAIR_ROWS = 405
EP = PAIR_ROWS * PAIR
WIN = 8
WINS = -(-N // WIN)
BLOCKS = EP // P

PI, PC = 107, 4
ITEMS = PI * PC
COLS = 2 * ITEMS
CI, CC = 100, 12
CITEMS = CI * CC
assert ITEMS >= -(-E // PAIR) + NT - 1 and ITEMS - (NT - 1) < PAIR_ROWS + 1
assert CITEMS >= -(-E // P) + WINS - 1 and CITEMS - 1 - (WINS - 1) < BLOCKS

NODE = D + 1 + R * H
HEAD = D + 2
MSG = H * HEAD
OUTC = MSG + 1
PAD_DST = 4000.0
C = 0.01
T_MAX = 1.0 - 1e-05
MAXNORM = (1.0 - 1e-05) / 0.1


def wait(eng, sem, value):
    eng.wait_ge(sem, value)
    eng.nop(nofuse=True)


def chain(eng, sem, start=0):
    count = [start]

    def step(ins):
        count[0] += 1
        ins.then_inc(sem, 1)
        eng.wait_ge(sem, count[0])
        return ins
    return step


class Scope:
    def __init__(self, nc, name):
        self.nc, self.name, self.ctx = nc, name, ExitStack()

    def __enter__(self):
        return self

    def __exit__(self, *a):
        return self.ctx.__exit__(*a)

    def sb(self, name, shape, dt=F32):
        return self.ctx.enter_context(self.nc.sbuf_tensor(f"{self.name}_{name}", shape, dt))

    def ps(self, name, shape, dt=F32):
        return self.ctx.enter_context(self.nc.psum_tensor(f"{self.name}_{name}", shape, dt))

    def sem(self, name):
        return self.ctx.enter_context(self.nc.semaphore(f"{self.name}_{name}"))

    def block(self):
        return self.ctx.enter_context(self.nc.Block())


def atanh_ratio_vector(v, eng, n2, t, w1, w2, out, n2_ready, norm_ready, ratio_ready, log_ready, k):
    v(eng.tensor_scalar(n2, n2, 1e-20, None, ALU.max))
    eng.sem_inc(n2_ready, 1)
    eng.wait_ge(norm_ready, k)
    v(eng.tensor_scalar(t, t, 0.1, 1e-10, ALU.mult, ALU.max))
    v(eng.tensor_scalar(t, t, T_MAX, None, ALU.min))
    v(eng.tensor_scalar(w1, t, -1.0, 1.0, ALU.mult, ALU.add))
    v(eng.reciprocal(w2, w1))
    v(eng.scalar_tensor_tensor(w1, t, 1.0, w2, ALU.add, ALU.mult))
    eng.sem_inc(ratio_ready, 1)
    v(eng.tensor_tensor(w2, t, t, ALU.mult))
    v(eng.tensor_scalar(out, w2, 1.0 / 9, 1.0 / 7, ALU.mult, ALU.add))
    v(eng.tensor_tensor(out, out, w2, ALU.mult))
    v(eng.scalar_tensor_tensor(out, out, 1.0 / 5, w2, ALU.add, ALU.mult))
    v(eng.scalar_tensor_tensor(out, out, 1.0 / 3, w2, ALU.add, ALU.mult))
    v(eng.tensor_scalar(out, out, 1.0, None, ALU.add))
    v(eng.reciprocal(w2, t))
    eng.wait_ge(log_ready, k)
    v(eng.scalar_tensor_tensor(w1, w1, 0.5, w2, ALU.mult, ALU.mult))
    v(eng.tensor_tensor(out, out, w1, ALU.subtract))
    v(eng.scalar_tensor_tensor(out, t, 0.1, out, ALU.is_lt, ALU.mult))
    v(eng.tensor_tensor(out, out, w1, ALU.add))


def atanh_ratio_scalar(eng, n2, t, w1, n2_ready, norm_ready, ratio_ready, log_ready, k):
    eng.wait_ge(n2_ready, k)
    eng.activation(t, n2, ACT.Sqrt).then_inc(norm_ready, 1)
    eng.wait_ge(ratio_ready, k)
    eng.activation(w1, w1, ACT.Ln).then_inc(log_ready, 1)


def layer_norm_vector(v, eng, x, sq, st, var_ready, root_ready, k):
    mean, var = st[:, 0, :], st[:, 1, :]
    bc = lambda a: a.unsqueeze(2).to_broadcast([P, NT, D])
    v(eng.tensor_reduce(mean, x, X, ALU.add))
    v(eng.tensor_scalar(mean, mean, 1.0 / D, None, ALU.mult))
    v(eng.tensor_tensor(x, x, bc(mean), ALU.subtract))
    v(eng.tensor_tensor(sq, x, x, ALU.mult))
    v(eng.tensor_reduce(var, sq, X, ALU.add))
    v(eng.tensor_scalar(var, var, 1.0 / D, 1e-05, ALU.mult, ALU.add))
    eng.sem_inc(var_ready, 1)
    eng.wait_ge(root_ready, k)
    v(eng.reciprocal(mean, var))
    v(eng.tensor_tensor(x, x, bc(mean), ALU.mult))


def layer_norm_scalar(eng, st, var_ready, root_ready, k):
    eng.wait_ge(var_ready, k)
    eng.activation(st[:, 1, :], st[:, 1, :], ACT.Sqrt).then_inc(root_ready, 1)


def constants(nc, g):
    with Scope(nc, "const") as s:
        filled, made = s.sem("filled"), s.sem("made")
        block = s.block()

        @block.gpsimd
        def _(pool):
            pool.memset(g.ident[:], 0.0).then_inc(filled, 1)
            pool.wait_ge(filled, 1)
            pool.affine_select(out=g.ident[:], in_=g.ident[:], compare_op=ALU.not_equal, fill=1.0, base=0,
                               pattern=[[-1, P]], channel_multiplier=1).then_inc(made, 1)
            pool.iota(g.count[:], [[1, P]], base=0, channel_multiplier=0,
                      allow_small_or_imprecise_dtypes=True).then_inc(made, 1)
            pool.memset(g.ones[:], 1.0).then_inc(made, 1)

        @block.vector
        def _(dve):
            dve.wait_ge(made, 3)
            dve.tensor_copy(g.ident_b[:], g.ident[:]).then_inc(filled, 1)
            dve.tensor_copy(g.ident_h[:], g.ident[:]).then_inc(filled, 1)
            dve.wait_ge(filled, 3)


def stage_edges(nc, g, src, dst, et):
    with Scope(nc, "stage") as s:
        pad_dst, pad_zero = s.sb("pad_dst", [1, EP - E], I32), s.sb("pad_zero", [1, EP - E], I32)
        filled, stored, x_cleared = s.sem("filled"), s.sem("stored"), s.sem("x_cleared")
        block = s.block()

        @block.vector
        def _(dve):
            dve.memset(pad_dst[:], int(PAD_DST)).then_inc(filled, 1)
            dve.memset(pad_zero[:], 0).then_inc(filled, 1)
            dve.memset(g.x[:], 0.0).then_inc(x_cleared, 1)

        @block.sync
        def _(sp):
            row = lambda a: a.rearrange("(a n) -> a n", a=1)
            for flat, given in ((g.flat_src, src), (g.flat_dst, dst), (g.flat_et, et)):
                sp.dma_start(flat[0:E].rearrange("(a n) -> a n", a=125), given.rearrange("(a n) -> a n", a=125)).then_inc(stored, 16)
            sp.wait_ge(filled, 2)
            for flat, pad in ((g.flat_src, pad_zero), (g.flat_dst, pad_dst), (g.flat_et, pad_zero)):
                sp.dma_start(row(flat[E:EP]), pad[:]).then_inc(stored, 16)
            sp.wait_ge(x_cleared, 1)
            sp.dma_start(g.x[:, 0:FULL, :], g.x_in[0:FULL * P, :].rearrange("(t p) d -> p t d", p=P)).then_inc(stored, 16)
            sp.dma_start(g.x[0:REST, FULL, :], g.x_in[FULL * P:N, :]).then_inc(stored, 16)
            sp.wait_ge(stored, 8 * 16)


def walk(nc, g, s, name, row_len, lanes, cols, tile, tiles):
    last_rows = EP // row_len
    lr, lc = 81, EP // row_len // 81
    last = s.sb(f"{name}_last", [lr, lc], I32)
    lastf = s.sb(f"{name}_lastf", [lr, lc])
    edge = s.sb(f"{name}_edge", [P, tiles - 1])
    below = s.sb(f"{name}_below", [lr, lc, tiles - 1], BF16)
    start = s.sb(f"{name}_start", [P, tiles - 1])
    number = s.sb(f"{name}_number", [lanes, cols])
    past = s.sb(f"{name}_past", [lanes, cols, tiles - 1], BF16)
    tile_of, row_of = s.sb(f"{name}_tile_of", [lanes, cols]), s.sb(f"{name}_row_of", [lanes, cols])
    row_int = s.sb(f"{name}_row_int", [lanes, cols], I32)
    tile_int = s.sb(f"{name}_tile_int", [lanes, cols], I32)
    starts = s.ps(f"{name}_starts", [P, 512])
    with Scope(nc, f"{name}_walk") as w:
        loaded, counted, compared, summed, own = (w.sem(n) for n in ("loaded", "counted", "compared", "summed", "own"))
        block = w.block()

        @block.sync
        def _(sp):
            ends = g.flat_dst.rearrange("(a b n) -> a b n", a=lr, n=row_len)
            sp.dma_start(last[:], ends[:, :, row_len - 1], allow_slow_non_contiguous=True).then_inc(loaded, 16)

        @block.gpsimd
        def _(pool):
            pool.iota(edge[:], [[tile, tiles - 1]], base=tile, channel_multiplier=0,
                      allow_small_or_imprecise_dtypes=True).then_inc(counted, 1)
            pool.iota(number[:], [[lanes, cols]], base=0, channel_multiplier=1,
                      allow_small_or_imprecise_dtypes=True).then_inc(counted, 1)

        @block.tensor
        def _(pe):
            pe.wait_ge(compared, 1)
            for c in range(lc):
                m = pe.matmul(starts[:, 0:tiles - 1], g.ones_b[0:lr, :], below[:, c, :], start=(c == 0), stop=(c == lc - 1))
            m.then_inc(summed, 1)

        @block.vector
        def _(dve):
            v = chain(dve, own)
            v(dve.memset(g.ones_b[:], 1.0))
            dve.wait_ge(loaded, 16)
            dve.wait_ge(counted, 2)
            v(dve.tensor_copy(lastf[:], last[:]))
            v(dve.tensor_tensor(below[:], lastf[:].unsqueeze(2).to_broadcast([lr, lc, tiles - 1]),
                                edge[0:lr, :].unsqueeze(1).to_broadcast([lr, lc, tiles - 1]), ALU.is_lt))
            dve.sem_inc(compared, 1)
            v(dve.tensor_scalar(start[:], edge[:], 1.0 / tile, None, ALU.mult))
            dve.wait_ge(summed, 1)
            v(dve.tensor_tensor(start[:], start[:], starts[:, 0:tiles - 1], ALU.add))
            v(dve.tensor_tensor(past[:], number[:].unsqueeze(2).to_broadcast([lanes, cols, tiles - 1]),
                                start[0:lanes, :].unsqueeze(1).to_broadcast([lanes, cols, tiles - 1]), ALU.is_ge))
            v(dve.tensor_reduce(tile_of[:], past[:], X, ALU.add))
            v(dve.tensor_tensor(row_of[:], number[:], tile_of[:], ALU.subtract))
            v(dve.tensor_copy(row_int[:], row_of[:]))
            v(dve.tensor_scalar(tile_int[:], tile_of[:], 1.0, None, ALU.mult))
    return tile_of, tile_int, row_int


def gather_rows(nc, g, name, flats, outs, row_int, lanes, cols, row_len, tile_int, tile_dram):
    with Scope(nc, f"{name}_rows") as w:
        landed, stored = w.sem("landed"), w.sem("stored")
        block = w.block()

        @block.gpsimd
        def _(pool):
            for flat, out in zip(flats, outs):
                for c in range(cols):
                    pool.indirect_dma_start(
                        out=out[:, c, :], out_offset=None, in_=flat.rearrange("(r n) -> r n", n=row_len),
                        in_offset=bass.IndirectOffsetOnAxis(ap=row_int[:, c:c + 1], axis=0)).then_inc(landed, 16)
            pool.wait_ge(landed, 16 * len(flats) * cols)

        @block.sync
        def _(sp):
            sp.dma_start(tile_dram[0:lanes * cols].rearrange("(c p) -> p c", p=lanes), tile_int[:],
                         allow_slow_non_contiguous=True).then_inc(stored, 16)
            sp.wait_ge(stored, 16)


def items_layer0(nc, g):
    with Scope(nc, "it0") as s:
        tile_of, tile_int, row_int = walk(nc, g, s, "it0", PAIR, PI, PC, P, NT)
        rows = [s.sb(n, [PI, PC, PAIR], I32) for n in ("src", "dst", "et")]
        gather_rows(nc, g, "it0", (g.flat_src, g.flat_dst, g.flat_et), rows, row_int, PI, PC, PAIR, tile_int, g.tile0_dram)
        srcf, dstf, etf, lane, key, w = (s.sb(n, [PI, PC, PAIR]) for n in ("srcf", "dstf", "etf", "lane", "key", "w"))
        guard = s.sb("guard", [1, 2])
        turned = [s.ps(f"turned{k}", [P, PC, P]) for k in range(2)]
        with Scope(nc, "it0b") as q:
            own, ready, turn, copied, stored = (q.sem(n) for n in ("own", "ready", "turn", "copied", "stored"))
            block = q.block()
            jobs = [(srcf, g.src_col), (etf, g.msg_col), (lane, g.lane_col), (w, g.et_col)]

            @block.vector
            def _(dve):
                v = chain(dve, own)
                v(dve.memset(guard[:], -1.0))
                v(dve.memset(g.lane_col[:, COLS:], -1.0))
                for f, i in zip((srcf, dstf, w), rows):
                    v(dve.tensor_copy(f[:], i[:]))
                v(dve.scalar_tensor_tensor(etf[:], srcf[:], float(R), w[:], ALU.mult, ALU.add))
                for c in range(PC):
                    v(dve.tensor_scalar(key[:, c, 0:1], tile_of[:, c:c + 1], float(P), None, ALU.mult))
                    v(dve.tensor_scalar(lane[:, c, :], dstf[:, c, :], key[:, c, 0:1], None, ALU.subtract))
                v(dve.tensor_scalar(key[:], lane[:], 0.0, None, ALU.is_ge))
                v(dve.scalar_tensor_tensor(key[:], lane[:], float(P), key[:], ALU.is_lt, ALU.mult))
                v(dve.scalar_tensor_tensor(key[:], dstf[:], 1.0, key[:], ALU.add, ALU.mult))
                dve.sem_inc(ready, 1)
                n = 0
                for _, col in jobs:
                    for k in range(2):
                        n += 1
                        dve.wait_ge(turn, n)
                        dve.tensor_copy(col[:, 0:COLS].rearrange("p (c i k) -> p c i k", c=PC, k=2)[:, :, :, k],
                                        turned[k][:, :, 0:PI]).then_inc(copied, 1)
                dve.wait_ge(copied, n)

            @block.tensor
            def _(pe):
                pe.wait_ge(ready, 1)
                n = 0
                for arr, _ in jobs:
                    for k in range(2):
                        if n >= 2:
                            pe.wait_ge(copied, n - 1)
                        for c in range(PC):
                            m = pe.transpose(turned[k][:, c, 0:PI], arr[:, c, k * P:(k + 1) * P], g.ident[0:PI, 0:PI])
                        m.then_inc(turn, 1)
                        n += 1

            @block.sync
            def _(sp):
                sp.wait_ge(ready, 1)
                sp.dma_start(g.key_dram[1:1 + ITEMS * PAIR].rearrange("(c p n) -> p c n", c=PC, n=PAIR), key[:]).then_inc(stored, 16)
                ends = g.key_dram[0:2 + ITEMS * PAIR].rearrange("(a n) -> a n", a=1)
                sp.dma_start(ends[:, 0:1], guard[:, 0:1]).then_inc(stored, 16)
                sp.dma_start(ends[:, 1 + ITEMS * PAIR:2 + ITEMS * PAIR], guard[:, 1:2]).then_inc(stored, 16)
                sp.wait_ge(stored, 48)


def node_table(nc, g, attn_vec, xT, factor):
    with Scope(nc, "node") as s:
        av, avT = s.sb("av", [R * H, D]), s.sb("avT", [D, R * H])
        sq = s.sb("sq", [P, NT, D])
        n2, t, w1, w2 = (s.sb(n, [P, NT]) for n in ("n2", "t", "w1", "w2"))
        px = [s.ps(f"px{k}", [P, 4, P]) for k in range(2)]
        pv, pd = s.ps("pv", [P, 512]), s.ps("pd", [P, 2, 512])
        loaded, own, turn, turned, dots, table, stored, n2_ready, norm_ready, ratio_ready, log_ready = (
            s.sem(n) for n in ("loaded", "own", "turn", "turned", "dots", "table", "stored", "n2_ready", "norm_ready",
                               "ratio_ready", "log_ready"))
        block = s.block()
        groups = range(0, NT, 4)
        half = 512 // (R * H)

        @block.sync
        def _(sp):
            sp.dma_start(av[:], attn_vec.rearrange("r h d -> (r h) d")).then_inc(loaded, 16)
            sp.wait_ge(table, 1)
            sp.dma_start(g.node_dram.rearrange("(t p) d -> p t d", p=P), g.node[:]).then_inc(stored, 16)
            sp.wait_ge(stored, 16)

        @block.tensor
        def _(pe):
            pe.wait_ge(loaded, 16)
            pe.transpose(pv[0:D, 0:R * H], av[:], g.ident[0:R * H, 0:R * H]).then_inc(turn, 1)
            for n, q in enumerate(groups):
                if n >= 2:
                    pe.wait_ge(turned, n)
                for i in range(q, min(q + 4, NT)):
                    m = pe.transpose(px[n % 2][0:D, i - q, :], g.x[:, i, :], g.ident[:])
                m.then_inc(turn, 1)
            pe.wait_ge(turned, 1 + len(groups))
            for i in range(NT):
                a = i % half * R * H
                m = pe.matmul(pd[:, i // half, a:a + R * H], xT[:, i, :], avT[:], start=True, stop=True)
            m.then_inc(dots, 1)

        @block.scalar
        def _(act):
            atanh_ratio_scalar(act, n2[:], t[:], w1[:], n2_ready, norm_ready, ratio_ready, log_ready, 1)

        @block.vector
        def _(dve):
            v = chain(dve, own)
            dve.wait_ge(turn, 1)
            dve.tensor_copy(avT[:], pv[0:D, 0:R * H]).then_inc(turned, 1)
            for n, q in enumerate(groups):
                dve.wait_ge(turn, n + 2)
                k = min(4, NT - q)
                dve.tensor_copy(xT[:, q:q + k, :], px[n % 2][0:D, 0:k, :]).then_inc(turned, 1)
            v(dve.tensor_copy(g.node[:, :, 0:D], g.x[:]))
            v(dve.tensor_tensor(sq[:], g.x[:], g.x[:], ALU.mult))
            v(dve.tensor_reduce(n2[:], sq[:], X, ALU.add))
            v(dve.tensor_copy(g.node[:, :, D:D + 1], n2[:].unsqueeze(2)))
            dve.wait_ge(dots, 1)
            for b in range(2):
                k = min(half, NT - b * half)
                v(dve.tensor_copy(g.node[:, b * half:b * half + k, D + 1:NODE],
                                  pd[:, b, 0:k * R * H].rearrange("p (t c) -> p t c", t=k)))
            dve.sem_inc(table, 1)
            atanh_ratio_vector(v, dve, n2[:], t[:], w1[:], w2[:], factor[:], n2_ready, norm_ready, ratio_ready, log_ready, 1)


def message_table(nc, g, rel_weight, xT, factor):
    with Scope(nc, "msg") as s:
        w = s.sb("w", [D, R, H, D])
        m2, nrm, th, u, lam, coef = (s.sb(n, [P, 2, R * H]) for n in ("m2", "nrm", "th", "u", "lam", "coef"))
        sq = s.sb("sq", [P, 2, R * H, D])
        row = s.sb("row", [P, 2, R * H, HEAD])
        pm = [s.ps(f"pm{k}", [P, R * H, D]) for k in range(2)]
        loaded, own, product, squared, m2_ready, root, tanh_done, row_ready = (
            s.sem(n) for n in ("loaded", "own", "product", "squared", "m2_ready", "root", "tanh_done", "row_ready"))
        row_stored = [s.sem(f"row_stored{b}") for b in range(2)]
        block = s.block()

        @block.sync
        def _(sp):
            sp.dma_start(w[:], rel_weight.rearrange("r h i o -> i r h o")).then_inc(loaded, 16)
            for i in range(NT):
                b = i % 2
                sp.wait_ge(row_ready, i + 1)
                sp.dma_start(g.msg_dram[i * P * R:(i + 1) * P * R, :].rearrange("(p r) c -> p (r c)", r=R),
                             row[:, b].rearrange("p a c -> p (a c)")).then_inc(row_stored[b], 16)
            sp.wait_ge(row_stored[0], 16 * ((NT + 1) // 2))
            sp.wait_ge(row_stored[1], 16 * (NT // 2))

        @block.tensor
        def _(pe):
            pe.wait_ge(loaded, 16)
            for i in range(NT):
                if i >= 2:
                    pe.wait_ge(row_ready, i - 1)
                for q in range(R // 2):
                    m = pe.matmul(pm[i % 2][:, q * 2 * H:(q + 1) * 2 * H, :].rearrange("p a d -> p (a d)"), xT[:, i, :],
                                  w[:, 2 * q:2 * q + 2].rearrange("i r h o -> i (r h o)"), start=True, stop=True)
                m.then_inc(product, 1)

        @block.scalar
        def _(act):
            for i in range(NT):
                b = i % 2
                act.wait_ge(product, i + 1)
                if i >= 2:
                    act.wait_ge(row_ready, i - 1)
                act.activation(sq[:, b], pm[b][:], ACT.Square).then_inc(squared, 1)
                act.wait_ge(m2_ready, i + 1)
                act.activation(nrm[:, b], m2[:, b], ACT.Sqrt).then_inc(root, 1)
                act.wait_ge(root, i + 1)
                act.activation(th[:, b], nrm[:, b], ACT.Tanh, scale=0.1).then_inc(tanh_done, 1)

        @block.vector
        def _(dve):
            v = chain(dve, own)
            v(dve.memset(row[:, :, :, D + 1:HEAD], 1.0))
            for i in range(NT):
                b = i % 2
                f = factor[:, i:i + 1]
                dve.wait_ge(squared, i + 1)
                v(dve.tensor_reduce(m2[:, b], sq[:, b], X, ALU.add))
                v(dve.tensor_scalar(m2[:, b], m2[:, b], f, f, ALU.mult, ALU.mult))
                v(dve.tensor_scalar(m2[:, b], m2[:, b], 1e-20, None, ALU.max))
                dve.sem_inc(m2_ready, 1)
                dve.wait_ge(tanh_done, i + 1)
                v(dve.tensor_tensor(u[:, b], th[:, b], th[:, b], ALU.mult))
                v(dve.tensor_scalar(u[:, b], u[:, b], -1.0, 1.0, ALU.mult, ALU.add))
                v(dve.tensor_scalar(u[:, b], u[:, b], 1e-06, 0.5, ALU.add, ALU.mult))
                v(dve.reciprocal(lam[:, b], u[:, b]))
                v(dve.reciprocal(coef[:, b], nrm[:, b]))
                v(dve.tensor_tensor(coef[:, b], coef[:, b], th[:, b], ALU.mult))
                v(dve.tensor_scalar(coef[:, b], coef[:, b], f, 10.0, ALU.mult, ALU.mult))
                v(dve.tensor_tensor(coef[:, b], coef[:, b], lam[:, b], ALU.mult))
                if i >= 2:
                    dve.wait_ge(row_stored[b], 16 * (i // 2))
                v(dve.tensor_copy(row[:, b, :, D:D + 1], lam[:, b].unsqueeze(2)))
                v(dve.tensor_tensor(row[:, b, :, 0:D], pm[b][:], coef[:, b].unsqueeze(2).to_broadcast([P, R * H, D]), ALU.mult))
                dve.sem_inc(row_ready, 1)


def edge_products(nc, g, a):
    with Scope(nc, "prod") as s:
        idx = s.sb("idx", [P, 2, 4], I32)
        xs = s.sb("xs", [P, 2, 4, NODE])
        oh = s.sb("oh", [P, 2, 4, P], BF16)
        ohT = s.sb("ohT", [P, 2, 4, P])
        rel = s.sb("rel", [P, 2, 4, R])
        prod = s.sb("prod", [P, 2, 4, D])
        ws, wd = s.sb("ws", [P, 2, 4, R * H]), s.sb("wd", [P, 2, 4, R * H])
        turned = [s.ps(f"turned{k}", [P, 4, P], BF16) for k in range(2)]
        xd = [s.ps(f"xd{k}", [P, 4, P]) for k in range(2)]
        landed = [s.sem(f"landed{k}") for k in range(2)]
        idx_ready, slot_free, oh_ready, turn, ohT_ready, xd_ready, sq_taken, own = (
            s.sem(n) for n in ("idx_ready", "slot_free", "oh_ready", "turn", "ohT_ready", "xd_ready", "sq_taken", "own"))
        primed = s.sem("primed")
        tiles = s.sb("tiles", [1, ITEMS], I32)
        block = s.block()
        STEPS = COLS // 4
        OWN = 8

        @block.sync
        def _(sp):
            sp.dma_start(tiles[:], g.tile0_dram[0:ITEMS].rearrange("(a n) -> a n", a=1)).then_inc(primed, 16)
            sp.wait_ge(primed, 16)

        @block.gpsimd
        def _(pool):
            with pool.Fori(0, STEPS // 2) as turn_of_two:
                it = turn_of_two * 2
                for k in range(2):
                    wait(pool, slot_free, it + k + 1)
                    pool.tensor_copy(idx[:, k, :], g.src_col[:, bass.ds((it + k) * 4, 4)]).then_inc(idx_ready, 1)
                    wait(pool, idx_ready, it + k + 1)
                    for j in range(4):
                        pool.indirect_dma_start(
                            out=xs[:, k, j, :], out_offset=None, in_=g.node_dram[:, :],
                            in_offset=bass.IndirectOffsetOnAxis(ap=idx[:, k, j:j + 1], axis=0)).then_inc(landed[k], 16)

        @block.tensor
        def _(pe):
            pe.wait_ge(primed, 16)
            with pe.Fori(0, STEPS // 2) as turn_of_two:
                it = turn_of_two * 2
                for k in range(2):
                    wait(pe, oh_ready, it + k + 1)
                    for j in range(4):
                        m = pe.transpose(turned[k][:, j, :], oh[:, k, j, :], g.ident_b[:])
                    m.then_inc(turn, 1)
                    wait(pe, ohT_ready, it + k + 1)
                    for j in range(2):
                        tile = pe.value_load(tiles[0:1, bass.ds((it + k) * 2 + j, 1)], min_val=0, max_val=NT - 1)
                        for h in range(2):
                            m = pe.matmul(xd[k][:, 2 * j + h, 0:NODE], ohT[:, k, 2 * j + h, :],
                                          g.node[:, bass.ds(tile, 1), :].rearrange("p a d -> p (a d)"), start=True, stop=True)
                    m.then_inc(xd_ready, 1)

        @block.scalar
        def _(act):
            with act.Fori(0, STEPS // 2) as turn_of_two:
                it = turn_of_two * 2
                for k in range(2):
                    wait(act, turn, it + k + 1)
                    act.copy(ohT[:, k], turned[k][:]).then_inc(ohT_ready, 1)
                    wait(act, landed[k], it * 32 + 64)
                    act.copy(a.s2[:, bass.ds((it + k) * 4, 4)], xs[:, k, :, D]).then_inc(sq_taken, 1)

        @block.vector
        def _(dve):
            def one_hot(slot, cols):
                dve.tensor_tensor(oh[:, slot], g.count[:].unsqueeze(1).to_broadcast([P, 4, P]),
                                  g.lane_col[:, cols].unsqueeze(2).to_broadcast([P, 4, P]), ALU.is_equal).then_inc(oh_ready, 1)

            dve.sem_inc(slot_free, 2)
            one_hot(0, slice(0, 4))
            with dve.Fori(0, STEPS // 2) as turn_of_two:
                it = turn_of_two * 2
                for k in range(2):
                    base = (it + k) * OWN
                    cols = bass.ds((it + k) * 4, 4)
                    one_hot(1 - k, bass.ds((it + k) * 4 + 4, 4))
                    dve.tensor_tensor(rel[:, k], g.count[:, 0:R].unsqueeze(1).to_broadcast([P, 4, R]),
                                      g.et_col[:, cols].unsqueeze(2).to_broadcast([P, 4, R]), ALU.is_equal).then_inc(own, 1)
                    wait(dve, landed[k], it * 32 + 64)
                    wait(dve, own, base + 1)
                    picked = rel[:, k].unsqueeze(3).to_broadcast([P, 4, R, H])
                    dve.tensor_tensor(ws[:, k].rearrange("p j (r h) -> p j r h", r=R),
                                      xs[:, k, :, D + 1:NODE].rearrange("p j (r h) -> p j r h", r=R), picked,
                                      ALU.mult).then_inc(own, 1)
                    wait(dve, own, base + 2)
                    dve.tensor_reduce(a.ps[:, cols, :], ws[:, k].rearrange("p j (r h) -> p j h r", r=R), X,
                                      ALU.add).then_inc(own, 1)
                    wait(dve, xd_ready, it + k + 1)
                    dve.tensor_tensor(prod[:, k], xd[k][:, :, 0:D], xs[:, k, :, 0:D], ALU.mult).then_inc(own, 1)
                    dve.tensor_tensor(wd[:, k].rearrange("p j (r h) -> p j r h", r=R),
                                      xd[k][:, :, D + 1:NODE].rearrange("p j (r h) -> p j r h", r=R), picked,
                                      ALU.mult).then_inc(own, 1)
                    wait(dve, own, base + 4)
                    dve.tensor_reduce(a.gram[:, cols], prod[:, k], X, ALU.add).then_inc(own, 1)
                    wait(dve, own, base + 5)
                    dve.tensor_reduce(a.pd[:, cols, :], wd[:, k].rearrange("p j (r h) -> p j h r", r=R), X,
                                      ALU.add).then_inc(own, 1)
                    dve.tensor_copy(a.d2[:, cols], xd[k][:, :, D]).then_inc(own, 1)
                    wait(dve, sq_taken, it + k + 1)
                    wait(dve, own, base + 8)
                    dve.sem_inc(slot_free, 1)


def edge_weights(nc, g, a):
    with Scope(nc, "wts") as s:
        w0, w1, w2, w3 = (s.sb(n, [P, COLS]) for n in ("w0", "w1", "w2", "w3"))
        own, n2_ready, norm_ready, ratio_ready, log_ready = (
            s.sem(n) for n in ("own", "n2_ready", "norm_ready", "ratio_ready", "log_ready"))
        block = s.block()
        G, s2, d2 = a.gram[:], a.s2[:], a.d2[:]

        @block.scalar
        def _(act):
            atanh_ratio_scalar(act, G, w0[:], w1[:], n2_ready, norm_ready, ratio_ready, log_ready, 1)

        @block.vector
        def _(dve):
            v = chain(dve, own)
            v(dve.tensor_scalar(w0[:], G, -2 * C, 1.0, ALU.mult, ALU.add))
            v(dve.tensor_tensor(w1[:], s2, d2, ALU.mult))
            v(dve.scalar_tensor_tensor(w1[:], w1[:], C * C, w0[:], ALU.mult, ALU.add))
            v(dve.tensor_scalar(w1[:], w1[:], 1e-10, None, ALU.max))
            v(dve.reciprocal(w3[:], w1[:]))
            v(dve.scalar_tensor_tensor(w0[:], d2, C, w0[:], ALU.mult, ALU.add))
            v(dve.tensor_scalar(w1[:], s2, -C, 1.0, ALU.mult, ALU.add))
            v(dve.tensor_tensor(w0[:], w0[:], w3[:], ALU.mult))
            v(dve.tensor_tensor(w1[:], w1[:], w3[:], ALU.mult))
            v(dve.tensor_tensor(a.ps[:], a.ps[:], w0[:].unsqueeze(2).to_broadcast([P, COLS, H]), ALU.mult))
            v(dve.tensor_tensor(a.pd[:], a.pd[:], w1[:].unsqueeze(2).to_broadcast([P, COLS, H]), ALU.mult))
            v(dve.tensor_tensor(a.ps[:], a.ps[:], a.pd[:], ALU.subtract))
            v(dve.scalar_tensor_tensor(w2[:], G, -2.0, w0[:], ALU.mult, ALU.mult))
            v(dve.tensor_tensor(w2[:], w2[:], w1[:], ALU.mult))
            v(dve.tensor_tensor(w0[:], w0[:], w0[:], ALU.mult))
            v(dve.tensor_tensor(w0[:], w0[:], s2, ALU.mult))
            v(dve.tensor_tensor(w1[:], w1[:], w1[:], ALU.mult))
            v(dve.tensor_tensor(w1[:], w1[:], d2, ALU.mult))
            v(dve.tensor_tensor(w0[:], w0[:], w1[:], ALU.add))
            v(dve.tensor_tensor(G, w0[:], w2[:], ALU.add))
            atanh_ratio_vector(v, dve, G, w0[:], w1[:], w2[:], w3[:], n2_ready, norm_ready, ratio_ready, log_ready, 1)
            v(dve.tensor_tensor(a.ps[:], a.ps[:], w3[:].unsqueeze(2).to_broadcast([P, COLS, H]), ALU.mult))
            v(dve.scalar_tensor_tensor(a.ps[:], a.ps[:], 0.2, a.ps[:], ALU.mult, ALU.max))

    SEQ = 8 * P
    BIG = -1e30
    with Scope(nc, "scan") as s:
        sc = s.sb("sc", [PI, H, SEQ])
        fwd, bwd = s.sb("fwd", [PI, H, SEQ]), s.sb("bwd", [PI, H, SEQ])
        kp, kc, kn = (s.sb(n, [PI, SEQ]) for n in ("kp", "kc", "kn"))
        ends = s.sb("ends", [PI, 4, H])
        chainT = s.sb("chainT", [H, 4, PI])
        carry = s.sb("carry", [H, 2, PI + 1])
        cin = s.sb("cin", [PI, 2, H])
        turned = [s.ps(f"turned{k}", [P, 4, P]) for k in range(2)]
        pe_ends = s.ps("ends_turned", [P, 512])
        loaded, turn, taken, own, ends_ready, endsT, carry_ready, carried, ex_ready, back, backed = (
            s.sem(n) for n in ("loaded", "turn", "taken", "own", "ends_ready", "endsT", "carry_ready", "carried",
                               "ex_ready", "back", "backed"))
        block = s.block()

        @block.sync
        def _(sp):
            for d, k in enumerate((kp, kc, kn)):
                sp.dma_start(k[:], g.key_dram[d:d + PI * SEQ].rearrange("(q n) -> q n", n=SEQ)).then_inc(loaded, 16)

        @block.tensor
        def _(pe):
            n = 0
            for h in range(H):
                for q in range(0, 8, 4):
                    if n >= 2:
                        pe.wait_ge(taken, n - 1)
                    for m in range(q, q + 4):
                        last = pe.transpose(turned[n % 2][0:PI, m - q, :], a.ps[:, m::8, h], g.ident[:])
                    last.then_inc(turn, 1)
                    n += 1
            for d in range(2):
                pe.wait_ge(ends_ready, d + 1)
                for b in range(2):
                    m = pe.transpose(pe_ends[0:H, b * P:b * P + PI], ends[:, 2 * d + b, :], g.ident[0:PI, 0:PI])
                m.then_inc(endsT, 1)
                pe.wait_ge(carry_ready, d + 1)
                c = carry[:, 0, 0:PI] if d == 0 else carry[:, 1, 1:PI + 1]
                pe.transpose(pe_ends[0:PI, 256:256 + H], c, g.ident[0:H, 0:H]).then_inc(carried, 1)
            n = 0
            pe.wait_ge(ex_ready, 1)
            pe.wait_ge(taken, 8)
            for h in range(H):
                for q in range(0, 8, 4):
                    if n >= 2:
                        pe.wait_ge(backed, n - 1)
                    for m in range(q, q + 4):
                        last = pe.transpose(turned[n % 2][:, m - q, 0:PI], sc[:, h, m * P:(m + 1) * P], g.ident[0:PI, 0:PI])
                    last.then_inc(back, 1)
                    n += 1

        @block.scalar
        def _(act):
            act.wait_ge(carry_ready, 3)
            act.activation(sc[:], sc[:], ACT.Exp).then_inc(ex_ready, 1)

        @block.vector
        def _(dve):
            v = chain(dve, own)
            n = 0
            for h in range(H):
                for q in range(0, 8, 4):
                    dve.wait_ge(turn, n + 1)
                    dve.tensor_copy(sc[:, h, q * P:(q + 4) * P].rearrange("p (m e) -> p m e", m=4), turned[n % 2][0:PI]).then_inc(taken, 1)
                    n += 1
            dve.wait_ge(taken, n)
            dve.wait_ge(loaded, 48)
            v(dve.tensor_tensor(kp[:], kp[:], kc[:], ALU.not_equal))
            v(dve.tensor_scalar(kp[:], kp[:], BIG, None, ALU.mult))
            v(dve.tensor_tensor(kn[:], kn[:], kc[:], ALU.not_equal))
            v(dve.tensor_scalar(kn[:], kn[:], BIG, None, ALU.mult))
            v(dve.memset(carry[:], BIG))
            for d, (brk, src, out) in enumerate(((kp, sc, fwd), (kn, fwd, bwd))):
                flip = (lambda t: t) if d == 0 else (lambda t: t[:, ::-1])
                last = SEQ - 1 if d == 0 else 0
                for h in range(H):
                    v(dve.tensor_tensor_scan(flip(out[:, h, :]), flip(brk[:]), flip(src[:, h, :]), BIG, ALU.add, ALU.max))
                v(dve.tensor_copy(ends[:, 2 * d, :], out[:, :, last]))
                v(dve.tensor_reduce(ends[:, 2 * d + 1, 0:1], brk[:], X, ALU.min))
                v(dve.tensor_copy(ends[:, 2 * d + 1, 1:H], ends[:, 2 * d + 1, 0:1].to_broadcast([PI, H - 1])))
                dve.sem_inc(ends_ready, 1)
                dve.wait_ge(endsT, d + 1)
                v(dve.tensor_copy(chainT[:, 2 * d:2 * d + 2, :], pe_ends[0:H, 0:2 * P].rearrange("p (b n) -> p b n", b=2)[:, :, 0:PI]))
                to = carry[:, 0, 1:PI + 1] if d == 0 else carry[:, 1, 0:PI]
                v(dve.tensor_tensor_scan(flip(to), flip(chainT[:, 2 * d + 1, :]), flip(chainT[:, 2 * d, :]), BIG, ALU.add, ALU.max))
                dve.sem_inc(carry_ready, 1)
                dve.wait_ge(carried, d + 1)
                v(dve.tensor_copy(cin[:, d, :], pe_ends[0:PI, 256:256 + H]))
                for h in range(H):
                    v(dve.tensor_tensor_scan(flip(out[:, h, :]), flip(brk[:]), flip(src[:, h, :]), cin[:, d, h:h + 1], ALU.add, ALU.max))
            v(dve.tensor_tensor(sc[:], sc[:], bwd[:], ALU.subtract))
            dve.sem_inc(carry_ready, 1)
            n = 0
            for h in range(H):
                for q in range(0, 8, 4):
                    dve.wait_ge(back, n + 1)
                    out = g.ex[:].rearrange("p (q m) h -> p m q h", m=8)[:, q:q + 4, :, h]
                    dve.tensor_copy(out, turned[n % 2][:, :, 0:PI]).then_inc(backed, 1)
                    n += 1
            dve.wait_ge(backed, n)


def edge_sums(nc, g):
    with Scope(nc, "sums") as s:
        idx = s.sb("idx", [P, 2, 4], I32)
        msg = s.sb("msg", [P, 2, 4, MSG])
        val = s.sb("val", [P, 2, 4, OUTC])
        oh = s.sb("oh", [P, 2, 4, P])
        part = [s.ps(f"part{k}", [P, 2, 512]) for k in range(2)]
        tiles = s.sb("tiles", [1, ITEMS + 2], I32)
        landed = [s.sem(f"landed{k}") for k in range(2)]
        idx_ready, slot_free, val_ready, part_ready, part_added, primed, own, cleared = (
            s.sem(n) for n in ("idx_ready", "slot_free", "val_ready", "part_ready", "part_added", "primed", "own", "cleared"))
        block = s.block()
        STEPS = COLS // 4

        @block.sync
        def _(sp):
            sp.wait_ge(cleared, 1)
            sp.dma_start(tiles[:, 2:], g.tile0_dram[0:ITEMS].rearrange("(a n) -> a n", a=1)).then_inc(primed, 16)
            sp.wait_ge(primed, 16)

        @block.gpsimd
        def _(pool):
            with pool.Fori(0, STEPS // 2) as turn_of_two:
                it = turn_of_two * 2
                for k in range(2):
                    wait(pool, slot_free, it + k + 1)
                    pool.tensor_copy(idx[:, k, :], g.msg_col[:, bass.ds((it + k) * 4, 4)]).then_inc(idx_ready, 1)
                    wait(pool, idx_ready, it + k + 1)
                    for j in range(4):
                        pool.indirect_dma_start(
                            out=msg[:, k, j, :], out_offset=None, in_=g.msg_dram[:, :],
                            in_offset=bass.IndirectOffsetOnAxis(ap=idx[:, k, j:j + 1], axis=0)).then_inc(landed[k], 16)

        @block.tensor
        def _(pe):
            with pe.Fori(0, STEPS // 2) as turn_of_two:
                it = turn_of_two * 2
                for k in range(2):
                    wait(pe, val_ready, it + k + 1)
                    for j in range(2):
                        for h in range(2):
                            m = pe.matmul(part[k][:, j, 0:OUTC], oh[:, k, 2 * j + h, :], val[:, k, 2 * j + h, :],
                                          start=(h == 0), stop=(h == 1))
                    m.then_inc(part_ready, 1)

        @block.vector
        def _(dve):
            v = chain(dve, own)
            dve.memset(tiles[:, 0:2], 0).then_inc(cleared, 1)
            v(dve.memset(g.sums[:], 0.0))
            v(dve.memset(val[:, :, :, MSG:OUTC], 1.0))
            dve.wait_ge(primed, 16)
            v(dve.memset(part[1][:], 0.0))
            dve.sem_inc(slot_free, 2)
            dve.sem_inc(part_ready, 1)

            def add(part, tiles_at, n):
                for j in range(2):
                    tile = dve.value_load(tiles[0:1, tiles_at(j)], min_val=0, max_val=NT - 1)
                    at = g.sums[:, bass.ds(tile, 1), :].rearrange("p a c -> p (a c)")
                    dve.tensor_tensor(at, at, part[:, j, 0:OUTC], ALU.add).then_inc(part_added, 1)
                    wait(dve, part_added, n + j)

            with dve.Fori(0, STEPS // 2) as turn_of_two:
                it = turn_of_two * 2
                for k in range(2):
                    cols = bass.ds((it + k) * 4, 4)
                    dve.tensor_tensor(oh[:, k], g.count[:].unsqueeze(1).to_broadcast([P, 4, P]),
                                      g.lane_col[:, cols].unsqueeze(2).to_broadcast([P, 4, P]), ALU.is_equal).then_inc(own, 1)
                    wait(dve, landed[k], it * 32 + 64)
                    dve.tensor_tensor(val[:, k, :, 0:MSG].rearrange("p j (h c) -> p j h c", h=H),
                                      msg[:, k].rearrange("p j (h c) -> p j h c", h=H),
                                      g.ex[:, cols, :].unsqueeze(3).to_broadcast([P, 4, H, HEAD]), ALU.mult).then_inc(own, 1)
                    wait(dve, own, (it + k) * 2 + 5)
                    dve.sem_inc(val_ready, 1)
                    dve.sem_inc(slot_free, 1)
                    wait(dve, part_ready, it + k + 1)
                    add(part[1 - k], lambda j: bass.ds((it + k) * 2 + j, 1), (it + k) * 2 + 1)
            dve.wait_ge(part_ready, STEPS + 1)
            add(part[1], lambda j: slice(ITEMS + j, ITEMS + j + 1), 2 * STEPS + 1)


def finish_layer0(nc, g):
    with Scope(nc, "fin0") as s:
        TH = NT * H
        sq = s.sb("sq", [P, NT, D])
        sq4 = s.sb("sq4", [P, NT, D])
        h_new = s.sb("h_new", [P, NT, D])
        inv, den, coef, n2, t, w1, w2, f = (s.sb(n, [P, NT, H]) for n in ("inv", "den", "coef", "n2", "t", "w1", "w2", "f"))
        a2, nrm, th = (s.sb(n, [P, NT]) for n in ("a2", "nrm", "th"))
        st = s.sb("st", [P, 2, NT])
        own, n2_ready, norm_ready, ratio_ready, log_ready, a2_ready, root, tanh_done, var_ready, root_ready, shrink_ready = (
            s.sem(n) for n in ("own", "n2_ready", "norm_ready", "ratio_ready", "log_ready", "a2_ready", "root",
                               "tanh_done", "var_ready", "root_ready", "shrink_ready"))
        block = s.block()
        heads = g.sums[:, :, 0:MSG].rearrange("p t (h c) -> p t h c", h=H)

        @block.scalar
        def _(act):
            atanh_ratio_scalar(act, n2[:], t[:], w1[:], n2_ready, norm_ready, ratio_ready, log_ready, 1)
            act.wait_ge(n2_ready, 2)
            act.activation(w1[:], n2[:], ACT.Sqrt).then_inc(shrink_ready, 1)
            act.wait_ge(a2_ready, 1)
            act.activation(nrm[:], a2[:], ACT.Sqrt).then_inc(root, 1)
            act.wait_ge(root, 1)
            act.activation(th[:], nrm[:], ACT.Tanh, scale=0.1).then_inc(tanh_done, 1)
            layer_norm_scalar(act, st, var_ready, root_ready, 1)

        @block.vector
        def _(dve):
            v = chain(dve, own)
            v(dve.tensor_scalar(inv[:], heads[:, :, :, D + 1], 0.5, None, ALU.max))
            v(dve.reciprocal(inv[:], inv[:]))
            v(dve.tensor_tensor(den[:], heads[:, :, :, D], inv[:], ALU.mult))
            v(dve.tensor_scalar(den[:], den[:], 1e-06, None, ALU.add))
            v(dve.reciprocal(coef[:], den[:]))
            v(dve.tensor_tensor(coef[:], coef[:], inv[:], ALU.mult))
            for h in range(H):
                v(dve.tensor_tensor(sq[:], heads[:, :, h, 0:D], coef[:, :, h:h + 1].to_broadcast([P, NT, D]), ALU.mult))
                v(dve.tensor_tensor(sq4[:], sq[:], sq[:], ALU.mult))
                v(dve.tensor_reduce(n2[:, :, h], sq4[:], X, ALU.add))
            atanh_ratio_vector(v, dve, n2[:], t[:], w1[:], w2[:], f[:], n2_ready, norm_ready, ratio_ready, log_ready, 1)
            v(dve.tensor_scalar(n2[:], n2[:], MAXNORM * MAXNORM, 1.0 / (MAXNORM * MAXNORM), ALU.max, ALU.mult))
            dve.sem_inc(n2_ready, 1)
            dve.wait_ge(shrink_ready, 1)
            v(dve.reciprocal(w2[:], w1[:]))
            v(dve.tensor_tensor(f[:], f[:], w2[:], ALU.mult))
            v(dve.scalar_tensor_tensor(coef[:], coef[:], 1.0 / H, f[:], ALU.mult, ALU.mult))
            bc = lambda a, h: a[:, :, h:h + 1].to_broadcast([P, NT, D])
            v(dve.tensor_tensor(h_new[:], heads[:, :, 0, 0:D], bc(coef, 0), ALU.mult))
            for h in range(1, H):
                v(dve.tensor_tensor(sq[:], heads[:, :, h, 0:D], bc(coef, h), ALU.mult))
                v(dve.tensor_tensor(h_new[:], h_new[:], sq[:], ALU.add))
            v(dve.tensor_tensor(sq[:], h_new[:], h_new[:], ALU.mult))
            v(dve.tensor_reduce(a2[:], sq[:], X, ALU.add))
            v(dve.tensor_scalar(a2[:], a2[:], 1e-20, None, ALU.max))
            dve.sem_inc(a2_ready, 1)
            dve.wait_ge(tanh_done, 1)
            v(dve.reciprocal(a2[:], nrm[:]))
            v(dve.scalar_tensor_tensor(a2[:], a2[:], 10.0, th[:], ALU.mult, ALU.mult))
            v(dve.tensor_tensor(h_new[:], h_new[:], a2[:].unsqueeze(2).to_broadcast([P, NT, D]), ALU.mult))
            v(dve.tensor_tensor(g.x[:], g.x[:], h_new[:], ALU.add))
            v(dve.tensor_copy(g.deg_in[:], g.sums[:, :, MSG]))
            layer_norm_vector(v, dve, g.x[:], sq[:], st, var_ready, root_ready, 1)


def items_matrix(nc, g):
    if True:
        lo_col, hi_col, win_col, tiles = g.lo_col, g.hi_col, g.win_col, g.tiles1
        with Scope(nc, "cmi") as q:
            tile_of, tile_int, row_int = walk(nc, g, q, "cmi", P, CI, CC, WIN, WINS)
            rows = [q.sb(n, [CI, CC, P], I32) for n in ("src", "dst")]
            lane_of, tile_src = q.sb("lane_of", [CI, CC, P], I32), q.sb("tile_src", [CI, CC, P], I32)
            gather_rows(nc, g, "cmi", (g.flat_src, g.flat_dst), rows, row_int, CI, CC, P, tile_int, g.tile1_dram)
            lof, hif, win = (q.sb(n, [CI, CC, P]) for n in ("lof", "hif", "win"))
            turned = [q.ps(f"turned{k}", [P, 4, P]) for k in range(2)]
            own, ready, turn, copied, loaded, zeroed = (q.sem(n) for n in ("own", "ready", "turn", "copied", "loaded", "zeroed"))
            block = q.block()
            jobs = [(lof, lo_col), (hif, hi_col), (win, win_col)]

            @block.sync
            def _(sp):
                sp.wait_ge(own, 1)
                sp.dma_start(tiles[:, 4:], g.tile1_dram[0:CITEMS].rearrange("(a n) -> a n", a=1)).then_inc(loaded, 16)
                sp.wait_ge(loaded, 16)

            @block.vector
            def _(dve):
                v = chain(dve, own)
                v(dve.memset(tiles[:, 0:4], 0))
                for col in (lo_col, hi_col, win_col):
                    v(dve.memset(col[:, CITEMS:], -1.0))
                v(dve.tensor_scalar(lane_of[:], rows[0][:], P - 1, None, ALU.bitwise_and))
                v(dve.tensor_copy(lof[:], lane_of[:]))
                v(dve.tensor_scalar(tile_src[:], rows[0][:], 7, None, ALU.logical_shift_right))
                v(dve.tensor_copy(hif[:], tile_src[:]))
                v(dve.tensor_scalar(tile_of[:], tile_of[:], float(WIN), None, ALU.mult))
                v(dve.tensor_copy(win[:], rows[1][:]))
                v(dve.tensor_tensor(win[:], win[:], tile_of[:].unsqueeze(2).to_broadcast([CI, CC, P]), ALU.subtract))
                dve.sem_inc(ready, 1)
                n = 0
                for _, col in jobs:
                    for c in range(0, CC, 4):
                        n += 1
                        dve.wait_ge(turn, n)
                        dve.tensor_copy(col[:, c * CI:(c + 4) * CI].rearrange("p (c i) -> p c i", c=4),
                                        turned[(n - 1) % 2][:, :, 0:CI]).then_inc(copied, 1)
                dve.wait_ge(copied, n)

            @block.tensor
            def _(pe):
                pe.wait_ge(ready, 1)
                n = 0
                for arr, _ in jobs:
                    for c in range(0, CC, 4):
                        if n >= 2:
                            pe.wait_ge(copied, n - 1)
                        for j in range(4):
                            m = pe.transpose(turned[n % 2][:, j, 0:CI], arr[:, c + j, :], g.ident[0:CI, 0:CI])
                        m.then_inc(turn, 1)
                        n += 1


def count_matrix(nc, g):
    if True:
        with Scope(nc, "cmb") as q:
            lo_col, hi_col, win_col, tiles = g.lo_col, g.hi_col, g.win_col, g.tiles1
            lo = q.sb("lo", [P, 2, 4, P], BF16)
            hi = q.sb("hi", [P, 2, 4, NT], BF16)
            win = q.sb("win", [P, 2, 4, WIN], BF16)
            cell = q.sb("cell", [P, 2, 4, NT, WIN], BF16)
            got = q.sb("got", [P, 2, 4, NT, WIN], F16)
            part = [q.ps(f"part{k}", [P, 2, 512]) for k in range(4)]
            own, zeroed, cell_ready, part_ready, part_taken, added, fresh, own_pool = (
                q.sem(n) for n in ("own", "zeroed", "cell_ready", "part_ready", "part_taken", "added", "fresh", "own_pool"))
            block = q.block()
            STEPS = CITEMS // 4
            ZEROED_BY_VECTOR = 17

            @block.vector
            def _(dve):
                for i in range(0, ZEROED_BY_VECTOR):
                    m = dve.memset(g.matrix[:, i, :], 0.0)
                m.then_inc(zeroed, 1)
                with dve.Fori(0, STEPS // 2) as turn_of_two:
                    it = turn_of_two * 2
                    for k in range(2):
                        cols = bass.ds((it + k) * 4, 4)
                        base = (it + k) * 4
                        eq = lambda out, n, col: dve.tensor_tensor(
                            out, g.count[:, 0:n].unsqueeze(1).to_broadcast([P, 4, n]),
                            col[:, cols].unsqueeze(2).to_broadcast([P, 4, n]), ALU.is_equal)
                        wait(dve, part_ready, it + k + 1)
                        eq(lo[:, k], P, lo_col).then_inc(own, 1)
                        eq(hi[:, k], NT, hi_col).then_inc(own, 1)
                        eq(win[:, k], WIN, win_col).then_inc(own, 1)
                        wait(dve, own, base + 3)
                        dve.tensor_tensor(cell[:, k], hi[:, k].unsqueeze(3).to_broadcast([P, 4, NT, WIN]),
                                          win[:, k].unsqueeze(2).to_broadcast([P, 4, NT, WIN]), ALU.mult).then_inc(own, 1)
                        wait(dve, own, base + 4)
                        dve.sem_inc(cell_ready, 1)

            @block.tensor
            def _(pe):
                pe.sem_inc(part_ready, 2)
                with pe.Fori(0, STEPS // 2) as turn_of_two:
                    it = turn_of_two * 2
                    for k in range(2):
                        wait(pe, cell_ready, it + k + 1)
                        wait(pe, part_taken, it + k + 1)
                        for j in range(4):
                            m = pe.matmul(part[2 * k + j // 2][:, j % 2, 0:NT * WIN], lo[:, k, j, :],
                                          cell[:, k, j].rearrange("p a b -> p (a b)"), start=True, stop=True)
                        m.then_inc(part_ready, 1)

            @block.scalar
            def _(act):
                act.sem_inc(part_taken, 2)
                with act.Fori(0, STEPS // 2) as turn_of_two:
                    it = turn_of_two * 2
                    for k in range(2):
                        wait(act, part_ready, it + k + 3)
                        wait(act, added, it + k + 1)
                        act.copy(got[:, k, 0:2].rearrange("p j a b -> p j (a b)"), part[2 * k][:, :, 0:NT * WIN]).then_inc(fresh, 1)
                        act.copy(got[:, k, 2:4].rearrange("p j a b -> p j (a b)"), part[2 * k + 1][:, :, 0:NT * WIN]).then_inc(fresh, 1)
                        wait(act, fresh, (it + k) * 2 + 2)
                        act.sem_inc(part_taken, 1)

            @block.gpsimd
            def _(pool):
                pool.sem_inc(added, 2)
                for i in range(ZEROED_BY_VECTOR, NT):
                    m = pool.memset(g.matrix[:, i, :], 0.0)
                m.then_inc(zeroed, 1)
                pool.wait_ge(zeroed, 2)
                with pool.Fori(0, STEPS // 2) as turn_of_two:
                    it = turn_of_two * 2
                    for k in range(2):
                        wait(pool, fresh, (it + k) * 2 + 2)
                        for j in range(4):
                            tile = pool.value_load(tiles[0:1, bass.ds((it + k) * 4 + 4 + j, 1)], min_val=0, max_val=WINS - 1)
                            at = g.matrix[:, :, bass.ds(tile * WIN, WIN)]
                            ins = pool.tensor_tensor(at, at, got[:, k, j], ALU.add)
                            ins.then_inc(own_pool, 1)
                            wait(pool, own_pool, (it + k) * 4 + j + 1)
                        pool.sem_inc(added, 1)


def out_degrees(nc, g):
    with Scope(nc, "deg") as s:
        deg, m, r = s.sb("deg", [P, 2, NT]), s.sb("m", [P, 2, NT]), s.sb("r", [P, 2, NT])
        own, ready, root = s.sem("own"), s.sem("ready"), s.sem("root")
        block = s.block()

        @block.scalar
        def _(act):
            act.wait_ge(ready, 1)
            act.activation(r[:], m[:], ACT.Sqrt).then_inc(root, 1)

        @block.vector
        def _(dve):
            v = chain(dve, own)
            v(dve.tensor_reduce(deg[:, 0, :], g.matrix[:], X, ALU.add))
            v(dve.tensor_copy(deg[:, 1, :], g.deg_in[:]))
            v(dve.tensor_scalar(m[:], deg[:], 1.0, None, ALU.max))
            dve.sem_inc(ready, 1)
            v(dve.reciprocal(g.per_deg[:], m[:]))
            dve.wait_ge(root, 1)
            v(dve.reciprocal(m[:], r[:]))
            v(dve.scalar_tensor_tensor(g.root_deg[:], deg[:], 0.0, m[:], ALU.is_gt, ALU.mult))


def graph_layer(nc, g, name, pre, reverse, scale_in, scale_out, w_dram, b_dram, relu, out=None):
    with Scope(nc, name) as s:
        has_w = w_dram is not None
        w = s.sb("w", [D, D])
        bias = s.sb("bias", [P, D])
        xT = s.sb("xT", [D, 4, P])
        feat = s.sb("feat", [P, NT, D])
        parts = s.sb("parts", [P, NT, 3, D], BF16)
        agg = feat
        st = s.sb("st", [P, 2, NT])
        flip = s.sb("flip", [P, 2, 8, P], F16)
        px = s.ps("px", [P, 4, P])
        pw = s.ps("pw", [P, 4, D])
        pc = [s.ps(f"pc{k}", [P, 512]) for k in range(2)]
        pt = [s.ps(f"pt{k}", [P, 8, P], F16) for k in range(2)]
        loaded, own, ready, turn, turned, multiplied, parts_ready, summed, taken, flipped, var_ready, root_ready, stored = (
            s.sem(n) for n in ("loaded", "own", "ready", "turn", "turned", "multiplied", "parts_ready", "summed", "taken",
                               "flipped", "var_ready", "root_ready", "stored"))
        flip_turn = s.sem("flip_turn")
        block = s.block()
        bc = lambda a: a.unsqueeze(2).to_broadcast([P, NT, D])
        groups = list(range(0, NT, 4))
        jgroups = list(range(0, NT, 8))

        @block.sync
        def _(sp):
            if has_w:
                sp.dma_start(w[:], w_dram[:, :]).then_inc(loaded, 16)
                sp.dma_start(bias[:], b_dram.rearrange("(a n) -> a n", a=1).to_broadcast([P, D])).then_inc(loaded, 16)
                sp.wait_ge(loaded, 32)
            if out is not None:
                sp.wait_ge(stored, 1)
                sp.dma_start(out[0:FULL * P, :].rearrange("(t p) d -> p t d", p=P), g.x[:, 0:FULL, :]).then_inc(loaded, 16)
                sp.dma_start(out[FULL * P:N, :], g.x[0:REST, FULL, :]).then_inc(loaded, 16)
                sp.wait_ge(loaded, 32)

        @block.scalar
        def _(act):
            if reverse:
                n = 0
                for i in range(NT):
                    for q in jgroups:
                        k = min(8, NT - q)
                        act.wait_ge(flip_turn, n + 1)
                        act.copy(flip[:, n % 2, 0:k, :], pt[n % 2][:, 0:k, :]).then_inc(flipped, 1)
                        n += 1
            layer_norm_scalar(act, st, var_ready, root_ready, 1)

        def times_w_tensor(pe, src):
            pe.wait_ge(loaded, 32)
            pe.wait_ge(ready, 1)
            for n, q in enumerate(groups):
                k = min(4, NT - q)
                if n:
                    pe.wait_ge(multiplied, n)
                for i in range(k):
                    m = pe.transpose(px[0:D, i, :], src[:, q + i, :], g.ident[:])
                m.then_inc(turn, 1)
                pe.wait_ge(turned, n + 1)
                for i in range(k):
                    m = pe.matmul(pw[:, i, :], xT[:, i, :], w[:], start=True, stop=True)
                m.then_inc(turn, 1)

        def times_w_vector(dve, out):
            for n, q in enumerate(groups):
                k = min(4, NT - q)
                dve.wait_ge(turn, 2 * n + 1)
                dve.tensor_copy(xT[:, 0:k, :], px[0:D, 0:k, :]).then_inc(turned, 1)
                dve.wait_ge(turn, 2 * n + 2)
                dve.tensor_copy(out[:, q:q + k, :], pw[:, 0:k, :]).then_inc(multiplied, 1)
            dve.wait_ge(multiplied, len(groups))

        @block.tensor
        def _(pe):
            if pre:
                times_w_tensor(pe, g.x)
            pe.wait_ge(parts_ready, 1)
            n = 0
            if not reverse:
                for j in range(NT):
                    if j >= 2:
                        pe.wait_ge(taken, j - 1)
                    for i in range(NT):
                        m = pe.matmul(pc[j % 2][:, 0:3 * D], g.matrix[:, i, j * P:(j + 1) * P],
                                      parts[:, i].rearrange("p a d -> p (a d)"), start=(i == 0), stop=(i == NT - 1))
                    m.then_inc(summed, 1)
            else:
                steps = [(i, q) for i in range(NT) for q in jgroups]

                def turn_group(n):
                    i, q = steps[n]
                    if n >= 2:
                        pe.wait_ge(flipped, n - 1)
                    for j in range(q, min(q + 8, NT)):
                        m = pe.transpose(pt[n % 2][:, j - q, :], g.matrix[:, i, j * P:(j + 1) * P], g.ident_h[:])
                    m.then_inc(flip_turn, 1)

                turn_group(0)
                for n, (i, q) in enumerate(steps):
                    if n + 1 < len(steps):
                        turn_group(n + 1)
                    pe.wait_ge(flipped, n + 1)
                    if q == 0 and i >= 2:
                        pe.wait_ge(taken, i - 1)
                    for j in range(q, min(q + 8, NT)):
                        m = pe.matmul(pc[i % 2][:, 0:3 * D], flip[:, n % 2, j - q, :],
                                      parts[:, j].rearrange("p a d -> p (a d)"), start=(j == 0), stop=(j == NT - 1))
                    if q == jgroups[-1]:
                        m.then_inc(summed, 1)
            if has_w and not pre:
                times_w_tensor(pe, agg)

        @block.vector
        def _(dve):
            v = chain(dve, own)
            if pre:
                dve.sem_inc(ready, 1)
                times_w_vector(dve, feat)
                v(dve.tensor_tensor(feat[:], feat[:], bc(scale_in), ALU.mult))
            else:
                v(dve.tensor_tensor(feat[:], g.x[:], bc(scale_in), ALU.mult))
            for b in range(3):
                v(dve.tensor_copy(parts[:, :, b, :], feat[:]))
                if b < 2:
                    v(dve.tensor_tensor(feat[:], feat[:], parts[:, :, b, :], ALU.subtract))
            dve.sem_inc(parts_ready, 1)
            for j in range(NT):
                dve.wait_ge(summed, j + 1)
                dve.tensor_reduce(agg[:, j, :], pc[j % 2][:, 0:3 * D].rearrange("p (b d) -> p d b", b=3), X, ALU.add).then_inc(taken, 1)
            dve.wait_ge(taken, NT)
            v(dve.tensor_tensor(agg[:], agg[:], bc(scale_out), ALU.mult))
            if has_w and not pre:
                dve.sem_inc(ready, 1)
                times_w_vector(dve, agg)
            if has_w:
                v(dve.tensor_tensor(agg[:], agg[:], bias[:].unsqueeze(1).to_broadcast([P, NT, D]), ALU.add))
            if relu:
                v(dve.tensor_scalar(agg[:], agg[:], 0.0, None, ALU.max))
            v(dve.tensor_tensor(g.x[:], g.x[:], agg[:], ALU.add))
            layer_norm_vector(v, dve, g.x[:], agg[:], st, var_ready, root_ready, 1)
            if out is not None:
                dve.sem_inc(stored, 1)


class Shared:
    pass


def build(nc, x, src, dst, edge_type_8, rel_weight, attn_vec, rel_emb, W1, b1, W2, b2, out):
    g = Shared()
    g.x_in = x
    dram = lambda name, shape, dt=F32: nc.dram_tensor(name, shape, dt).ap()
    g.flat_src, g.flat_dst, g.flat_et = (dram(n, [EP], I32) for n in ("flat_src", "flat_dst", "flat_et"))
    g.key_dram = dram("keys", [ITEMS * PAIR + 2])
    g.node_dram = dram("node_table", [NP, NODE])
    g.msg_dram = dram("message_table", [NP * R, MSG])
    g.tile0_dram, g.tile1_dram = dram("tiles0", [ITEMS], I32), dram("tiles1", [CITEMS], I32)
    with Scope(nc, "g") as s:
        g.ident, g.ident_b, g.ident_h = s.sb("ident", [P, P]), s.sb("ident_b", [P, P], BF16), s.sb("ident_h", [P, P], F16)
        g.count, g.ones, g.ones_b = s.sb("count", [P, P]), s.sb("ones", [P, 1]), s.sb("ones_b", [P, P], BF16)
        g.x = s.sb("x", [P, NT, D])
        g.deg_in = s.sb("deg_in", [P, NT])
        g.per_deg, g.root_deg = s.sb("per_deg", [P, 2, NT]), s.sb("root_deg", [P, 2, NT])
        constants(nc, g)
        stage_edges(nc, g, src, dst, edge_type_8)
        with Scope(nc, "l0") as l0:
            g.src_col, g.msg_col = (l0.sb(n, [P, COLS], I32) for n in ("src_col", "msg_col"))
            g.lane_col, g.et_col = l0.sb("lane_col", [P, COLS + 4]), l0.sb("et_col", [P, COLS])
            items_layer0(nc, g)
            g.ex = l0.sb("ex", [P, COLS, H])
            with Scope(nc, "l0n") as n0:
                g.node = n0.sb("node", [P, NT, NODE])
                with Scope(nc, "l0t") as t0:
                    xT, factor = t0.sb("xT", [D, NT, P]), t0.sb("factor", [P, NT])
                    node_table(nc, g, attn_vec, xT, factor)
                    message_table(nc, g, rel_weight, xT, factor)
                with Scope(nc, "l0a") as a0:
                    a = Shared()
                    a.s2, a.d2, a.gram = (a0.sb(n, [P, COLS]) for n in ("s2", "d2", "gram"))
                    a.ps, a.pd = a0.sb("ps", [P, COLS, H]), a0.sb("pd", [P, COLS, H])
                    edge_products(nc, g, a)
                    edge_weights(nc, g, a)
            g.sums = l0.sb("sums", [P, NT, OUTC])
            edge_sums(nc, g)
            finish_layer0(nc, g)
        with Scope(nc, "m") as m:
            g.lo_col, g.hi_col, g.win_col = (m.sb(n, [P, CITEMS + 4]) for n in ("lo_col", "hi_col", "win_col"))
            g.tiles1 = m.sb("tiles1", [1, CITEMS + 4], I32)
            items_matrix(nc, g)
            g.matrix = m.sb("matrix", [P, NT, NP], F16)
            count_matrix(nc, g)
            out_degrees(nc, g)
            deg_out, deg_in = 0, 1
            graph_layer(nc, g, "conv1", True, False, g.root_deg[:, deg_out], g.root_deg[:, deg_in], W1, b1, False)
            graph_layer(nc, g, "conv2", False, True, g.root_deg[:, deg_out], g.root_deg[:, deg_out], W2, b2, True)
            graph_layer(nc, g, "mean3", False, False, g.per_deg[:, deg_out], g.per_deg[:, deg_in], None, None, False, out)


_INS = ["x", "src", "dst", "edge_type_8", "L0_gnn_rel_weight", "L0_gnn_attn_vec", "L0_gnn_rel_emb", "L1_gnn_W",
        "L1_gnn_b", "L2_gnn_weight", "L2_gnn_bias"]


def kernel(**inputs):
    import numpy as _np
    import concourse.bacc as _bacc
    from concourse import mybir as _mybir
    from concourse.bass_utils import run_bass_kernel_spmd as _run

    nc = _bacc.Bacc("TRN2", target_bir_lowering=False, num_devices=1)
    arrays, args = {}, []
    for name in _INS:
        a = _np.ascontiguousarray(inputs[name])
        arrays[f"in_{name}"] = a
        args.append(nc.dram_tensor(f"in_{name}", a.shape, _mybir.dt.from_np(a.dtype), kind="ExternalInput").ap())
    args.append(nc.dram_tensor("out_0", (N, D), F32, kind="ExternalOutput").ap())
    build(nc, *args)
    r = _run(nc, [arrays], core_ids=[0])
    return r.results[0]["out_0"]
```

```python
from contextlib import ExitStack

import concourse.bass as bass
from concourse import mybir

P = 128
F32 = mybir.dt.float32
F16 = mybir.dt.float16
BF16 = mybir.dt.bfloat16
I32 = mybir.dt.int32
ALU = mybir.AluOpType
ACT = mybir.ActivationFunctionType
X = mybir.AxisListType.X

N, D = 3125, 64
E = 103125
R, H = 8, 4
NT = -(-N // P)
FULL = N // P
REST = N - FULL * P
NP = NT * P

PAIR = 2 * P
PAIR_ROWS = 408
EP = PAIR_ROWS * PAIR
WIN = 8
WINS = -(-N // WIN)
BLOCKS = EP // P

PI, PC = 108, 4
ITEMS = PI * PC
COLS = 2 * ITEMS
CI, CC = 100, 12
CITEMS = CI * CC
assert ITEMS >= -(-E // PAIR) + NT - 1 and ITEMS - (NT - 1) < PAIR_ROWS + 1
assert CITEMS >= -(-E // P) + WINS - 1 and CITEMS - 1 - (WINS - 1) < BLOCKS

NODE = D + 1 + R * H
HEAD = D + 2
MSG = H * HEAD
OUTC = MSG + 1
PAD_DST = 4000.0
C = 0.01
T_MAX = 1.0 - 1e-05
MAXNORM = (1.0 - 1e-05) / 0.1


def wait(eng, sem, value):
    eng.wait_ge(sem, value)
    eng.nop(nofuse=True)


def chain(eng, sem, start=0):
    count = [start]

    def step(ins):
        count[0] += 1
        ins.then_inc(sem, 1)
        eng.wait_ge(sem, count[0])
        return ins
    return step


class Scope:
    def __init__(self, nc, name):
        self.nc, self.name, self.ctx = nc, name, ExitStack()

    def __enter__(self):
        return self

    def __exit__(self, *a):
        return self.ctx.__exit__(*a)

    def sb(self, name, shape, dt=F32):
        return self.ctx.enter_context(self.nc.sbuf_tensor(f"{self.name}_{name}", shape, dt))

    def ps(self, name, shape, dt=F32):
        return self.ctx.enter_context(self.nc.psum_tensor(f"{self.name}_{name}", shape, dt))

    def sem(self, name):
        return self.ctx.enter_context(self.nc.semaphore(f"{self.name}_{name}"))

    def block(self):
        return self.ctx.enter_context(self.nc.Block())


def atanh_ratio_vector(v, eng, n2, t, w1, w2, out, n2_ready, norm_ready, ratio_ready, log_ready, k):
    v(eng.tensor_scalar(n2, n2, 1e-20, None, ALU.max))
    eng.sem_inc(n2_ready, 1)
    eng.wait_ge(norm_ready, k)
    v(eng.tensor_scalar(t, t, 0.1, 1e-10, ALU.mult, ALU.max))
    v(eng.tensor_scalar(t, t, T_MAX, None, ALU.min))
    v(eng.tensor_scalar(w1, t, -1.0, 1.0, ALU.mult, ALU.add))
    v(eng.reciprocal(w2, w1))
    v(eng.scalar_tensor_tensor(w1, t, 1.0, w2, ALU.add, ALU.mult))
    eng.sem_inc(ratio_ready, 1)
    v(eng.tensor_tensor(w2, t, t, ALU.mult))
    v(eng.tensor_scalar(out, w2, 1.0 / 9, 1.0 / 7, ALU.mult, ALU.add))
    v(eng.tensor_tensor(out, out, w2, ALU.mult))
    v(eng.scalar_tensor_tensor(out, out, 1.0 / 5, w2, ALU.add, ALU.mult))
    v(eng.scalar_tensor_tensor(out, out, 1.0 / 3, w2, ALU.add, ALU.mult))
    v(eng.tensor_scalar(out, out, 1.0, None, ALU.add))
    v(eng.reciprocal(w2, t))
    eng.wait_ge(log_ready, k)
    v(eng.scalar_tensor_tensor(w1, w1, 0.5, w2, ALU.mult, ALU.mult))
    v(eng.tensor_tensor(out, out, w1, ALU.subtract))
    v(eng.scalar_tensor_tensor(out, t, 0.1, out, ALU.is_lt, ALU.mult))
    v(eng.tensor_tensor(out, out, w1, ALU.add))


def atanh_ratio_scalar(eng, n2, t, w1, n2_ready, norm_ready, ratio_ready, log_ready, k):
    eng.wait_ge(n2_ready, k)
    eng.activation(t, n2, ACT.Sqrt).then_inc(norm_ready, 1)
    eng.wait_ge(ratio_ready, k)
    eng.activation(w1, w1, ACT.Ln).then_inc(log_ready, 1)


def layer_norm_vector(v, eng, x, sq, st, var_ready, root_ready, k):
    mean, var = st[:, 0, :], st[:, 1, :]
    bc = lambda a: a.unsqueeze(2).to_broadcast([P, NT, D])
    v(eng.tensor_reduce(mean, x, X, ALU.add))
    v(eng.tensor_scalar(mean, mean, 1.0 / D, None, ALU.mult))
    v(eng.tensor_tensor(x, x, bc(mean), ALU.subtract))
    v(eng.tensor_tensor(sq, x, x, ALU.mult))
    v(eng.tensor_reduce(var, sq, X, ALU.add))
    v(eng.tensor_scalar(var, var, 1.0 / D, 1e-05, ALU.mult, ALU.add))
    eng.sem_inc(var_ready, 1)
    eng.wait_ge(root_ready, k)
    v(eng.reciprocal(mean, var))
    v(eng.tensor_tensor(x, x, bc(mean), ALU.mult))


def layer_norm_scalar(eng, st, var_ready, root_ready, k):
    eng.wait_ge(var_ready, k)
    eng.activation(st[:, 1, :], st[:, 1, :], ACT.Sqrt).then_inc(root_ready, 1)


def constants(nc, g):
    with Scope(nc, "const") as s:
        filled, made = s.sem("filled"), s.sem("made")
        block = s.block()

        @block.gpsimd
        def _(pool):
            pool.memset(g.ident[:], 0.0).then_inc(filled, 1)
            pool.wait_ge(filled, 1)
            pool.affine_select(out=g.ident[:], in_=g.ident[:], compare_op=ALU.not_equal, fill=1.0, base=0,
                               pattern=[[-1, P]], channel_multiplier=1).then_inc(made, 1)
            pool.iota(g.count[:], [[1, P]], base=0, channel_multiplier=0,
                      allow_small_or_imprecise_dtypes=True).then_inc(made, 1)
            pool.iota(g.count_b[:], [[1, 2 * P]], base=0, channel_multiplier=0,
                      allow_small_or_imprecise_dtypes=True).then_inc(made, 1)

        @block.vector
        def _(dve):
            dve.wait_ge(made, 3)
            dve.tensor_copy(g.ident_b[:], g.ident[:]).then_inc(filled, 1)
            dve.tensor_copy(g.ident_h[:], g.ident[:]).then_inc(filled, 1)
            dve.wait_ge(filled, 3)


def stage_edges(nc, g, src, dst, et):
    with Scope(nc, "stage") as s:
        pad_dst, pad_zero = s.sb("pad_dst", [1, EP - E], I32), s.sb("pad_zero", [1, EP - E], I32)
        filled, stored, x_cleared = s.sem("filled"), s.sem("stored"), s.sem("x_cleared")
        block = s.block()

        @block.vector
        def _(dve):
            dve.memset(pad_dst[:], int(PAD_DST)).then_inc(filled, 1)
            dve.memset(pad_zero[:], 0).then_inc(filled, 1)
            dve.memset(g.x[:], 0.0).then_inc(x_cleared, 1)

        @block.sync
        def _(sp):
            row = lambda a: a.rearrange("(a n) -> a n", a=1)
            for flat, given in ((g.flat_src, src), (g.flat_dst, dst), (g.flat_et, et)):
                sp.dma_start(flat[0:E].rearrange("(a n) -> a n", a=125), given.rearrange("(a n) -> a n", a=125)).then_inc(stored, 16)
            sp.wait_ge(filled, 2)
            for flat, pad in ((g.flat_src, pad_zero), (g.flat_dst, pad_dst), (g.flat_et, pad_zero)):
                sp.dma_start(row(flat[E:EP]), pad[:]).then_inc(stored, 16)
            sp.wait_ge(x_cleared, 1)
            sp.dma_start(g.x[:, 0:FULL, :], g.x_in[0:FULL * P, :].rearrange("(t p) d -> p t d", p=P)).then_inc(stored, 16)
            sp.dma_start(g.x[0:REST, FULL, :], g.x_in[FULL * P:N, :]).then_inc(stored, 16)
            sp.wait_ge(stored, 8 * 16)


def walk(nc, g, s, name, row_len, lanes, cols, tile, tiles, unit):
    last_rows = EP // row_len
    lr, lc = 102, EP // row_len // 102
    last = s.sb(f"{name}_last", [lr, lc], I32)
    lastf = s.sb(f"{name}_lastf", [lr, lc])
    edge = s.sb(f"{name}_edge", [P, tiles - 1])
    below = s.sb(f"{name}_below", [lr, lc, tiles - 1], BF16)
    start = s.sb(f"{name}_start", [P, tiles - 1])
    number = s.sb(f"{name}_number", [lanes, cols])
    past = s.sb(f"{name}_past", [lanes, cols, tiles - 1], BF16)
    tile_of, row_of = s.sb(f"{name}_tile_of", [lanes, cols]), s.sb(f"{name}_row_of", [lanes, cols])
    row_int = s.sb(f"{name}_row_int", [lanes, cols], I32)
    tile_int = s.sb(f"{name}_tile_int", [lanes, cols], I32)
    starts = s.ps(f"{name}_starts", [P, 512])
    with Scope(nc, f"{name}_walk") as w:
        loaded, counted, compared, summed, own = (w.sem(n) for n in ("loaded", "counted", "compared", "summed", "own"))
        block = w.block()

        @block.sync
        def _(sp):
            ends = g.flat_dst.rearrange("(a b n) -> a b n", a=lr, n=row_len)
            sp.dma_start(last[:], ends[:, :, row_len - 1], allow_slow_non_contiguous=True).then_inc(loaded, 16)

        @block.gpsimd
        def _(pool):
            pool.iota(edge[:], [[tile, tiles - 1]], base=tile, channel_multiplier=0,
                      allow_small_or_imprecise_dtypes=True).then_inc(counted, 1)
            pool.iota(number[:], [[lanes, cols]], base=0, channel_multiplier=1,
                      allow_small_or_imprecise_dtypes=True).then_inc(counted, 1)

        @block.tensor
        def _(pe):
            pe.wait_ge(compared, 1)
            for c in range(lc):
                m = pe.matmul(starts[:, 0:tiles - 1], g.ones_b[0:lr, :], below[:, c, :], start=(c == 0), stop=(c == lc - 1))
            m.then_inc(summed, 1)

        @block.vector
        def _(dve):
            v = chain(dve, own)
            v(dve.memset(g.ones_b[:], 1.0))
            dve.wait_ge(loaded, 16)
            dve.wait_ge(counted, 2)
            v(dve.tensor_copy(lastf[:], last[:]))
            v(dve.tensor_tensor(below[:], lastf[:].unsqueeze(2).to_broadcast([lr, lc, tiles - 1]),
                                edge[0:lr, :].unsqueeze(1).to_broadcast([lr, lc, tiles - 1]), ALU.is_lt))
            dve.sem_inc(compared, 1)
            v(dve.tensor_scalar(start[:], edge[:], 1.0 / tile, None, ALU.mult))
            dve.wait_ge(summed, 1)
            v(dve.tensor_tensor(start[:], start[:], starts[:, 0:tiles - 1], ALU.add))
            v(dve.tensor_tensor(past[:], number[:].unsqueeze(2).to_broadcast([lanes, cols, tiles - 1]),
                                start[0:lanes, :].unsqueeze(1).to_broadcast([lanes, cols, tiles - 1]), ALU.is_ge))
            v(dve.tensor_reduce(tile_of[:], past[:], X, ALU.add))
            v(dve.tensor_tensor(row_of[:], number[:], tile_of[:], ALU.subtract))
            v(dve.tensor_copy(row_int[:], row_of[:]))
            v(dve.tensor_scalar(tile_int[:], tile_of[:], unit, None, ALU.mult))
    return tile_of, tile_int, row_int


def gather_rows(nc, g, name, flats, outs, row_int, lanes, cols, row_len, tile_int, tile_dram):
    with Scope(nc, f"{name}_rows") as w:
        landed, stored = w.sem("landed"), w.sem("stored")
        block = w.block()

        @block.gpsimd
        def _(pool):
            for flat, out in zip(flats, outs):
                for c in range(cols):
                    pool.indirect_dma_start(
                        out=out[:, c, :], out_offset=None, in_=flat.rearrange("(r n) -> r n", n=row_len),
                        in_offset=bass.IndirectOffsetOnAxis(ap=row_int[:, c:c + 1], axis=0)).then_inc(landed, 16)
            pool.wait_ge(landed, 16 * len(flats) * cols)

        @block.sync
        def _(sp):
            sp.dma_start(tile_dram[0:lanes * cols].rearrange("(c p) -> p c", p=lanes), tile_int[:],
                         allow_slow_non_contiguous=True).then_inc(stored, 16)
            sp.wait_ge(stored, 16)


def items_layer0(nc, g):
    with Scope(nc, "it0") as s:
        tile_of, tile_int, row_int = walk(nc, g, s, "it0", PAIR, PI, PC, P, NT, 1.0)
        rows = [s.sb(n, [PI, PC, PAIR], I32) for n in ("src", "dst", "et")]
        gather_rows(nc, g, "it0", (g.flat_src, g.flat_dst, g.flat_et), rows, row_int, PI, PC, PAIR, tile_int, g.tile0_dram)
        srcf, dstf, etf, lane, key, w = (s.sb(n, [PI, PC, PAIR]) for n in ("srcf", "dstf", "etf", "lane", "key", "w"))
        guard = s.sb("guard", [1, 2])
        turned = [s.ps(f"turned{k}", [P, PC, P]) for k in range(2)]
        with Scope(nc, "it0b") as q:
            own, ready, turn, copied, stored = (q.sem(n) for n in ("own", "ready", "turn", "copied", "stored"))
            block = q.block()
            jobs = [(srcf, g.src_col), (etf, g.msg_col), (lane, g.lane_col), (w, g.et_col)]

            @block.vector
            def _(dve):
                v = chain(dve, own)
                v(dve.memset(guard[:], -1.0))
                v(dve.memset(g.lane_col[:, COLS:], -1.0))
                for f, i in zip((srcf, dstf, w), rows):
                    v(dve.tensor_copy(f[:], i[:]))
                v(dve.scalar_tensor_tensor(etf[:], srcf[:], float(R), w[:], ALU.mult, ALU.add))
                for c in range(PC):
                    v(dve.tensor_scalar(key[:, c, 0:1], tile_of[:, c:c + 1], float(P), None, ALU.mult))
                    v(dve.tensor_scalar(lane[:, c, :], dstf[:, c, :], key[:, c, 0:1], None, ALU.subtract))
                v(dve.tensor_scalar(key[:], lane[:], 0.0, None, ALU.is_ge))
                v(dve.scalar_tensor_tensor(key[:], lane[:], float(P), key[:], ALU.is_lt, ALU.mult))
                v(dve.scalar_tensor_tensor(key[:], dstf[:], 1.0, key[:], ALU.add, ALU.mult))
                dve.sem_inc(ready, 1)
                n = 0
                for _, col in jobs:
                    for k in range(2):
                        n += 1
                        dve.wait_ge(turn, n)
                        dve.tensor_copy(col[:, 0:COLS].rearrange("p (c i k) -> p c i k", c=PC, k=2)[:, :, :, k],
                                        turned[k][:, :, 0:PI]).then_inc(copied, 1)
                dve.wait_ge(copied, n)

            @block.tensor
            def _(pe):
                pe.wait_ge(ready, 1)
                n = 0
                for arr, _ in jobs:
                    for k in range(2):
                        if n >= 2:
                            pe.wait_ge(copied, n - 1)
                        for c in range(PC):
                            m = pe.transpose(turned[k][:, c, 0:PI], arr[:, c, k * P:(k + 1) * P], g.ident[0:PI, 0:PI])
                        m.then_inc(turn, 1)
                        n += 1

            @block.sync
            def _(sp):
                sp.wait_ge(ready, 1)
                sp.dma_start(g.key_dram[1:1 + ITEMS * PAIR].rearrange("(c p n) -> p c n", c=PC, n=PAIR), key[:]).then_inc(stored, 16)
                ends = g.key_dram[0:2 + ITEMS * PAIR].rearrange("(a n) -> a n", a=1)
                sp.dma_start(ends[:, 0:1], guard[:, 0:1]).then_inc(stored, 16)
                sp.dma_start(ends[:, 1 + ITEMS * PAIR:2 + ITEMS * PAIR], guard[:, 1:2]).then_inc(stored, 16)
                sp.wait_ge(stored, 48)


def node_table(nc, g, attn_vec, xT, factor):
    with Scope(nc, "node") as s:
        av, avT = s.sb("av", [R * H, D]), s.sb("avT", [D, R * H])
        sq = s.sb("sq", [P, NT, D])
        n2, t, w1, w2 = (s.sb(n, [P, NT]) for n in ("n2", "t", "w1", "w2"))
        px = [s.ps(f"px{k}", [P, 4, P]) for k in range(2)]
        pv, pd = s.ps("pv", [P, 512]), s.ps("pd", [P, 2, 512])
        loaded, own, turn, turned, dots, table, stored, n2_ready, norm_ready, ratio_ready, log_ready = (
            s.sem(n) for n in ("loaded", "own", "turn", "turned", "dots", "table", "stored", "n2_ready", "norm_ready",
                               "ratio_ready", "log_ready"))
        block = s.block()
        groups = range(0, NT, 4)
        half = 512 // (R * H)

        @block.sync
        def _(sp):
            sp.dma_start(av[:], attn_vec.rearrange("r h d -> (r h) d")).then_inc(loaded, 16)
            sp.wait_ge(table, 1)
            sp.dma_start(g.node_dram.rearrange("(t p) d -> p t d", p=P), g.node[:]).then_inc(stored, 16)
            sp.wait_ge(stored, 16)

        @block.tensor
        def _(pe):
            pe.wait_ge(loaded, 16)
            pe.transpose(pv[0:D, 0:R * H], av[:], g.ident[0:R * H, 0:R * H]).then_inc(turn, 1)
            for n, q in enumerate(groups):
                if n >= 2:
                    pe.wait_ge(turned, n)
                for i in range(q, min(q + 4, NT)):
                    m = pe.transpose(px[n % 2][0:D, i - q, :], g.x[:, i, :], g.ident[:])
                m.then_inc(turn, 1)
            pe.wait_ge(turned, 1 + len(groups))
            for i in range(NT):
                a = i % half * R * H
                m = pe.matmul(pd[:, i // half, a:a + R * H], xT[:, i, :], avT[:], start=True, stop=True)
            m.then_inc(dots, 1)

        @block.scalar
        def _(act):
            atanh_ratio_scalar(act, n2[:], t[:], w1[:], n2_ready, norm_ready, ratio_ready, log_ready, 1)

        @block.vector
        def _(dve):
            v = chain(dve, own)
            dve.wait_ge(turn, 1)
            dve.tensor_copy(avT[:], pv[0:D, 0:R * H]).then_inc(turned, 1)
            for n, q in enumerate(groups):
                dve.wait_ge(turn, n + 2)
                k = min(4, NT - q)
                dve.tensor_copy(xT[:, q:q + k, :], px[n % 2][0:D, 0:k, :]).then_inc(turned, 1)
            v(dve.tensor_copy(g.node[:, :, 0:D], g.x[:]))
            v(dve.tensor_tensor(sq[:], g.x[:], g.x[:], ALU.mult))
            v(dve.tensor_reduce(n2[:], sq[:], X, ALU.add))
            v(dve.tensor_copy(g.node[:, :, D:D + 1], n2[:].unsqueeze(2)))
            dve.wait_ge(dots, 1)
            for b in range(2):
                k = min(half, NT - b * half)
                v(dve.tensor_copy(g.node[:, b * half:b * half + k, D + 1:NODE],
                                  pd[:, b, 0:k * R * H].rearrange("p (t c) -> p t c", t=k)))
            dve.sem_inc(table, 1)
            atanh_ratio_vector(v, dve, n2[:], t[:], w1[:], w2[:], factor[:], n2_ready, norm_ready, ratio_ready, log_ready, 1)


def message_table(nc, g, rel_weight, xT, factor):
    with Scope(nc, "msg") as s:
        w = s.sb("w", [D, R, H, D])
        m2, nrm, th, u, lam, coef = (s.sb(n, [P, 2, R * H]) for n in ("m2", "nrm", "th", "u", "lam", "coef"))
        sq = s.sb("sq", [P, 2, R * H, D])
        row = s.sb("row", [P, 2, R * H, HEAD])
        pm = [s.ps(f"pm{k}", [P, R * H, D]) for k in range(2)]
        loaded, own, product, squared, m2_ready, root, tanh_done, row_ready = (
            s.sem(n) for n in ("loaded", "own", "product", "squared", "m2_ready", "root", "tanh_done", "row_ready"))
        row_stored = [s.sem(f"row_stored{b}") for b in range(2)]
        block = s.block()

        @block.sync
        def _(sp):
            sp.dma_start(w[:], rel_weight.rearrange("r h i o -> i r h o")).then_inc(loaded, 16)
            for i in range(NT):
                b = i % 2
                sp.wait_ge(row_ready, i + 1)
                sp.dma_start(g.msg_dram[i * P * R:(i + 1) * P * R, :].rearrange("(p r) c -> p (r c)", r=R),
                             row[:, b].rearrange("p a c -> p (a c)")).then_inc(row_stored[b], 16)
            sp.wait_ge(row_stored[0], 16 * ((NT + 1) // 2))
            sp.wait_ge(row_stored[1], 16 * (NT // 2))

        @block.tensor
        def _(pe):
            pe.wait_ge(loaded, 16)
            for i in range(NT):
                if i >= 2:
                    pe.wait_ge(row_ready, i - 1)
                for q in range(R // 2):
                    m = pe.matmul(pm[i % 2][:, q * 2 * H:(q + 1) * 2 * H, :].rearrange("p a d -> p (a d)"), xT[:, i, :],
                                  w[:, 2 * q:2 * q + 2].rearrange("i r h o -> i (r h o)"), start=True, stop=True)
                m.then_inc(product, 1)

        @block.scalar
        def _(act):
            for i in range(NT):
                b = i % 2
                act.wait_ge(product, i + 1)
                if i >= 2:
                    act.wait_ge(row_ready, i - 1)
                act.activation(sq[:, b], pm[b][:], ACT.Square).then_inc(squared, 1)
                act.wait_ge(m2_ready, i + 1)
                act.activation(nrm[:, b], m2[:, b], ACT.Sqrt).then_inc(root, 1)
                act.wait_ge(root, i + 1)
                act.activation(th[:, b], nrm[:, b], ACT.Tanh, scale=0.1).then_inc(tanh_done, 1)

        @block.vector
        def _(dve):
            v = chain(dve, own)
            v(dve.memset(row[:, :, :, D + 1:HEAD], 1.0))
            for i in range(NT):
                b = i % 2
                f = factor[:, i:i + 1]
                dve.wait_ge(squared, i + 1)
                v(dve.tensor_reduce(m2[:, b], sq[:, b], X, ALU.add))
                v(dve.tensor_scalar(m2[:, b], m2[:, b], f, f, ALU.mult, ALU.mult))
                v(dve.tensor_scalar(m2[:, b], m2[:, b], 1e-20, None, ALU.max))
                dve.sem_inc(m2_ready, 1)
                dve.wait_ge(tanh_done, i + 1)
                v(dve.tensor_tensor(u[:, b], th[:, b], th[:, b], ALU.mult))
                v(dve.tensor_scalar(u[:, b], u[:, b], -1.0, 1.0, ALU.mult, ALU.add))
                v(dve.tensor_scalar(u[:, b], u[:, b], 1e-06, 0.5, ALU.add, ALU.mult))
                v(dve.reciprocal(lam[:, b], u[:, b]))
                v(dve.reciprocal(coef[:, b], nrm[:, b]))
                v(dve.tensor_tensor(coef[:, b], coef[:, b], th[:, b], ALU.mult))
                v(dve.tensor_scalar(coef[:, b], coef[:, b], f, 10.0, ALU.mult, ALU.mult))
                v(dve.tensor_tensor(coef[:, b], coef[:, b], lam[:, b], ALU.mult))
                if i >= 2:
                    dve.wait_ge(row_stored[b], 16 * (i // 2))
                v(dve.tensor_copy(row[:, b, :, D:D + 1], lam[:, b].unsqueeze(2)))
                v(dve.tensor_tensor(row[:, b, :, 0:D], pm[b][:], coef[:, b].unsqueeze(2).to_broadcast([P, R * H, D]), ALU.mult))
                dve.sem_inc(row_ready, 1)


def edge_products(nc, g, a):
    with Scope(nc, "prod") as s:
        idx = s.sb("idx", [P, 2, 4], I32)
        xs = s.sb("xs", [P, 2, 4, NODE])
        oh = s.sb("oh", [P, 2, 4, P], BF16)
        ohT = s.sb("ohT", [P, 2, 4, P])
        rel = s.sb("rel", [P, 2, 4, R])
        prod = s.sb("prod", [P, 2, 4, D])
        ws, wd = s.sb("ws", [P, 2, 4, R * H]), s.sb("wd", [P, 2, 4, R * H])
        turned = [s.ps(f"turned{k}", [P, 4, P], BF16) for k in range(2)]
        xd = [s.ps(f"xd{k}", [P, 4, P]) for k in range(2)]
        landed = [s.sem(f"landed{k}") for k in range(2)]
        idx_ready, slot_free, oh_ready, turn, ohT_ready, xd_ready, sq_taken, own = (
            s.sem(n) for n in ("idx_ready", "slot_free", "oh_ready", "turn", "ohT_ready", "xd_ready", "sq_taken", "own"))
        primed = s.sem("primed")
        tiles = s.sb("tiles", [1, ITEMS], I32)
        block = s.block()
        STEPS = COLS // 4
        OWN = 8

        @block.sync
        def _(sp):
            sp.dma_start(tiles[:], g.tile0_dram[0:ITEMS].rearrange("(a n) -> a n", a=1)).then_inc(primed, 16)
            sp.wait_ge(primed, 16)

        @block.gpsimd
        def _(pool):
            with pool.Fori(0, STEPS // 2) as turn_of_two:
                it = turn_of_two * 2
                for k in range(2):
                    wait(pool, slot_free, it + k + 1)
                    pool.tensor_copy(idx[:, k, :], g.src_col[:, bass.ds((it + k) * 4, 4)]).then_inc(idx_ready, 1)
                    wait(pool, idx_ready, it + k + 1)
                    for j in range(4):
                        pool.indirect_dma_start(
                            out=xs[:, k, j, :], out_offset=None, in_=g.node_dram[:, :],
                            in_offset=bass.IndirectOffsetOnAxis(ap=idx[:, k, j:j + 1], axis=0)).then_inc(landed[k], 16)

        @block.tensor
        def _(pe):
            pe.wait_ge(primed, 16)
            with pe.Fori(0, STEPS // 2) as turn_of_two:
                it = turn_of_two * 2
                for k in range(2):
                    wait(pe, oh_ready, it + k + 1)
                    for j in range(4):
                        m = pe.transpose(turned[k][:, j, :], oh[:, k, j, :], g.ident_b[:])
                    m.then_inc(turn, 1)
                    wait(pe, ohT_ready, it + k + 1)
                    for j in range(2):
                        tile = pe.value_load(tiles[0:1, bass.ds((it + k) * 2 + j, 1)], min_val=0, max_val=NT - 1)
                        for h in range(2):
                            m = pe.matmul(xd[k][:, 2 * j + h, 0:NODE], ohT[:, k, 2 * j + h, :],
                                          g.node[:, bass.ds(tile, 1), :].rearrange("p a d -> p (a d)"), start=True, stop=True)
                    m.then_inc(xd_ready, 1)

        @block.scalar
        def _(act):
            with act.Fori(0, STEPS // 2) as turn_of_two:
                it = turn_of_two * 2
                for k in range(2):
                    wait(act, turn, it + k + 1)
                    act.copy(ohT[:, k], turned[k][:]).then_inc(ohT_ready, 1)
                    wait(act, landed[k], it * 32 + 64)
                    act.copy(a.s2[:, bass.ds((it + k) * 4, 4)], xs[:, k, :, D]).then_inc(sq_taken, 1)

        @block.vector
        def _(dve):
            def one_hot(slot, cols):
                dve.tensor_tensor(oh[:, slot], g.count[:].unsqueeze(1).to_broadcast([P, 4, P]),
                                  g.lane_col[:, cols].unsqueeze(2).to_broadcast([P, 4, P]), ALU.is_equal).then_inc(oh_ready, 1)

            dve.sem_inc(slot_free, 2)
            one_hot(0, slice(0, 4))
            with dve.Fori(0, STEPS // 2) as turn_of_two:
                it = turn_of_two * 2
                for k in range(2):
                    base = (it + k) * OWN
                    cols = bass.ds((it + k) * 4, 4)
                    one_hot(1 - k, bass.ds((it + k) * 4 + 4, 4))
                    dve.tensor_tensor(rel[:, k], g.count[:, 0:R].unsqueeze(1).to_broadcast([P, 4, R]),
                                      g.et_col[:, cols].unsqueeze(2).to_broadcast([P, 4, R]), ALU.is_equal).then_inc(own, 1)
                    wait(dve, landed[k], it * 32 + 64)
                    wait(dve, own, base + 1)
                    picked = rel[:, k].unsqueeze(3).to_broadcast([P, 4, R, H])
                    dve.tensor_tensor(ws[:, k].rearrange("p j (r h) -> p j r h", r=R),
                                      xs[:, k, :, D + 1:NODE].rearrange("p j (r h) -> p j r h", r=R), picked,
                                      ALU.mult).then_inc(own, 1)
                    wait(dve, own, base + 2)
                    dve.tensor_reduce(a.ps[:, cols, :], ws[:, k].rearrange("p j (r h) -> p j h r", r=R), X,
                                      ALU.add).then_inc(own, 1)
                    wait(dve, xd_ready, it + k + 1)
                    dve.tensor_tensor(prod[:, k], xd[k][:, :, 0:D], xs[:, k, :, 0:D], ALU.mult).then_inc(own, 1)
                    dve.tensor_tensor(wd[:, k].rearrange("p j (r h) -> p j r h", r=R),
                                      xd[k][:, :, D + 1:NODE].rearrange("p j (r h) -> p j r h", r=R), picked,
                                      ALU.mult).then_inc(own, 1)
                    wait(dve, own, base + 4)
                    dve.tensor_reduce(a.gram[:, cols], prod[:, k], X, ALU.add).then_inc(own, 1)
                    wait(dve, own, base + 5)
                    dve.tensor_reduce(a.pd[:, cols, :], wd[:, k].rearrange("p j (r h) -> p j h r", r=R), X,
                                      ALU.add).then_inc(own, 1)
                    dve.tensor_copy(a.d2[:, cols], xd[k][:, :, D]).then_inc(own, 1)
                    wait(dve, sq_taken, it + k + 1)
                    wait(dve, own, base + 8)
                    dve.sem_inc(slot_free, 1)


def edge_weights(nc, g, a):
    with Scope(nc, "wts") as s:
        w0, w1, w2, w3 = (s.sb(n, [P, COLS]) for n in ("w0", "w1", "w2", "w3"))
        own, n2_ready, norm_ready, ratio_ready, log_ready = (
            s.sem(n) for n in ("own", "n2_ready", "norm_ready", "ratio_ready", "log_ready"))
        block = s.block()
        G, s2, d2 = a.gram[:], a.s2[:], a.d2[:]

        @block.scalar
        def _(act):
            atanh_ratio_scalar(act, G, w0[:], w1[:], n2_ready, norm_ready, ratio_ready, log_ready, 1)

        @block.vector
        def _(dve):
            v = chain(dve, own)
            v(dve.tensor_scalar(w0[:], G, -2 * C, 1.0, ALU.mult, ALU.add))
            v(dve.tensor_tensor(w1[:], s2, d2, ALU.mult))
            v(dve.scalar_tensor_tensor(w1[:], w1[:], C * C, w0[:], ALU.mult, ALU.add))
            v(dve.tensor_scalar(w1[:], w1[:], 1e-10, None, ALU.max))
            v(dve.reciprocal(w3[:], w1[:]))
            v(dve.scalar_tensor_tensor(w0[:], d2, C, w0[:], ALU.mult, ALU.add))
            v(dve.tensor_scalar(w1[:], s2, -C, 1.0, ALU.mult, ALU.add))
            v(dve.tensor_tensor(w0[:], w0[:], w3[:], ALU.mult))
            v(dve.tensor_tensor(w1[:], w1[:], w3[:], ALU.mult))
            v(dve.tensor_tensor(a.ps[:], a.ps[:], w0[:].unsqueeze(2).to_broadcast([P, COLS, H]), ALU.mult))
            v(dve.tensor_tensor(a.pd[:], a.pd[:], w1[:].unsqueeze(2).to_broadcast([P, COLS, H]), ALU.mult))
            v(dve.tensor_tensor(a.ps[:], a.ps[:], a.pd[:], ALU.subtract))
            v(dve.scalar_tensor_tensor(w2[:], G, -2.0, w0[:], ALU.mult, ALU.mult))
            v(dve.tensor_tensor(w2[:], w2[:], w1[:], ALU.mult))
            v(dve.tensor_tensor(w0[:], w0[:], w0[:], ALU.mult))
            v(dve.tensor_tensor(w0[:], w0[:], s2, ALU.mult))
            v(dve.tensor_tensor(w1[:], w1[:], w1[:], ALU.mult))
            v(dve.tensor_tensor(w1[:], w1[:], d2, ALU.mult))
            v(dve.tensor_tensor(w0[:], w0[:], w1[:], ALU.add))
            v(dve.tensor_tensor(G, w0[:], w2[:], ALU.add))
            atanh_ratio_vector(v, dve, G, w0[:], w1[:], w2[:], w3[:], n2_ready, norm_ready, ratio_ready, log_ready, 1)
            v(dve.tensor_tensor(a.ps[:], a.ps[:], w3[:].unsqueeze(2).to_broadcast([P, COLS, H]), ALU.mult))
            v(dve.scalar_tensor_tensor(a.ps[:], a.ps[:], 0.2, a.ps[:], ALU.mult, ALU.max))

    SEQ = 8 * P
    BIG = -1e30
    with Scope(nc, "scan") as s:
        sc = s.sb("sc", [PI, H, SEQ])
        fwd, bwd = s.sb("fwd", [PI, H, SEQ]), s.sb("bwd", [PI, H, SEQ])
        kp, kc, kn = (s.sb(n, [PI, SEQ]) for n in ("kp", "kc", "kn"))
        ends = s.sb("ends", [PI, 4, H])
        chainT = s.sb("chainT", [H, 4, PI])
        carry = s.sb("carry", [H, 2, PI + 1])
        cin = s.sb("cin", [PI, 2, H])
        turned = [s.ps(f"turned{k}", [P, 4, P]) for k in range(2)]
        pe_ends = s.ps("ends_turned", [P, 512])
        loaded, turn, taken, own, ends_ready, endsT, carry_ready, carried, ex_ready, back, backed = (
            s.sem(n) for n in ("loaded", "turn", "taken", "own", "ends_ready", "endsT", "carry_ready", "carried",
                               "ex_ready", "back", "backed"))
        block = s.block()

        @block.sync
        def _(sp):
            for d, k in enumerate((kp, kc, kn)):
                sp.dma_start(k[:], g.key_dram[d:d + PI * SEQ].rearrange("(q n) -> q n", n=SEQ)).then_inc(loaded, 16)

        @block.tensor
        def _(pe):
            n = 0
            for h in range(H):
                for q in range(0, 8, 4):
                    if n >= 2:
                        pe.wait_ge(taken, n - 1)
                    for m in range(q, q + 4):
                        last = pe.transpose(turned[n % 2][0:PI, m - q, :], a.ps[:, m::8, h], g.ident[:])
                    last.then_inc(turn, 1)
                    n += 1
            for d in range(2):
                pe.wait_ge(ends_ready, d + 1)
                for b in range(2):
                    m = pe.transpose(pe_ends[0:H, b * P:b * P + PI], ends[:, 2 * d + b, :], g.ident[0:PI, 0:PI])
                m.then_inc(endsT, 1)
                pe.wait_ge(carry_ready, d + 1)
                c = carry[:, 0, 0:PI] if d == 0 else carry[:, 1, 1:PI + 1]
                pe.transpose(pe_ends[0:PI, 256:256 + H], c, g.ident[0:H, 0:H]).then_inc(carried, 1)
            n = 0
            pe.wait_ge(ex_ready, 1)
            pe.wait_ge(taken, 8)
            for h in range(H):
                for q in range(0, 8, 4):
                    if n >= 2:
                        pe.wait_ge(backed, n - 1)
                    for m in range(q, q + 4):
                        last = pe.transpose(turned[n % 2][:, m - q, 0:PI], sc[:, h, m * P:(m + 1) * P], g.ident[0:PI, 0:PI])
                    last.then_inc(back, 1)
                    n += 1

        @block.scalar
        def _(act):
            act.wait_ge(carry_ready, 3)
            act.activation(sc[:], sc[:], ACT.Exp).then_inc(ex_ready, 1)

        @block.vector
        def _(dve):
            v = chain(dve, own)
            n = 0
            for h in range(H):
                for q in range(0, 8, 4):
                    dve.wait_ge(turn, n + 1)
                    dve.tensor_copy(sc[:, h, q * P:(q + 4) * P].rearrange("p (m e) -> p m e", m=4), turned[n % 2][0:PI]).then_inc(taken, 1)
                    n += 1
            dve.wait_ge(taken, n)
            dve.wait_ge(loaded, 48)
            v(dve.tensor_tensor(kp[:], kp[:], kc[:], ALU.not_equal))
            v(dve.tensor_scalar(kp[:], kp[:], BIG, None, ALU.mult))
            v(dve.tensor_tensor(kn[:], kn[:], kc[:], ALU.not_equal))
            v(dve.tensor_scalar(kn[:], kn[:], BIG, None, ALU.mult))
            v(dve.memset(carry[:], BIG))
            for d, (brk, src, out) in enumerate(((kp, sc, fwd), (kn, fwd, bwd))):
                flip = (lambda t: t) if d == 0 else (lambda t: t[:, ::-1])
                last = SEQ - 1 if d == 0 else 0
                for h in range(H):
                    v(dve.tensor_tensor_scan(flip(out[:, h, :]), flip(brk[:]), flip(src[:, h, :]), BIG, ALU.add, ALU.max))
                v(dve.tensor_copy(ends[:, 2 * d, :], out[:, :, last]))
                v(dve.tensor_reduce(ends[:, 2 * d + 1, 0:1], brk[:], X, ALU.min))
                v(dve.tensor_copy(ends[:, 2 * d + 1, 1:H], ends[:, 2 * d + 1, 0:1].to_broadcast([PI, H - 1])))
                dve.sem_inc(ends_ready, 1)
                dve.wait_ge(endsT, d + 1)
                v(dve.tensor_copy(chainT[:, 2 * d:2 * d + 2, :], pe_ends[0:H, 0:2 * P].rearrange("p (b n) -> p b n", b=2)[:, :, 0:PI]))
                to = carry[:, 0, 1:PI + 1] if d == 0 else carry[:, 1, 0:PI]
                v(dve.tensor_tensor_scan(flip(to), flip(chainT[:, 2 * d + 1, :]), flip(chainT[:, 2 * d, :]), BIG, ALU.add, ALU.max))
                dve.sem_inc(carry_ready, 1)
                dve.wait_ge(carried, d + 1)
                v(dve.tensor_copy(cin[:, d, :], pe_ends[0:PI, 256:256 + H]))
                for h in range(H):
                    v(dve.tensor_tensor_scan(flip(out[:, h, :]), flip(brk[:]), flip(src[:, h, :]), cin[:, d, h:h + 1], ALU.add, ALU.max))
            v(dve.tensor_tensor(sc[:], sc[:], bwd[:], ALU.subtract))
            dve.sem_inc(carry_ready, 1)
            n = 0
            for h in range(H):
                for q in range(0, 8, 4):
                    dve.wait_ge(back, n + 1)
                    out = g.ex[:].rearrange("p (q m) h -> p m q h", m=8)[:, q:q + 4, :, h]
                    dve.tensor_copy(out, turned[n % 2][:, :, 0:PI]).then_inc(backed, 1)
                    n += 1
            dve.wait_ge(backed, n)


def edge_sums(nc, g):
    with Scope(nc, "sums") as s:
        S = 4
        SLOTS = 4
        STEPS = COLS // S
        idx = s.sb("idx", [P, SLOTS, S], I32)
        msg = s.sb("msg", [P, SLOTS, S, MSG])
        val = s.sb("val", [P, 2, S, OUTC])
        oh = s.sb("oh", [P, 2, S, P])
        part = [s.ps(f"part{k}", [P, 2, 512]) for k in range(2)]
        tiles = s.sb("tiles", [1, ITEMS + 2], I32)
        landed = [s.sem(f"landed{k}") for k in range(SLOTS)]
        idx_ready, slot_free, val_ready, part_ready, primed, own, cleared = (
            s.sem(n) for n in ("idx_ready", "slot_free", "val_ready", "part_ready", "primed", "own", "cleared"))
        block = s.block()

        @block.sync
        def _(sp):
            sp.wait_ge(cleared, 1)
            sp.dma_start(tiles[:, 2:], g.tile0_dram[0:ITEMS].rearrange("(a n) -> a n", a=1)).then_inc(primed, 16)
            sp.wait_ge(primed, 16)

        @block.gpsimd
        def _(pool):
            with pool.Fori(0, STEPS // SLOTS) as r:
                for k in range(SLOTS):
                    wait(pool, slot_free, r * SLOTS + k + 1)
                    pool.tensor_copy(idx[:, k, :], g.msg_col[:, bass.ds((r * SLOTS + k) * S, S)]).then_inc(idx_ready, 1)
                    wait(pool, idx_ready, r * SLOTS + k + 1)
                    for j in range(S):
                        pool.indirect_dma_start(
                            out=msg[:, k, j, :], out_offset=None, in_=g.msg_dram[:, :],
                            in_offset=bass.IndirectOffsetOnAxis(ap=idx[:, k, j:j + 1], axis=0)).then_inc(landed[k], 16)

        @block.tensor
        def _(pe):
            with pe.Fori(0, STEPS // 2) as r:
                for k in range(2):
                    wait(pe, val_ready, r * 2 + k + 1)
                    for j in range(2):
                        for h in range(2):
                            m = pe.matmul(part[k][:, j, 0:OUTC], oh[:, k, 2 * j + h, :], val[:, k, 2 * j + h, :],
                                          start=(h == 0), stop=(h == 1))
                    m.then_inc(part_ready, 1)

        @block.vector
        def _(dve):
            def tiles_of(items):
                return nc.values_load_multi_w_load_instructions(
                    tiles[0:1, items], engines=[mybir.EngineType.DVE], min_val=0, max_val=NT - 1,
                    skip_runtime_bounds_check_because="an item's tile is a count of NT - 1 comparisons")[1]

            def add(part, at, j):
                to = g.sums[:, bass.ds(at[j], 1), :].rearrange("p a c -> p (a c)")
                dve.tensor_tensor(to, to, part[:, j, 0:OUTC], ALU.add).then_inc(own, 1)

            dve.memset(tiles[:, 0:2], 0).then_inc(cleared, 1)
            dve.memset(g.sums[:], 0.0)
            dve.memset(val[:, :, :, MSG:OUTC], 1.0)
            dve.memset(part[1][:], 0.0).then_inc(cleared, 1)
            dve.wait_ge(cleared, 2)
            dve.wait_ge(primed, 16)
            dve.sem_inc(slot_free, SLOTS)
            dve.sem_inc(part_ready, 1)
            with dve.Fori(0, STEPS // SLOTS) as r:
                at = tiles_of(bass.ds(r * 2 * SLOTS, 2 * SLOTS))
                for k in range(SLOTS):
                    step = r * SLOTS + k
                    cols = bass.ds(step * S, S)
                    h = k % 2
                    dve.tensor_tensor(oh[:, h], g.count[:].unsqueeze(1).to_broadcast([P, S, P]),
                                      g.lane_col[:, cols].unsqueeze(2).to_broadcast([P, S, P]), ALU.is_equal).then_inc(own, 1)
                    wait(dve, landed[k], r * (S * 16) + S * 16)
                    dve.tensor_tensor(val[:, h, :, 0:MSG].rearrange("p j (h c) -> p j h c", h=H),
                                      msg[:, k].rearrange("p j (h c) -> p j h c", h=H),
                                      g.ex[:, cols, :].unsqueeze(3).to_broadcast([P, S, H, HEAD]), ALU.mult).then_inc(own, 1)
                    dve.wait_ge(own, 4 * k + 2)
                    dve.sem_inc(val_ready, 1)
                    dve.sem_inc(slot_free, 1)
                    wait(dve, part_ready, step + 1)
                    for j in range(2):
                        add(part[1 - h], at[2 * k:2 * k + 2], j)
                        dve.wait_ge(own, 4 * k + 2 + j + 1)
                dve.sem_clear(own)
            dve.wait_ge(part_ready, STEPS + 1)
            at = tiles_of(slice(ITEMS, ITEMS + 2))
            for j in range(2):
                add(part[1], at, j)
                dve.wait_ge(own, j + 1)


def finish_layer0(nc, g):
    with Scope(nc, "fin0") as s:
        TH = NT * H
        sq = s.sb("sq", [P, NT, D])
        sq4 = s.sb("sq4", [P, NT, D])
        h_new = s.sb("h_new", [P, NT, D])
        inv, den, coef, n2, t, w1, w2, f = (s.sb(n, [P, NT, H]) for n in ("inv", "den", "coef", "n2", "t", "w1", "w2", "f"))
        a2, nrm, th = (s.sb(n, [P, NT]) for n in ("a2", "nrm", "th"))
        st = s.sb("st", [P, 2, NT])
        own, n2_ready, norm_ready, ratio_ready, log_ready, a2_ready, root, tanh_done, var_ready, root_ready, shrink_ready = (
            s.sem(n) for n in ("own", "n2_ready", "norm_ready", "ratio_ready", "log_ready", "a2_ready", "root",
                               "tanh_done", "var_ready", "root_ready", "shrink_ready"))
        block = s.block()
        heads = g.sums[:, :, 0:MSG].rearrange("p t (h c) -> p t h c", h=H)

        @block.scalar
        def _(act):
            atanh_ratio_scalar(act, n2[:], t[:], w1[:], n2_ready, norm_ready, ratio_ready, log_ready, 1)
            act.wait_ge(n2_ready, 2)
            act.activation(w1[:], n2[:], ACT.Sqrt).then_inc(shrink_ready, 1)
            act.wait_ge(a2_ready, 1)
            act.activation(nrm[:], a2[:], ACT.Sqrt).then_inc(root, 1)
            act.wait_ge(root, 1)
            act.activation(th[:], nrm[:], ACT.Tanh, scale=0.1).then_inc(tanh_done, 1)
            layer_norm_scalar(act, st, var_ready, root_ready, 1)

        @block.vector
        def _(dve):
            v = chain(dve, own)
            v(dve.tensor_scalar(inv[:], heads[:, :, :, D + 1], 0.5, None, ALU.max))
            v(dve.reciprocal(inv[:], inv[:]))
            v(dve.tensor_tensor(den[:], heads[:, :, :, D], inv[:], ALU.mult))
            v(dve.tensor_scalar(den[:], den[:], 1e-06, None, ALU.add))
            v(dve.reciprocal(coef[:], den[:]))
            v(dve.tensor_tensor(coef[:], coef[:], inv[:], ALU.mult))
            for h in range(H):
                v(dve.tensor_tensor(sq[:], heads[:, :, h, 0:D], coef[:, :, h:h + 1].to_broadcast([P, NT, D]), ALU.mult))
                v(dve.tensor_tensor(sq4[:], sq[:], sq[:], ALU.mult))
                v(dve.tensor_reduce(n2[:, :, h], sq4[:], X, ALU.add))
            atanh_ratio_vector(v, dve, n2[:], t[:], w1[:], w2[:], f[:], n2_ready, norm_ready, ratio_ready, log_ready, 1)
            v(dve.tensor_scalar(n2[:], n2[:], MAXNORM * MAXNORM, 1.0 / (MAXNORM * MAXNORM), ALU.max, ALU.mult))
            dve.sem_inc(n2_ready, 1)
            dve.wait_ge(shrink_ready, 1)
            v(dve.reciprocal(w2[:], w1[:]))
            v(dve.tensor_tensor(f[:], f[:], w2[:], ALU.mult))
            v(dve.scalar_tensor_tensor(coef[:], coef[:], 1.0 / H, f[:], ALU.mult, ALU.mult))
            bc = lambda a, h: a[:, :, h:h + 1].to_broadcast([P, NT, D])
            v(dve.tensor_tensor(h_new[:], heads[:, :, 0, 0:D], bc(coef, 0), ALU.mult))
            for h in range(1, H):
                v(dve.tensor_tensor(sq[:], heads[:, :, h, 0:D], bc(coef, h), ALU.mult))
                v(dve.tensor_tensor(h_new[:], h_new[:], sq[:], ALU.add))
            v(dve.tensor_tensor(sq[:], h_new[:], h_new[:], ALU.mult))
            v(dve.tensor_reduce(a2[:], sq[:], X, ALU.add))
            v(dve.tensor_scalar(a2[:], a2[:], 1e-20, None, ALU.max))
            dve.sem_inc(a2_ready, 1)
            dve.wait_ge(tanh_done, 1)
            v(dve.reciprocal(a2[:], nrm[:]))
            v(dve.scalar_tensor_tensor(a2[:], a2[:], 10.0, th[:], ALU.mult, ALU.mult))
            v(dve.tensor_tensor(h_new[:], h_new[:], a2[:].unsqueeze(2).to_broadcast([P, NT, D]), ALU.mult))
            v(dve.tensor_tensor(g.x[:], g.x[:], h_new[:], ALU.add))
            v(dve.tensor_copy(g.deg_in[:], g.sums[:, :, MSG]))
            layer_norm_vector(v, dve, g.x[:], sq[:], st, var_ready, root_ready, 1)


def items_matrix(nc, g):
    if True:
        lo_col, cell_col, tiles = g.lo_col, g.cell_col, g.tiles1
        with Scope(nc, "cmi") as q:
            tile_of, tile_int, row_int = walk(nc, g, q, "cmi", P, CI, CC, WIN, WINS, float(WIN))
            rows = [q.sb(n, [CI, CC, P], I32) for n in ("src", "dst")]
            lane_of, tile_src = q.sb("lane_of", [CI, CC, P], I32), q.sb("tile_src", [CI, CC, P], I32)
            gather_rows(nc, g, "cmi", (g.flat_src, g.flat_dst), rows, row_int, CI, CC, P, tile_int, g.tile1_dram)
            lof, hif, win, inside = (q.sb(n, [CI, CC, P]) for n in ("lof", "hif", "win", "inside"))
            turned = [q.ps(f"turned{k}", [P, 4, P]) for k in range(2)]
            own, ready, turn, copied, loaded, zeroed = (q.sem(n) for n in ("own", "ready", "turn", "copied", "loaded", "zeroed"))
            block = q.block()
            jobs = [(lof, lo_col), (hif, cell_col)]

            @block.sync
            def _(sp):
                sp.dma_start(tiles[:, 8:], g.tile1_dram[0:CITEMS].rearrange("(a n) -> a n", a=1)).then_inc(loaded, 16)
                sp.wait_ge(loaded, 16)

            @block.vector
            def _(dve):
                v = chain(dve, own)
                v(dve.memset(tiles[:, 0:8], 0))
                v(dve.tensor_scalar(lane_of[:], rows[0][:], P - 1, None, ALU.bitwise_and))
                v(dve.tensor_copy(lof[:], lane_of[:]))
                v(dve.tensor_scalar(tile_src[:], rows[0][:], 7, None, ALU.logical_shift_right))
                v(dve.tensor_copy(hif[:], tile_src[:]))
                v(dve.tensor_scalar(tile_of[:], tile_of[:], float(WIN), None, ALU.mult))
                v(dve.tensor_copy(win[:], rows[1][:]))
                v(dve.tensor_tensor(win[:], win[:], tile_of[:].unsqueeze(2).to_broadcast([CI, CC, P]), ALU.subtract))
                v(dve.scalar_tensor_tensor(hif[:], hif[:], float(WIN), win[:], ALU.mult, ALU.add))
                v(dve.tensor_scalar(inside[:], win[:], 0.0, None, ALU.is_ge))
                v(dve.scalar_tensor_tensor(inside[:], win[:], float(WIN), inside[:], ALU.is_lt, ALU.mult))
                v(dve.scalar_tensor_tensor(hif[:], hif[:], 1.0, inside[:], ALU.add, ALU.mult))
                v(dve.tensor_scalar(hif[:], hif[:], -1.0, None, ALU.add))
                dve.sem_inc(ready, 1)
                n = 0
                for _, col in jobs:
                    for c in range(0, CC, 4):
                        n += 1
                        dve.wait_ge(turn, n)
                        dve.tensor_copy(col[:, c * CI:(c + 4) * CI].rearrange("p (c i) -> p c i", c=4),
                                        turned[(n - 1) % 2][:, :, 0:CI]).then_inc(copied, 1)
                dve.wait_ge(copied, n)

            @block.tensor
            def _(pe):
                pe.wait_ge(ready, 1)
                n = 0
                for arr, _ in jobs:
                    for c in range(0, CC, 4):
                        if n >= 2:
                            pe.wait_ge(copied, n - 1)
                        for j in range(4):
                            m = pe.transpose(turned[n % 2][:, j, 0:CI], arr[:, c + j, :], g.ident[0:CI, 0:CI])
                        m.then_inc(turn, 1)
                        n += 1


def count_matrix(nc, g):
    with Scope(nc, "cmb") as s:
        S = 4
        CELLS = NT * WIN
        lane = s.sb("lane", [P, 2, S, P], BF16)
        cell = s.sb("cell", [P, 2, S, CELLS], BF16)
        cell_now, lane_now = s.sb("cell_now", [P, 2 * S]), s.sb("lane_now", [P, 2 * S])
        lanes_ready = s.sem("lanes_ready")
        got = s.sb("got", [P, 2, S, CELLS], F16)
        part = [s.ps(f"part{k}", [P, 2, 512]) for k in range(4)]
        own, cleared, lane_ready, cell_ready, part_ready, part_taken, got_added, copied = (
            s.sem(n) for n in ("own", "cleared", "lane_ready", "cell_ready", "part_ready", "part_taken", "got_added", "copied"))
        zeroed = s.sem("zeroed")
        block = s.block()
        ROUNDS = CITEMS // (2 * S)

        @block.gpsimd
        def _(pool):
            for i in range(NT // 2, NT):
                m = pool.memset(g.matrix[:, i, :].bitcast(F32), 0.0)
            m.then_inc(zeroed, 1)

        @block.tensor
        def _(pe):
            pe.sem_inc(part_ready, 2)
            with pe.Fori(0, ROUNDS) as r:
                for k in range(2):
                    wait(pe, cell_ready, r * 2 + k + 1)
                    wait(pe, part_taken, r * 2 + k + 1)
                    for j in range(S):
                        m = pe.matmul(part[2 * k + j // 2][:, j % 2, 0:CELLS], lane[:, k, j, :], cell[:, k, j, :],
                                      start=True, stop=True)
                    m.then_inc(part_ready, 1)

        @block.scalar
        def _(act):
            act.sem_inc(part_taken, 2)
            act.sem_inc(copied, 2)
            with act.Fori(0, ROUNDS) as r:
                for k in range(2):
                    wait(act, part_ready, r * 2 + k + 3)
                    wait(act, got_added, r * 2 + k + 1)
                    act.copy(got[:, k, 0:2, :], part[2 * k][:, :, 0:CELLS])
                    act.copy(got[:, k, 2:4, :], part[2 * k + 1][:, :, 0:CELLS]).then_inc(copied, 1)
                    wait(act, copied, r * 2 + k + 3)
                    act.sem_inc(part_taken, 1)

        @block.vector
        def _(dve):
            for i in range(NT // 2):
                m = dve.memset(g.matrix[:, i, :].bitcast(F32), 0.0)
            m.then_inc(zeroed, 1)
            dve.wait_ge(zeroed, 2)

            def one_hots(k, j):
                n = k * S + j
                dve.tensor_scalar(lane[:, k, j, :], g.count_b[:, 0:P], lane_now[:, n:n + 1], None, ALU.is_equal)
                return dve.tensor_scalar(cell[:, k, j, :], g.count_b[:, 0:CELLS], cell_now[:, n:n + 1], None, ALU.is_equal)

            def add(k, j, at):
                to = g.matrix[:, :, bass.ds(at, WIN)]
                dve.tensor_tensor(to, to, got[:, k, j, :].rearrange("p (a b) -> p a b", b=WIN), ALU.add).then_inc(own, 1)

            def windows(items):
                return nc.values_load_multi_w_load_instructions(
                    g.tiles1[0:1, items], engines=[mybir.EngineType.DVE], min_val=0, max_val=(WINS - 1) * WIN,
                    skip_runtime_bounds_check_because="a window's start is a count of rows' ends, at most WINS - 1, times WIN")[1]

            dve.memset(got[:].rearrange("p k a b -> p (k a b)"), 0.0).then_inc(zeroed, 1)
            dve.wait_ge(zeroed, 3)
            with dve.Fori(0, ROUNDS) as r:
                dve.tensor_copy(cell_now[:], g.cell_col[:, bass.ds(r * 2 * S, 2 * S)]).then_inc(own, 1)
                dve.tensor_copy(lane_now[:], g.lo_col[:, bass.ds(r * 2 * S, 2 * S)]).then_inc(own, 1)
                at = windows(bass.ds(r * 2 * S, 2 * S))
                dve.wait_ge(own, 2)
                for k in range(2):
                    wait(dve, copied, r * 2 + k + 1)
                    for j in range(S):
                        add(k, j, at[k * S + j])
                        m = one_hots(k, j)
                        if j < S - 1:
                            dve.wait_ge(own, 2 + k * (S + 1) + j + 1)
                    m.then_inc(own, 1)
                    dve.wait_ge(own, 2 + (k + 1) * (S + 1))
                    dve.sem_inc(cell_ready, 1)
                    dve.sem_inc(got_added, 1)
                dve.sem_clear(own)
            dve.wait_ge(copied, 2 * ROUNDS + 2)
            at = windows(slice(CITEMS, CITEMS + 2 * S))
            for n in range(2 * S):
                add(n // S, n % S, at[n])
                dve.wait_ge(own, n + 1)


def out_degrees(nc, g):
    with Scope(nc, "deg") as s:
        deg, m, r = s.sb("deg", [P, 2, NT]), s.sb("m", [P, 2, NT]), s.sb("r", [P, 2, NT])
        own, ready, root, summed = s.sem("own"), s.sem("ready"), s.sem("root"), s.sem("summed")
        junk = s.sb("junk", [P, NP], F16)
        block = s.block()
        BY_VECTOR = 13

        @block.scalar
        def _(act):
            for i in range(BY_VECTOR, NT):
                act.activation(junk[:], g.matrix[:, i, :], ACT.Copy, accum_out=deg[:, 0, i:i + 1]).then_inc(summed, 1)
                act.wait_ge(summed, i + 1 - BY_VECTOR)
            act.wait_ge(ready, 1)
            act.activation(r[:], m[:], ACT.Sqrt).then_inc(root, 1)

        @block.vector
        def _(dve):
            v = chain(dve, own)
            v(dve.tensor_reduce(deg[:, 0, 0:BY_VECTOR], g.matrix[:, 0:BY_VECTOR, :], X, ALU.add))
            dve.wait_ge(summed, NT - BY_VECTOR)
            v(dve.tensor_copy(deg[:, 1, :], g.deg_in[:]))
            v(dve.tensor_scalar(m[:], deg[:], 1.0, None, ALU.max))
            dve.sem_inc(ready, 1)
            v(dve.reciprocal(g.per_deg[:], m[:]))
            dve.wait_ge(root, 1)
            v(dve.reciprocal(m[:], r[:]))
            v(dve.scalar_tensor_tensor(g.root_deg[:], deg[:], 0.0, m[:], ALU.is_gt, ALU.mult))


def graph_layer(nc, g, name, pre, reverse, scale_in, scale_out, w_dram, b_dram, relu, out=None):
    with Scope(nc, name) as s:
        has_w = w_dram is not None
        w = s.sb("w", [D, D])
        bias = s.sb("bias", [P, D])
        xT = s.sb("xT", [D, 4, P])
        feat = s.sb("feat", [P, NT, D])
        parts = s.sb("parts", [P, NT, 3, D], BF16)
        agg = feat
        st = s.sb("st", [P, 2, NT])
        flip = s.sb("flip", [P, 2, 8, P], F16)
        px = s.ps("px", [P, 4, P])
        pw = s.ps("pw", [P, 4, D])
        pc = [s.ps(f"pc{k}", [P, 512]) for k in range(2)]
        pt = [s.ps(f"pt{k}", [P, 8, P], F16) for k in range(2)]
        loaded, own, ready, turn, turned, multiplied, parts_ready, summed, taken, flipped, var_ready, root_ready, stored = (
            s.sem(n) for n in ("loaded", "own", "ready", "turn", "turned", "multiplied", "parts_ready", "summed", "taken",
                               "flipped", "var_ready", "root_ready", "stored"))
        flip_turn = s.sem("flip_turn")
        block = s.block()
        bc = lambda a: a.unsqueeze(2).to_broadcast([P, NT, D])
        groups = list(range(0, NT, 4))
        jgroups = list(range(0, NT, 8))

        @block.sync
        def _(sp):
            if has_w:
                sp.dma_start(w[:], w_dram[:, :]).then_inc(loaded, 16)
                sp.dma_start(bias[:], b_dram.rearrange("(a n) -> a n", a=1).to_broadcast([P, D])).then_inc(loaded, 16)
                sp.wait_ge(loaded, 32)
            if out is not None:
                sp.wait_ge(stored, 1)
                sp.dma_start(out[0:FULL * P, :].rearrange("(t p) d -> p t d", p=P), g.x[:, 0:FULL, :]).then_inc(loaded, 16)
                sp.dma_start(out[FULL * P:N, :], g.x[0:REST, FULL, :]).then_inc(loaded, 16)
                sp.wait_ge(loaded, 32)

        @block.scalar
        def _(act):
            if reverse:
                n = 0
                for i in range(NT):
                    for q in jgroups:
                        k = min(8, NT - q)
                        act.wait_ge(flip_turn, n + 1)
                        act.copy(flip[:, n % 2, 0:k, :], pt[n % 2][:, 0:k, :]).then_inc(flipped, 1)
                        n += 1
            layer_norm_scalar(act, st, var_ready, root_ready, 1)

        def times_w_tensor(pe, src):
            pe.wait_ge(loaded, 32)
            pe.wait_ge(ready, 1)
            for n, q in enumerate(groups):
                k = min(4, NT - q)
                if n:
                    pe.wait_ge(multiplied, n)
                for i in range(k):
                    m = pe.transpose(px[0:D, i, :], src[:, q + i, :], g.ident[:])
                m.then_inc(turn, 1)
                pe.wait_ge(turned, n + 1)
                for i in range(k):
                    m = pe.matmul(pw[:, i, :], xT[:, i, :], w[:], start=True, stop=True)
                m.then_inc(turn, 1)

        def times_w_vector(dve, out):
            for n, q in enumerate(groups):
                k = min(4, NT - q)
                dve.wait_ge(turn, 2 * n + 1)
                dve.tensor_copy(xT[:, 0:k, :], px[0:D, 0:k, :]).then_inc(turned, 1)
                dve.wait_ge(turn, 2 * n + 2)
                dve.tensor_copy(out[:, q:q + k, :], pw[:, 0:k, :]).then_inc(multiplied, 1)
            dve.wait_ge(multiplied, len(groups))

        @block.tensor
        def _(pe):
            if pre:
                times_w_tensor(pe, g.x)
            pe.wait_ge(parts_ready, 1)
            n = 0
            if not reverse:
                for j in range(NT):
                    if j >= 2:
                        pe.wait_ge(taken, j - 1)
                    for i in range(NT):
                        m = pe.matmul(pc[j % 2][:, 0:3 * D], g.matrix[:, i, j * P:(j + 1) * P],
                                      parts[:, i].rearrange("p a d -> p (a d)"), start=(i == 0), stop=(i == NT - 1))
                    m.then_inc(summed, 1)
            else:
                steps = [(i, q) for i in range(NT) for q in jgroups]

                def turn_group(n):
                    i, q = steps[n]
                    if n >= 2:
                        pe.wait_ge(flipped, n - 1)
                    for j in range(q, min(q + 8, NT)):
                        m = pe.transpose(pt[n % 2][:, j - q, :], g.matrix[:, i, j * P:(j + 1) * P], g.ident_h[:])
                    m.then_inc(flip_turn, 1)

                turn_group(0)
                for n, (i, q) in enumerate(steps):
                    if n + 1 < len(steps):
                        turn_group(n + 1)
                    pe.wait_ge(flipped, n + 1)
                    if q == 0 and i >= 2:
                        pe.wait_ge(taken, i - 1)
                    for j in range(q, min(q + 8, NT)):
                        m = pe.matmul(pc[i % 2][:, 0:3 * D], flip[:, n % 2, j - q, :],
                                      parts[:, j].rearrange("p a d -> p (a d)"), start=(j == 0), stop=(j == NT - 1))
                    if q == jgroups[-1]:
                        m.then_inc(summed, 1)
            if has_w and not pre:
                times_w_tensor(pe, agg)

        @block.vector
        def _(dve):
            v = chain(dve, own)
            if pre:
                dve.sem_inc(ready, 1)
                times_w_vector(dve, feat)
                v(dve.tensor_tensor(feat[:], feat[:], bc(scale_in), ALU.mult))
            else:
                v(dve.tensor_tensor(feat[:], g.x[:], bc(scale_in), ALU.mult))
            for b in range(3):
                v(dve.tensor_copy(parts[:, :, b, :], feat[:]))
                if b < 2:
                    v(dve.tensor_tensor(feat[:], feat[:], parts[:, :, b, :], ALU.subtract))
            dve.sem_inc(parts_ready, 1)
            for j in range(NT):
                dve.wait_ge(summed, j + 1)
                dve.tensor_reduce(agg[:, j, :], pc[j % 2][:, 0:3 * D].rearrange("p (b d) -> p d b", b=3), X, ALU.add).then_inc(taken, 1)
            dve.wait_ge(taken, NT)
            v(dve.tensor_tensor(agg[:], agg[:], bc(scale_out), ALU.mult))
            if has_w and not pre:
                dve.sem_inc(ready, 1)
                times_w_vector(dve, agg)
            if has_w:
                v(dve.tensor_tensor(agg[:], agg[:], bias[:].unsqueeze(1).to_broadcast([P, NT, D]), ALU.add))
            if relu:
                v(dve.tensor_scalar(agg[:], agg[:], 0.0, None, ALU.max))
            v(dve.tensor_tensor(g.x[:], g.x[:], agg[:], ALU.add))
            layer_norm_vector(v, dve, g.x[:], agg[:], st, var_ready, root_ready, 1)
            if out is not None:
                dve.sem_inc(stored, 1)


class Shared:
    pass


def build(nc, x, src, dst, edge_type_8, rel_weight, attn_vec, rel_emb, W1, b1, W2, b2, out):
    g = Shared()
    g.x_in = x
    dram = lambda name, shape, dt=F32: nc.dram_tensor(name, shape, dt).ap()
    g.flat_src, g.flat_dst, g.flat_et = (dram(n, [EP], I32) for n in ("flat_src", "flat_dst", "flat_et"))
    g.key_dram = dram("keys", [ITEMS * PAIR + 2])
    g.node_dram = dram("node_table", [NP, NODE])
    g.msg_dram = dram("message_table", [NP * R, MSG])
    g.tile0_dram, g.tile1_dram = dram("tiles0", [ITEMS], I32), dram("tiles1", [CITEMS], I32)
    with Scope(nc, "g") as s:
        g.ident, g.ident_b, g.ident_h = s.sb("ident", [P, P]), s.sb("ident_b", [P, P], BF16), s.sb("ident_h", [P, P], F16)
        g.count, g.ones, g.ones_b = s.sb("count", [P, P]), s.sb("ones", [P, 1]), s.sb("ones_b", [P, P], BF16)
        g.count_b = s.sb("count_b", [P, 2 * P], BF16)
        g.x = s.sb("x", [P, NT, D])
        g.deg_in = s.sb("deg_in", [P, NT])
        g.per_deg, g.root_deg = s.sb("per_deg", [P, 2, NT]), s.sb("root_deg", [P, 2, NT])
        constants(nc, g)
        stage_edges(nc, g, src, dst, edge_type_8)
        with Scope(nc, "l0") as l0:
            g.src_col, g.msg_col = (l0.sb(n, [P, COLS], I32) for n in ("src_col", "msg_col"))
            g.lane_col, g.et_col = l0.sb("lane_col", [P, COLS + 4]), l0.sb("et_col", [P, COLS])
            items_layer0(nc, g)
            g.ex = l0.sb("ex", [P, COLS, H])
            with Scope(nc, "l0n") as n0:
                g.node = n0.sb("node", [P, NT, NODE])
                with Scope(nc, "l0t") as t0:
                    xT, factor = t0.sb("xT", [D, NT, P]), t0.sb("factor", [P, NT])
                    node_table(nc, g, attn_vec, xT, factor)
                    message_table(nc, g, rel_weight, xT, factor)
                with Scope(nc, "l0a") as a0:
                    a = Shared()
                    a.s2, a.d2, a.gram = (a0.sb(n, [P, COLS]) for n in ("s2", "d2", "gram"))
                    a.ps, a.pd = a0.sb("ps", [P, COLS, H]), a0.sb("pd", [P, COLS, H])
                    edge_products(nc, g, a)
                    edge_weights(nc, g, a)
            g.sums = l0.sb("sums", [P, NT, OUTC])
            edge_sums(nc, g)
            finish_layer0(nc, g)
        with Scope(nc, "m") as m:
            g.lo_col, g.cell_col = (m.sb(n, [P, CITEMS]) for n in ("lo_col", "cell_col"))
            g.tiles1 = m.sb("tiles1", [1, CITEMS + 8], I32)
            items_matrix(nc, g)
            g.matrix = m.sb("matrix", [P, NT, NP], F16)
            count_matrix(nc, g)
            out_degrees(nc, g)
            deg_out, deg_in = 0, 1
            graph_layer(nc, g, "conv1", True, False, g.root_deg[:, deg_out], g.root_deg[:, deg_in], W1, b1, False)
            graph_layer(nc, g, "conv2", False, True, g.root_deg[:, deg_out], g.root_deg[:, deg_out], W2, b2, True)
            graph_layer(nc, g, "mean3", False, False, g.per_deg[:, deg_out], g.per_deg[:, deg_in], None, None, False, out)


_INS = ["x", "src", "dst", "edge_type_8", "L0_gnn_rel_weight", "L0_gnn_attn_vec", "L0_gnn_rel_emb", "L1_gnn_W",
        "L1_gnn_b", "L2_gnn_weight", "L2_gnn_bias"]


def kernel(**inputs):
    import numpy as _np
    import concourse.bacc as _bacc
    from concourse import mybir as _mybir
    from concourse.bass_utils import run_bass_kernel_spmd as _run

    nc = _bacc.Bacc("TRN2", target_bir_lowering=False, num_devices=1)
    arrays, args = {}, []
    for name in _INS:
        a = _np.ascontiguousarray(inputs[name])
        arrays[f"in_{name}"] = a
        args.append(nc.dram_tensor(f"in_{name}", a.shape, _mybir.dt.from_np(a.dtype), kind="ExternalInput").ap())
    args.append(nc.dram_tensor("out_0", (N, D), F32, kind="ExternalOutput").ap())
    build(nc, *args)
    r = _run(nc, [arrays], core_ids=[0])
    return r.results[0]["out_0"]
```

```python
from contextlib import ExitStack

import concourse.bass as bass
from concourse import mybir

P = 128
F32 = mybir.dt.float32
F16 = mybir.dt.float16
BF16 = mybir.dt.bfloat16
I32 = mybir.dt.int32
ALU = mybir.AluOpType
ACT = mybir.ActivationFunctionType
X = mybir.AxisListType.X

N, D = 3125, 64
E = 103125
R, H = 8, 4
NT = -(-N // P)
FULL = N // P
REST = N - FULL * P
NP = NT * P

PAIR = 2 * P
PAIR_ROWS = 408
EP = PAIR_ROWS * PAIR
WIN = 8
WINS = -(-N // WIN)

PI, PC = 108, 4
ITEMS = PI * PC
COLS = 2 * ITEMS
CELLS = NT * WIN
CI, CC = 108, 12
CITEMS = CI * CC
STEP = 3
ROUND = 4 * STEP
SPAN = ROUND + 1
S = 4
STEPS = COLS // S
BODY = 8
assert ITEMS >= -(-E // PAIR) + NT - 1 and ITEMS - (NT - 1) < PAIR_ROWS + 1
assert CITEMS >= -(-E // P) + WINS - 1 and EP - E >= P
assert STEPS % BODY == 0 and CITEMS == 2 * STEPS * STEP

NODE = D + 1 + R * H
HEAD = D + 2
MSG = H * HEAD
OUTC = MSG + 1
PAD_DST = 4000.0
C = 0.01
T_MAX = 1.0 - 1e-05
MAXNORM = (1.0 - 1e-05) / 0.1


def wait(eng, sem, value):
    eng.wait_ge(sem, value)
    eng.nop(nofuse=True)


def chain(eng, sem, start=0):
    count = [start]

    def step(ins):
        count[0] += 1
        ins.then_inc(sem, 1)
        eng.wait_ge(sem, count[0])
        return ins
    return step


class Scope:
    used = []

    def __init__(self, nc, name):
        self.nc, self.name, self.ctx = nc, name, ExitStack()

    def __enter__(self):
        return self

    def __exit__(self, *a):
        return self.ctx.__exit__(*a)

    def sb(self, name, shape, dt=F32):
        return self.ctx.enter_context(self.nc.sbuf_tensor(f"{self.name}_{name}", shape, dt))

    def ps(self, name, shape, dt=F32):
        return self.ctx.enter_context(self.nc.psum_tensor(f"{self.name}_{name}", shape, dt))

    def sem(self, name):
        handle = self.nc.alloc_semaphore(name=f"{self.name}_{name}")
        self.ctx.callback(Scope.used.append, handle)
        return handle

    def block(self):
        return self.ctx.enter_context(self.nc.Block())


def clear_used_semaphores(nc):
    nc.clear_and_free_semaphores(list(Scope.used))
    Scope.used.clear()
    nc.all_engine_barrier()


def atanh_ratio_vector(v, eng, n2, t, w1, w2, out, n2_ready, norm_ready, ratio_ready, log_ready, k):
    v(eng.tensor_scalar(n2, n2, 1e-20, None, ALU.max))
    eng.sem_inc(n2_ready, 1)
    eng.wait_ge(norm_ready, k)
    v(eng.tensor_scalar(t, t, 0.1, 1e-10, ALU.mult, ALU.max))
    v(eng.tensor_scalar(t, t, T_MAX, None, ALU.min))
    v(eng.tensor_scalar(w1, t, -1.0, 1.0, ALU.mult, ALU.add))
    v(eng.reciprocal(w2, w1))
    v(eng.scalar_tensor_tensor(w1, t, 1.0, w2, ALU.add, ALU.mult))
    eng.sem_inc(ratio_ready, 1)
    v(eng.tensor_tensor(w2, t, t, ALU.mult))
    v(eng.tensor_scalar(out, w2, 1.0 / 9, 1.0 / 7, ALU.mult, ALU.add))
    v(eng.tensor_tensor(out, out, w2, ALU.mult))
    v(eng.scalar_tensor_tensor(out, out, 1.0 / 5, w2, ALU.add, ALU.mult))
    v(eng.scalar_tensor_tensor(out, out, 1.0 / 3, w2, ALU.add, ALU.mult))
    v(eng.tensor_scalar(out, out, 1.0, None, ALU.add))
    v(eng.reciprocal(w2, t))
    eng.wait_ge(log_ready, k)
    v(eng.scalar_tensor_tensor(w1, w1, 0.5, w2, ALU.mult, ALU.mult))
    v(eng.tensor_tensor(out, out, w1, ALU.subtract))
    v(eng.scalar_tensor_tensor(out, t, 0.1, out, ALU.is_lt, ALU.mult))
    v(eng.tensor_tensor(out, out, w1, ALU.add))


def atanh_ratio_scalar(eng, n2, t, w1, n2_ready, norm_ready, ratio_ready, log_ready, k):
    eng.wait_ge(n2_ready, k)
    eng.activation(t, n2, ACT.Sqrt).then_inc(norm_ready, 1)
    eng.wait_ge(ratio_ready, k)
    eng.activation(w1, w1, ACT.Ln).then_inc(log_ready, 1)


def layer_norm_vector(v, eng, x, sq, st, var_ready, root_ready, k):
    mean, var = st[:, 0, :], st[:, 1, :]
    bc = lambda a: a.unsqueeze(2).to_broadcast([P, NT, D])
    v(eng.tensor_reduce(mean, x, X, ALU.add))
    v(eng.tensor_scalar(mean, mean, 1.0 / D, None, ALU.mult))
    v(eng.tensor_tensor(x, x, bc(mean), ALU.subtract))
    v(eng.tensor_tensor(sq, x, x, ALU.mult))
    v(eng.tensor_reduce(var, sq, X, ALU.add))
    v(eng.tensor_scalar(var, var, 1.0 / D, 1e-05, ALU.mult, ALU.add))
    eng.sem_inc(var_ready, 1)
    eng.wait_ge(root_ready, k)
    v(eng.reciprocal(mean, var))
    v(eng.tensor_tensor(x, x, bc(mean), ALU.mult))


def layer_norm_scalar(eng, st, var_ready, root_ready, k):
    eng.wait_ge(var_ready, k)
    eng.activation(st[:, 1, :], st[:, 1, :], ACT.Sqrt).then_inc(root_ready, 1)


def constants(nc, g):
    with Scope(nc, "const") as s:
        filled, made = s.sem("filled"), s.sem("made")
        block = s.block()

        @block.gpsimd
        def _(pool):
            pool.memset(g.ident[:], 0.0).then_inc(filled, 1)
            pool.wait_ge(filled, 1)
            pool.affine_select(out=g.ident[:], in_=g.ident[:], compare_op=ALU.not_equal, fill=1.0, base=0,
                               pattern=[[-1, P]], channel_multiplier=1).then_inc(made, 1)
            pool.iota(g.count[:], [[1, P]], base=0, channel_multiplier=0,
                      allow_small_or_imprecise_dtypes=True).then_inc(made, 1)
            pool.iota(g.count_b[:], [[1, 2 * P]], base=0, channel_multiplier=0,
                      allow_small_or_imprecise_dtypes=True).then_inc(made, 1)

        @block.vector
        def _(dve):
            dve.wait_ge(made, 3)
            dve.tensor_copy(g.ident_b[:], g.ident[:]).then_inc(filled, 1)
            dve.tensor_copy(g.ident_h[:], g.ident[:]).then_inc(filled, 1)
            dve.memset(g.one[:], 1.0).then_inc(filled, 1)
            dve.wait_ge(filled, 4)


def stage_edges(nc, g, src, dst, et):
    with Scope(nc, "stage") as s:
        pad_dst, pad_zero = s.sb("pad_dst", [1, EP - E], I32), s.sb("pad_zero", [1, EP - E], I32)
        filled, stored, x_cleared = s.sem("filled"), s.sem("stored"), s.sem("x_cleared")
        block = s.block()

        @block.vector
        def _(dve):
            dve.memset(pad_dst[:], int(PAD_DST)).then_inc(filled, 1)
            dve.memset(pad_zero[:], 0).then_inc(filled, 1)
            dve.memset(g.x[:], 0.0).then_inc(x_cleared, 1)

        @block.sync
        def _(sp):
            row = lambda a: a.rearrange("(a n) -> a n", a=1)
            for flat, given in ((g.flat_src, src), (g.flat_dst, dst), (g.flat_et, et)):
                sp.dma_start(flat[0:E].rearrange("(a n) -> a n", a=125), given.rearrange("(a n) -> a n", a=125)).then_inc(stored, 16)
            sp.wait_ge(filled, 2)
            for flat, pad in ((g.flat_src, pad_zero), (g.flat_dst, pad_dst), (g.flat_et, pad_zero)):
                sp.dma_start(row(flat[E:EP]), pad[:]).then_inc(stored, 16)
            sp.wait_ge(x_cleared, 1)
            sp.dma_start(g.x[:, 0:FULL, :], g.x_in[0:FULL * P, :].rearrange("(t p) d -> p t d", p=P)).then_inc(stored, 16)
            sp.dma_start(g.x[0:REST, FULL, :], g.x_in[FULL * P:N, :]).then_inc(stored, 16)
            sp.wait_ge(stored, 8 * 16)


def walk(nc, g, s, name, row_len, lanes, cols, tile, tiles):
    lr, lc = 102, EP // row_len // 102
    last = s.sb(f"{name}_last", [lr, lc], I32)
    lastf = s.sb(f"{name}_lastf", [lr, lc])
    edge = s.sb(f"{name}_edge", [P, tiles - 1])
    below = s.sb(f"{name}_below", [lr, lc, tiles - 1], BF16)
    start = s.sb(f"{name}_start", [P, tiles - 1])
    number = s.sb(f"{name}_number", [lanes, cols])
    past = s.sb(f"{name}_past", [lanes, cols, tiles - 1], BF16)
    tile_of, row_of = s.sb(f"{name}_tile_of", [lanes, cols]), s.sb(f"{name}_row_of", [lanes, cols])
    row_int = s.sb(f"{name}_row_int", [lanes, cols], I32)
    tile_int = s.sb(f"{name}_tile_int", [lanes, cols], I32)
    starts = s.ps(f"{name}_starts", [P, 512])
    with Scope(nc, f"{name}_walk") as w:
        loaded, counted, compared, summed, own = (w.sem(n) for n in ("loaded", "counted", "compared", "summed", "own"))
        block = w.block()

        @block.sync
        def _(sp):
            ends = g.flat_dst.rearrange("(a b n) -> a b n", a=lr, n=row_len)
            sp.dma_start(last[:], ends[:, :, row_len - 1], allow_slow_non_contiguous=True).then_inc(loaded, 16)

        @block.gpsimd
        def _(pool):
            pool.iota(edge[:], [[tile, tiles - 1]], base=tile, channel_multiplier=0,
                      allow_small_or_imprecise_dtypes=True).then_inc(counted, 1)
            pool.iota(number[:], [[lanes, cols]], base=0, channel_multiplier=1,
                      allow_small_or_imprecise_dtypes=True).then_inc(counted, 1)

        @block.tensor
        def _(pe):
            pe.wait_ge(compared, 1)
            for c in range(lc):
                m = pe.matmul(starts[:, 0:tiles - 1], g.ones_b[0:lr, :], below[:, c, :], start=(c == 0), stop=(c == lc - 1))
            m.then_inc(summed, 1)

        @block.vector
        def _(dve):
            v = chain(dve, own)
            v(dve.memset(g.ones_b[:], 1.0))
            dve.wait_ge(loaded, 16)
            dve.wait_ge(counted, 2)
            v(dve.tensor_copy(lastf[:], last[:]))
            v(dve.tensor_tensor(below[:], lastf[:].unsqueeze(2).to_broadcast([lr, lc, tiles - 1]),
                                edge[0:lr, :].unsqueeze(1).to_broadcast([lr, lc, tiles - 1]), ALU.is_lt))
            dve.sem_inc(compared, 1)
            v(dve.tensor_scalar(start[:], edge[:], 1.0 / tile, None, ALU.mult))
            dve.wait_ge(summed, 1)
            v(dve.tensor_tensor(start[:], start[:], starts[:, 0:tiles - 1], ALU.add))
            v(dve.tensor_tensor(past[:], number[:].unsqueeze(2).to_broadcast([lanes, cols, tiles - 1]),
                                start[0:lanes, :].unsqueeze(1).to_broadcast([lanes, cols, tiles - 1]), ALU.is_ge))
            v(dve.tensor_reduce(tile_of[:], past[:], X, ALU.add))
            v(dve.tensor_tensor(row_of[:], number[:], tile_of[:], ALU.subtract))
            v(dve.tensor_scalar(row_of[:], row_of[:], float(EP // row_len - 1), None, ALU.min))
            v(dve.tensor_copy(row_int[:], row_of[:]))
            v(dve.tensor_copy(tile_int[:], tile_of[:]))
    return tile_of, tile_int, row_int


def gather_rows(pool, jobs, landed):
    count = 0
    for flats, outs, row_int, cols, row_len in jobs:
        for flat, out in zip(flats, outs):
            for c in range(cols):
                pool.indirect_dma_start(
                    out=out[:, c, :], out_offset=None, in_=flat.rearrange("(r n) -> r n", n=row_len),
                    in_offset=bass.IndirectOffsetOnAxis(ap=row_int[:, c:c + 1], axis=0)).then_inc(landed, 16)
                count += 16
    pool.wait_ge(landed, count)


def items_layer0(nc, g, tile_of, rows):
    with Scope(nc, "it0") as s:
        srcf, dstf, etf, lane, key, w = (s.sb(n, [PI, PC, PAIR]) for n in ("srcf", "dstf", "etf", "lane", "key", "w"))
        guard = s.sb("guard", [1, 2])
        turned = [s.ps(f"turned{k}", [P, PC, P]) for k in range(2)]
        with Scope(nc, "it0b") as q:
            own, ready, turn, copied, stored = (q.sem(n) for n in ("own", "ready", "turn", "copied", "stored"))
            block = q.block()
            jobs = [(srcf, g.src_col), (etf, g.msg_col), (lane, g.lane_col), (w, g.et_col)]

            @block.vector
            def _(dve):
                v = chain(dve, own)
                v(dve.memset(guard[:], -1.0))
                v(dve.memset(g.lane_col[:, COLS:], -1.0))
                for f, i in zip((srcf, dstf, w), rows):
                    v(dve.tensor_copy(f[:], i[:]))
                v(dve.scalar_tensor_tensor(etf[:], srcf[:], float(R), w[:], ALU.mult, ALU.add))
                for c in range(PC):
                    v(dve.tensor_scalar(key[:, c, 0:1], tile_of[:, c:c + 1], float(P), None, ALU.mult))
                    v(dve.tensor_scalar(lane[:, c, :], dstf[:, c, :], key[:, c, 0:1], None, ALU.subtract))
                v(dve.tensor_scalar(key[:], lane[:], 0.0, None, ALU.is_ge))
                v(dve.scalar_tensor_tensor(key[:], lane[:], float(P), key[:], ALU.is_lt, ALU.mult))
                v(dve.scalar_tensor_tensor(key[:], dstf[:], 1.0, key[:], ALU.add, ALU.mult))
                dve.sem_inc(ready, 1)
                n = 0
                for _, col in jobs:
                    for k in range(2):
                        n += 1
                        dve.wait_ge(turn, n)
                        dve.tensor_copy(col[:, 0:COLS].rearrange("p (c i k) -> p c i k", c=PC, k=2)[:, :, :, k],
                                        turned[k][:, :, 0:PI]).then_inc(copied, 1)
                dve.wait_ge(copied, n)

            @block.tensor
            def _(pe):
                pe.wait_ge(ready, 1)
                n = 0
                for arr, _ in jobs:
                    for k in range(2):
                        if n >= 2:
                            pe.wait_ge(copied, n - 1)
                        for c in range(PC):
                            m = pe.transpose(turned[k][:, c, 0:PI], arr[:, c, k * P:(k + 1) * P], g.ident[0:PI, 0:PI])
                        m.then_inc(turn, 1)
                        n += 1

            @block.sync
            def _(sp):
                sp.wait_ge(ready, 1)
                sp.dma_start(g.key_dram[1:1 + ITEMS * PAIR].rearrange("(c p n) -> p c n", c=PC, n=PAIR), key[:]).then_inc(stored, 16)
                ends = g.key_dram[0:2 + ITEMS * PAIR].rearrange("(a n) -> a n", a=1)
                sp.dma_start(ends[:, 0:1], guard[:, 0:1]).then_inc(stored, 16)
                sp.dma_start(ends[:, 1 + ITEMS * PAIR:2 + ITEMS * PAIR], guard[:, 1:2]).then_inc(stored, 16)
                sp.wait_ge(stored, 48)


def node_table(nc, g, attn_vec, xT, factor, row_jobs, tile_jobs):
    with Scope(nc, "node") as s:
        av, avT = s.sb("av", [R * H, D]), s.sb("avT", [D, R * H])
        sq = s.sb("sq", [P, NT, D])
        n2, t, w1, w2 = (s.sb(n, [P, NT]) for n in ("n2", "t", "w1", "w2"))
        px = [s.ps(f"px{k}", [P, 4, P]) for k in range(2)]
        pv, pd = s.ps("pv", [P, 512]), s.ps("pd", [P, 2, 512])
        loaded, landed, tiles_stored, own, turn, turned, dots, table, stored, n2_ready, norm_ready, ratio_ready, log_ready = (
            s.sem(n) for n in ("loaded", "landed", "tiles_stored", "own", "turn", "turned", "dots", "table", "stored",
                               "n2_ready", "norm_ready",
                               "ratio_ready", "log_ready"))
        block = s.block()
        groups = range(0, NT, 4)
        half = 512 // (R * H)

        @block.gpsimd
        def _(pool):
            gather_rows(pool, row_jobs, landed)

        @block.sync
        def _(sp):
            sp.dma_start(av[:], attn_vec.rearrange("r h d -> (r h) d")).then_inc(loaded, 16)
            for tile_int, tile_dram, lanes in tile_jobs:
                sp.dma_start(tile_dram.rearrange("(c p) -> p c", p=lanes), tile_int[:],
                             allow_slow_non_contiguous=True).then_inc(tiles_stored, 16)
            sp.wait_ge(tiles_stored, 16 * len(tile_jobs))
            sp.wait_ge(table, 1)
            sp.dma_start(g.node_dram.rearrange("(t p) d -> p t d", p=P), g.node[:]).then_inc(stored, 16)
            sp.wait_ge(stored, 16)

        @block.tensor
        def _(pe):
            pe.wait_ge(loaded, 16)
            pe.transpose(pv[0:D, 0:R * H], av[:], g.ident[0:R * H, 0:R * H]).then_inc(turn, 1)
            for n, q in enumerate(groups):
                if n >= 2:
                    pe.wait_ge(turned, n)
                for i in range(q, min(q + 4, NT)):
                    m = pe.transpose(px[n % 2][0:D, i - q, :], g.x[:, i, :], g.ident[:])
                m.then_inc(turn, 1)
            pe.wait_ge(turned, 1 + len(groups))
            for i in range(NT):
                a = i % half * R * H
                m = pe.matmul(pd[:, i // half, a:a + R * H], xT[:, i, :], avT[:], start=True, stop=True)
            m.then_inc(dots, 1)

        @block.scalar
        def _(act):
            atanh_ratio_scalar(act, n2[:], t[:], w1[:], n2_ready, norm_ready, ratio_ready, log_ready, 1)

        @block.vector
        def _(dve):
            v = chain(dve, own)
            dve.wait_ge(turn, 1)
            dve.tensor_copy(avT[:], pv[0:D, 0:R * H]).then_inc(turned, 1)
            for n, q in enumerate(groups):
                dve.wait_ge(turn, n + 2)
                k = min(4, NT - q)
                dve.tensor_copy(xT[:, q:q + k, :], px[n % 2][0:D, 0:k, :]).then_inc(turned, 1)
            v(dve.tensor_copy(g.node[:, :, 0:D], g.x[:]))
            v(dve.tensor_tensor(sq[:], g.x[:], g.x[:], ALU.mult))
            v(dve.tensor_reduce(n2[:], sq[:], X, ALU.add))
            v(dve.tensor_copy(g.node[:, :, D:D + 1], n2[:].unsqueeze(2)))
            dve.wait_ge(dots, 1)
            for b in range(2):
                k = min(half, NT - b * half)
                v(dve.tensor_copy(g.node[:, b * half:b * half + k, D + 1:NODE],
                                  pd[:, b, 0:k * R * H].rearrange("p (t c) -> p t c", t=k)))
            dve.sem_inc(table, 1)
            atanh_ratio_vector(v, dve, n2[:], t[:], w1[:], w2[:], factor[:], n2_ready, norm_ready, ratio_ready, log_ready, 1)


def message_table(nc, g, rel_weight, xT, factor):
    with Scope(nc, "msg") as s:
        w = s.sb("w", [D, R, H, D])
        m2, th = (s.sb(n, [P, 2, R * H]) for n in ("m2", "th"))
        u_nrm, inverse = s.sb("u_nrm", [P, 2, 2, R * H]), s.sb("inverse", [P, 2, 2, R * H])
        u, nrm, lam, coef = u_nrm[:, :, 0], u_nrm[:, :, 1], inverse[:, :, 0], inverse[:, :, 1]
        sq, m = s.sb("sq", [P, 2, R * H, D]), s.sb("m", [P, 2, R * H, D])
        row = s.sb("row", [P, 2, R * H, HEAD])
        pm = [s.ps(f"pm{k}", [P, R * H, D]) for k in range(2)]
        loaded, own, pool_own, u_ready, inverted, coef_ready, product, squared, moved, m2_ready, root, tanh_done, row_ready = (
            s.sem(n) for n in ("loaded", "own", "pool_own", "u_ready", "inverted", "coef_ready", "product", "squared",
                               "moved", "m2_ready", "root", "tanh_done", "row_ready"))
        row_stored = [s.sem(f"row_stored{b}") for b in range(2)]
        block = s.block()

        @block.sync
        def _(sp):
            sp.dma_start(w[:], rel_weight.rearrange("r h i o -> i r h o")).then_inc(loaded, 16)
            for i in range(NT):
                b = i % 2
                sp.wait_ge(row_ready, i + 1)
                sp.dma_start(g.msg_dram[i * P * R:(i + 1) * P * R, :].rearrange("(p r) c -> p (r c)", r=R),
                             row[:, b].rearrange("p a c -> p (a c)")).then_inc(row_stored[b], 16)
            sp.wait_ge(row_stored[0], 16 * ((NT + 1) // 2))
            sp.wait_ge(row_stored[1], 16 * (NT // 2))

        @block.gpsimd
        def _(pool):
            p = chain(pool, pool_own)
            for i in range(NT):
                b = i % 2
                f = factor[:, i:i + 1]
                pool.wait_ge(tanh_done, i + 1)
                if i >= 2:
                    pool.wait_ge(row_stored[b], 16 * (i // 2))
                p(pool.tensor_tensor(u[:, b], th[:, b], th[:, b], ALU.mult))
                p(pool.tensor_scalar(u[:, b], u[:, b], -1.0, 1.0, ALU.mult, ALU.add))
                p(pool.tensor_scalar(u[:, b], u[:, b], 1e-06, 0.5, ALU.add, ALU.mult))
                pool.sem_inc(u_ready, 1)
                pool.wait_ge(inverted, i + 1)
                p(pool.tensor_tensor(coef[:, b], coef[:, b], th[:, b], ALU.mult))
                p(pool.tensor_scalar(coef[:, b], coef[:, b], f, 10.0, ALU.mult, ALU.mult))
                p(pool.tensor_tensor(coef[:, b], coef[:, b], lam[:, b], ALU.mult))
                p(pool.tensor_copy(row[:, b, :, D:D + 1], lam[:, b].unsqueeze(2)))
                pool.sem_inc(coef_ready, 1)

        @block.tensor
        def _(pe):
            pe.wait_ge(loaded, 16)
            for i in range(NT):
                if i >= 2:
                    pe.wait_ge(moved, i - 1)
                for q in range(R // 2):
                    m = pe.matmul(pm[i % 2][:, q * 2 * H:(q + 1) * 2 * H, :].rearrange("p a d -> p (a d)"), xT[:, i, :],
                                  w[:, 2 * q:2 * q + 2].rearrange("i r h o -> i (r h o)"), start=True, stop=True)
                m.then_inc(product, 1)

        @block.scalar
        def _(act):
            for i in range(NT):
                b = i % 2
                act.wait_ge(product, i + 1)
                if i >= 2:
                    act.wait_ge(m2_ready, i - 1)
                act.activation(sq[:, b], pm[b][:], ACT.Square).then_inc(squared, 1)
                if i >= 2:
                    act.wait_ge(row_ready, i - 1)
                act.copy(m[:, b], pm[b][:]).then_inc(moved, 1)
                act.wait_ge(m2_ready, i + 1)
                act.activation(nrm[:, b], m2[:, b], ACT.Sqrt).then_inc(root, 1)
                act.wait_ge(root, i + 1)
                act.activation(th[:, b], nrm[:, b], ACT.Tanh, scale=0.1).then_inc(tanh_done, 1)

        @block.vector
        def _(dve):
            v = chain(dve, own)
            v(dve.memset(row[:, :, :, D + 1:HEAD], 1.0))

            def norms(i):
                b = i % 2
                f = factor[:, i:i + 1]
                dve.wait_ge(squared, i + 1)
                v(dve.tensor_reduce(m2[:, b], sq[:, b], X, ALU.add))
                v(dve.tensor_scalar(m2[:, b], m2[:, b], f, f, ALU.mult, ALU.mult))
                v(dve.tensor_scalar(m2[:, b], m2[:, b], 1e-20, None, ALU.max))
                dve.sem_inc(m2_ready, 1)

            norms(0)
            for i in range(NT):
                b = i % 2
                dve.wait_ge(u_ready, i + 1)
                v(dve.reciprocal(inverse[:, b], u_nrm[:, b]))
                dve.sem_inc(inverted, 1)
                if i + 1 < NT:
                    norms(i + 1)
                dve.wait_ge(coef_ready, i + 1)
                v(dve.tensor_tensor(row[:, b, :, 0:D], m[:, b], coef[:, b].unsqueeze(2).to_broadcast([P, R * H, D]), ALU.mult))
                dve.sem_inc(row_ready, 1)


def counts_scope(s, first_round):
    c = Shared()
    c.first_round = first_round
    c.lane, c.cell = s.sb("lane", [P, 2, STEP, P], BF16), s.sb("cell", [P, 2, STEP, CELLS], BF16)
    c.off = s.sb("off", [P, STEP, P], BF16)
    c.cell_now, c.lane_now = s.sb("cell_now", [P, 2 * ROUND]), s.sb("lane_now", [P, 2 * ROUND])
    c.part = [s.ps(f"counts{k}", [P, 2, 512]) for k in range(2)]
    c.own, c.lane_own, c.lane_ready, c.cell_ready, c.part_ready, c.copied, c.flush_ready, c.flushed = (
        s.sem(n) for n in ("counts_own", "lane_own", "lane_ready", "cell_ready", "counts_ready", "counts_copied",
                           "flush_ready", "flushed"))
    return c


def counts_tensor(pe, c, step, k):
    wait(pe, c.cell_ready, step + 1)
    wait(pe, c.lane_ready, step + 1)
    for j in range(STEP):
        m = pe.matmul(c.part[k][:, j // 2, j % 2 * CELLS:(j % 2 + 1) * CELLS], c.lane[:, k, j, :], c.cell[:, k, j, :],
                      start=True, stop=True)
    m.then_inc(c.part_ready, 1)


def counts_scalar_prime(act, c):
    act.sem_inc(c.copied, 4)
    act.sem_inc(c.flushed, 16)


def lanes_scalar(act, g, c, r, k):
    if k == 0:
        act.copy(c.lane_now[:], g.minus_lane_col[:, bass.ds((r * 2 + c.first_round) * ROUND, 2 * ROUND)]).then_inc(c.lane_own, 1)
        act.wait_ge(c.lane_own, 1)
    for j in range(STEP):
        at = k * STEP + j
        m = act.activation(c.off[:, j, :], g.count_b[:, 0:P], ACT.Square, bias=c.lane_now[:, at:at + 1])
    m.then_inc(c.lane_own, 1)
    act.wait_ge(c.lane_own, 2 * k + 2)
    act.activation(c.lane[:, k % 2], c.off[:], ACT.Relu, bias=g.one[:], scale=-1.0).then_inc(c.lane_own, 1)
    act.wait_ge(c.lane_own, 2 * k + 3)
    act.sem_inc(c.lane_ready, 1)
    if k == BODY - 1:
        act.sem_clear(c.lane_own)


def counts_scalar(act, g, c, r, k):
    wait(act, c.part_ready, r * BODY + k + 1)
    if k % 4 == 2:
        q = k // 4
        wait(act, c.flushed, r * 32 + 16 * q + 16)
        act.copy(g.windows[:, 1 - q, CELLS:].bitcast(F32), g.zeros[:])
    act.copy(g.got[:, k % 4, 0:2 * CELLS], c.part[k % 2][:, 0, 0:2 * CELLS])
    act.copy(g.got[:, k % 4, 2 * CELLS:], c.part[k % 2][:, 1, 0:CELLS]).then_inc(c.copied, 1)


def counts_sync(sp, g, c, last):
    rounds = CITEMS // ROUND // 2

    def flush(n, q, wait_for):
        wait_for(sp, c.flush_ready, n + 1)
        base = sp.value_load(g.base[0:1, bass.ds(n + c.first_round, 1)], min_val=0, max_val=WINS - 1)
        sp.dma_start(g.matrix_dram[:, bass.ds(base, ROUND), :].rearrange("p w c -> p (w c)"),
                     g.windows[:, q, 0:ROUND * CELLS]).then_inc(c.flushed, 16)
        wait_for(sp, c.flushed, n * 16 + 32)

    with sp.Fori(0, rounds // 2) as r:
        for q in range(2):
            flush(r * 2 + q, q, wait)
    if last:
        flush(rounds, 0, lambda eng, sem, value: eng.wait_ge(sem, value))


def window_starts(nc, g, items):
    return nc.values_load_multi_w_load_instructions(
        g.starts[0:1, items], engines=[mybir.EngineType.DVE], min_val=0, max_val=ROUND * CELLS,
        skip_runtime_bounds_check_because="from one item to the next the window goes up by at most one")[1]


def counts_vector(nc, dve, g, c, r, k, meanwhile=lambda j: None):
    step, q, two, four = r * BODY + k, k // 4, k % 2, k % 4
    if k == 0:
        c.n = 1
        dve.tensor_copy(c.cell_now[:], g.cell_col[:, bass.ds((r * 2 + c.first_round) * ROUND, 2 * ROUND)]).then_inc(c.own, 1)
    if four == 0:
        c.at = window_starts(nc, g, bass.ds((r * 2 + q + c.first_round) * ROUND, ROUND))
    wait(dve, c.copied, step + 3)
    if four == 0:
        c.n += 1
        dve.tensor_copy(g.windows[:, q, 0:CELLS], g.windows[:, 1 - q, bass.ds(c.at[0], CELLS)]).then_inc(c.own, 1)
    for j in range(STEP):
        i = four * STEP + j
        dve.wait_ge(c.own, c.n)
        to = g.windows[:, q, bass.ds(c.at[i], CELLS)] if i else g.windows[:, q, 0:CELLS]
        c.n += 1
        dve.tensor_tensor(to, to, g.got[:, four, j * CELLS:(j + 1) * CELLS], ALU.add).then_inc(c.own, 1)
        at = k * STEP + j
        if j < STEP - 1:
            meanwhile(j)
        m = dve.tensor_scalar(c.cell[:, two, j, :], g.count_b[:, 0:CELLS], c.cell_now[:, at:at + 1], None, ALU.is_equal)
    if four == 3:
        c.n += 1
        m.then_inc(c.own, 1)
        dve.wait_ge(c.own, c.n)
        dve.sem_inc(c.cell_ready, 1)
        dve.sem_inc(c.flush_ready, 1)
    else:
        m.then_inc(c.cell_ready, 1)


def counts_vector_last(nc, dve, g, c):
    dve.wait_ge(c.copied, STEPS + 4)
    at = window_starts(nc, g, slice(CITEMS, CITEMS + ROUND))
    dve.tensor_copy(g.windows[:, 0, 0:CELLS], g.windows[:, 1, bass.ds(at[0], CELLS)]).then_inc(c.own, 1)
    for i in range(ROUND):
        dve.wait_ge(c.own, i + 1)
        to = g.windows[:, 0, bass.ds(at[i], CELLS)] if i else g.windows[:, 0, 0:CELLS]
        j = i % STEP
        dve.tensor_tensor(to, to, g.got[:, i // STEP, j * CELLS:(j + 1) * CELLS], ALU.add).then_inc(c.own, 1)
    dve.wait_ge(c.own, ROUND + 1)
    dve.sem_inc(c.flush_ready, 1)


def gathers(pool, out, table, cols, idx, idx_ready, slot_read, landed):
    with pool.Fori(0, STEPS // BODY) as r:
        for k in range(BODY):
            step = r * BODY + k
            for read in slot_read:
                wait(pool, read, step + 1)
            if k % 4 == 0:
                pool.tensor_copy(idx[:, k // 4], cols[:, bass.ds(step * S, 4 * S)]).then_inc(idx_ready, 1)
                wait(pool, idx_ready, r * 2 + k // 4 + 1)
            for j in range(S):
                at = k % 4 * S + j
                pool.indirect_dma_start(
                    out=out[:, k % 4, j, :], out_offset=None, in_=table[:, :],
                    in_offset=bass.IndirectOffsetOnAxis(ap=idx[:, k // 4, at:at + 1], axis=0)).then_inc(landed[k % 4], 16)


def edge_products(nc, g, a):
    with Scope(nc, "prod") as s:
        idx = s.sb("idx", [P, 2, 4 * S], I32)
        xs = s.sb("xs", [P, 4, S, NODE])
        oh = s.sb("oh", [P, 2, S, P], BF16)
        ohT = s.sb("ohT", [P, 2, S, P])
        rel = s.sb("rel", [P, 2, S, R])
        prod = s.sb("prod", [P, 2, S, D])
        ws, wd = s.sb("ws", [P, 2, S, R * H]), s.sb("wd", [P, 2, S, R * H])
        turned = [s.ps(f"turned{k}", [P, S, P], BF16) for k in range(2)]
        xd = [s.ps(f"xd{k}", [P, S, P]) for k in range(2)]
        landed = [s.sem(f"landed{k}") for k in range(4)]
        idx_ready, slot_free, oh_ready, turn, ohT_ready, xd_ready, sq_taken, own, primed = (
            s.sem(n) for n in ("idx_ready", "slot_free", "oh_ready", "turn", "ohT_ready", "xd_ready", "sq_taken", "own",
                               "primed"))
        tiles = s.sb("tiles", [1, ITEMS + 2], I32)
        c = counts_scope(s, 0)
        block = s.block()
        OWN = 8

        @block.sync
        def _(sp):
            sp.dma_start(tiles[:, 0:ITEMS], g.tile0_dram[0:ITEMS].rearrange("(a n) -> a n", a=1)).then_inc(primed, 16)
            sp.wait_ge(primed, 17)
            counts_sync(sp, g, c, False)

        @block.gpsimd
        def _(pool):
            gathers(pool, xs, g.node_dram, g.src_col, idx, idx_ready, (slot_free, sq_taken), landed)

        @block.tensor
        def _(pe):
            pe.wait_ge(primed, 17)

            def turn_one_hots(slot):
                for j in range(S):
                    m = pe.transpose(turned[slot][:, j, :], oh[:, slot, j, :], g.ident_b[:])
                m.then_inc(turn, 1)

            def targets(slot, at):
                for j in range(2):
                    for h in range(2):
                        m = pe.matmul(xd[slot][:, 2 * j + h, 0:NODE], ohT[:, slot, 2 * j + h, :],
                                      g.node[:, bass.ds(at[j], 1), :].rearrange("p a d -> p (a d)"), start=True, stop=True)
                m.then_inc(xd_ready, 1)

            def tiles_of(items):
                return nc.values_load_multi_w_load_instructions(
                    tiles[0:1, items], engines=[mybir.EngineType.PE], min_val=0, max_val=NT - 1,
                    skip_runtime_bounds_check_because="an item's tile is a count of NT - 1 comparisons")[1]

            for k in range(2):
                pe.wait_ge(oh_ready, k + 1)
                turn_one_hots(k)
            pe.wait_ge(ohT_ready, 1)
            targets(0, tiles_of(slice(0, 2)))
            with pe.Fori(0, STEPS // 2) as r:
                at = tiles_of(bass.ds(r * 4 + 2, 4))
                for k in range(2):
                    step = r * 2 + k
                    wait(pe, oh_ready, step + 3)
                    turn_one_hots(k)
                    wait(pe, ohT_ready, step + 2)
                    targets(1 - k, at[2 * k:2 * k + 2])
                    counts_tensor(pe, c, step, k)

        @block.scalar
        def _(act):
            counts_scalar_prime(act, c)
            act.sem_inc(sq_taken, 4)
            for k in range(2):
                act.wait_ge(turn, k + 1)
                act.copy(ohT[:, k], turned[k][:]).then_inc(ohT_ready, 1)
            with act.Fori(0, STEPS // BODY) as r:
                for k in range(BODY):
                    step = r * BODY + k
                    two = k % 2
                    lanes_scalar(act, g, c, r, k)
                    wait(act, turn, step + 3)
                    act.copy(ohT[:, two], turned[two][:]).then_inc(ohT_ready, 1)
                    wait(act, landed[k % 4], r * 128 + (k // 4) * 64 + 64)
                    act.copy(a.s2[:, bass.ds(step * S, S)], xs[:, k % 4, :, D]).then_inc(sq_taken, 1)
                    counts_scalar(act, g, c, r, k)

        @block.vector
        def _(dve):
            def one_hot(slot, cols):
                dve.tensor_tensor(oh[:, slot], g.count[:].unsqueeze(1).to_broadcast([P, S, P]),
                                  g.lane_col[:, cols].unsqueeze(2).to_broadcast([P, S, P]), ALU.is_equal).then_inc(oh_ready, 1)

            dve.memset(tiles[:, ITEMS:], 0).then_inc(primed, 1)
            dve.sem_inc(slot_free, 4)
            for k in range(2):
                one_hot(k, slice(k * S, (k + 1) * S))
            dve.wait_ge(turn, 1)
            with dve.Fori(0, STEPS // BODY) as r:
                for k in range(BODY):
                    step = r * BODY + k
                    two, four = k % 2, k % 4
                    base = k * OWN
                    cols = bass.ds(step * S, S)
                    one_hot(two, bass.ds(step * S + 2 * S, S))
                    dve.tensor_tensor(rel[:, two], g.count[:, 0:R].unsqueeze(1).to_broadcast([P, S, R]),
                                      g.et_col[:, cols].unsqueeze(2).to_broadcast([P, S, R]), ALU.is_equal).then_inc(own, 1)
                    counts_vector(nc, dve, g, c, r, k)
                    wait(dve, landed[four], r * 128 + (k // 4) * 64 + 64)
                    dve.wait_ge(own, base + 1)
                    picked = rel[:, two].unsqueeze(3).to_broadcast([P, S, R, H])
                    dve.tensor_tensor(ws[:, two].rearrange("p j (r h) -> p j r h", r=R),
                                      xs[:, four, :, D + 1:NODE].rearrange("p j (r h) -> p j r h", r=R), picked,
                                      ALU.mult).then_inc(own, 1)
                    wait(dve, xd_ready, step + 1)
                    dve.tensor_tensor(prod[:, two], xd[two][:, :, 0:D], xs[:, four, :, 0:D], ALU.mult).then_inc(own, 1)
                    dve.tensor_tensor(wd[:, two].rearrange("p j (r h) -> p j r h", r=R),
                                      xd[two][:, :, D + 1:NODE].rearrange("p j (r h) -> p j r h", r=R), picked,
                                      ALU.mult).then_inc(own, 1)
                    dve.wait_ge(own, base + 2)
                    dve.tensor_reduce(a.ps[:, cols, :], ws[:, two].rearrange("p j (r h) -> p j h r", r=R), X,
                                      ALU.add).then_inc(own, 1)
                    dve.wait_ge(own, base + 3)
                    dve.tensor_reduce(a.gram[:, cols], prod[:, two], X, ALU.add).then_inc(own, 1)
                    dve.wait_ge(own, base + 4)
                    dve.tensor_reduce(a.pd[:, cols, :], wd[:, two].rearrange("p j (r h) -> p j h r", r=R), X,
                                      ALU.add).then_inc(own, 1)
                    dve.tensor_copy(a.d2[:, cols], xd[two][:, :, D]).then_inc(own, 1)
                    dve.wait_ge(own, base + 8)
                    dve.sem_inc(slot_free, 1)
                dve.sem_clear(own)
                dve.sem_clear(c.own)


def edge_weights(nc, g, a):
    with Scope(nc, "wts") as s:
        w0, w1, w2, w3, w4, w5 = (s.sb(n, [P, COLS]) for n in ("w0", "w1", "w2", "w3", "w4", "w5"))
        factors_ready, z_ready, pool_own, own, n2_ready, norm_ready, ratio_ready, log_ready = (
            s.sem(n) for n in ("factors_ready", "z_ready", "pool_own", "own", "n2_ready", "norm_ready", "ratio_ready",
                               "log_ready"))
        block = s.block()
        G, s2, d2 = a.gram[:], a.s2[:], a.d2[:]

        @block.gpsimd
        def _(pool):
            p = chain(pool, pool_own)
            pool.wait_ge(factors_ready, 1)
            p(pool.tensor_tensor(a.ps[:], a.ps[:], w0[:].unsqueeze(2).to_broadcast([P, COLS, H]), ALU.mult))
            p(pool.tensor_tensor(a.pd[:], a.pd[:], w1[:].unsqueeze(2).to_broadcast([P, COLS, H]), ALU.mult))
            p(pool.tensor_tensor(a.ps[:], a.ps[:], a.pd[:], ALU.subtract))
            pool.sem_inc(z_ready, 1)

        @block.scalar
        def _(act):
            atanh_ratio_scalar(act, G, w4[:], w5[:], n2_ready, norm_ready, ratio_ready, log_ready, 1)

        @block.vector
        def _(dve):
            v = chain(dve, own)
            v(dve.tensor_scalar(w0[:], G, -2 * C, 1.0, ALU.mult, ALU.add))
            v(dve.tensor_tensor(w1[:], s2, d2, ALU.mult))
            v(dve.scalar_tensor_tensor(w1[:], w1[:], C * C, w0[:], ALU.mult, ALU.add))
            v(dve.tensor_scalar(w1[:], w1[:], 1e-10, None, ALU.max))
            v(dve.reciprocal(w3[:], w1[:]))
            v(dve.scalar_tensor_tensor(w0[:], d2, C, w0[:], ALU.mult, ALU.add))
            v(dve.tensor_scalar(w1[:], s2, -C, 1.0, ALU.mult, ALU.add))
            v(dve.tensor_tensor(w0[:], w0[:], w3[:], ALU.mult))
            v(dve.tensor_tensor(w1[:], w1[:], w3[:], ALU.mult))
            dve.sem_inc(factors_ready, 1)
            v(dve.scalar_tensor_tensor(w2[:], G, -2.0, w0[:], ALU.mult, ALU.mult))
            v(dve.tensor_tensor(w2[:], w2[:], w1[:], ALU.mult))
            v(dve.tensor_tensor(w4[:], w0[:], w0[:], ALU.mult))
            v(dve.tensor_tensor(w4[:], w4[:], s2, ALU.mult))
            v(dve.tensor_tensor(w5[:], w1[:], w1[:], ALU.mult))
            v(dve.tensor_tensor(w5[:], w5[:], d2, ALU.mult))
            v(dve.tensor_tensor(w4[:], w4[:], w5[:], ALU.add))
            v(dve.tensor_tensor(G, w4[:], w2[:], ALU.add))
            atanh_ratio_vector(v, dve, G, w4[:], w5[:], w2[:], w3[:], n2_ready, norm_ready, ratio_ready, log_ready, 1)
            dve.wait_ge(z_ready, 1)
            v(dve.tensor_tensor(a.ps[:], a.ps[:], w3[:].unsqueeze(2).to_broadcast([P, COLS, H]), ALU.mult))
            v(dve.scalar_tensor_tensor(a.ps[:], a.ps[:], 0.2, a.ps[:], ALU.mult, ALU.max))

    SEQ = 8 * P
    BIG = -1e30
    with Scope(nc, "scan") as s:
        sc = s.sb("sc", [PI, H, SEQ])
        fwd, bwd = s.sb("fwd", [PI, H, SEQ]), s.sb("bwd", [PI, H, SEQ])
        kp, kc, kn = (s.sb(n, [PI, SEQ]) for n in ("kp", "kc", "kn"))
        ends = s.sb("ends", [PI, 4, H])
        chainT = s.sb("chainT", [H, 4, PI])
        carry = s.sb("carry", [H, 2, PI + 1])
        cin = s.sb("cin", [PI, 2, H])
        turned = [s.ps(f"turned{k}", [P, 4, P]) for k in range(2)]
        pe_ends = s.ps("ends_turned", [P, 512])
        loaded, turn, taken, own, ends_ready, endsT, carry_ready, carried, ex_ready, back, backed = (
            s.sem(n) for n in ("loaded", "turn", "taken", "own", "ends_ready", "endsT", "carry_ready", "carried",
                               "ex_ready", "back", "backed"))
        block = s.block()

        @block.sync
        def _(sp):
            for d, k in enumerate((kp, kc, kn)):
                sp.dma_start(k[:], g.key_dram[d:d + PI * SEQ].rearrange("(q n) -> q n", n=SEQ)).then_inc(loaded, 16)

        @block.tensor
        def _(pe):
            n = 0
            for h in range(H):
                for q in range(0, 8, 4):
                    if n >= 2:
                        pe.wait_ge(taken, n - 1)
                    for m in range(q, q + 4):
                        last = pe.transpose(turned[n % 2][0:PI, m - q, :], a.ps[:, m::8, h], g.ident[:])
                    last.then_inc(turn, 1)
                    n += 1
            for d in range(2):
                pe.wait_ge(ends_ready, d + 1)
                for b in range(2):
                    m = pe.transpose(pe_ends[0:H, b * P:b * P + PI], ends[:, 2 * d + b, :], g.ident[0:PI, 0:PI])
                m.then_inc(endsT, 1)
                pe.wait_ge(carry_ready, d + 1)
                c = carry[:, 0, 0:PI] if d == 0 else carry[:, 1, 1:PI + 1]
                pe.transpose(pe_ends[0:PI, 256:256 + H], c, g.ident[0:H, 0:H]).then_inc(carried, 1)
            n = 0
            pe.wait_ge(ex_ready, 1)
            pe.wait_ge(taken, 8)
            for h in range(H):
                for q in range(0, 8, 4):
                    if n >= 2:
                        pe.wait_ge(backed, n - 1)
                    for m in range(q, q + 4):
                        last = pe.transpose(turned[n % 2][:, m - q, 0:PI], sc[:, h, m * P:(m + 1) * P], g.ident[0:PI, 0:PI])
                    last.then_inc(back, 1)
                    n += 1

        @block.scalar
        def _(act):
            act.wait_ge(carry_ready, 3)
            act.activation(sc[:], sc[:], ACT.Exp).then_inc(ex_ready, 1)

        @block.vector
        def _(dve):
            v = chain(dve, own)
            n = 0
            for h in range(H):
                for q in range(0, 8, 4):
                    dve.wait_ge(turn, n + 1)
                    dve.tensor_copy(sc[:, h, q * P:(q + 4) * P].rearrange("p (m e) -> p m e", m=4), turned[n % 2][0:PI]).then_inc(taken, 1)
                    n += 1
            dve.wait_ge(taken, n)
            dve.wait_ge(loaded, 48)
            v(dve.tensor_tensor(kp[:], kp[:], kc[:], ALU.not_equal))
            v(dve.tensor_scalar(kp[:], kp[:], BIG, None, ALU.mult))
            v(dve.tensor_tensor(kn[:], kn[:], kc[:], ALU.not_equal))
            v(dve.tensor_scalar(kn[:], kn[:], BIG, None, ALU.mult))
            v(dve.memset(carry[:], BIG))
            for d, (brk, src, out) in enumerate(((kp, sc, fwd), (kn, fwd, bwd))):
                flip = (lambda t: t) if d == 0 else (lambda t: t[:, ::-1])
                last = SEQ - 1 if d == 0 else 0
                for h in range(H):
                    v(dve.tensor_tensor_scan(flip(out[:, h, :]), flip(brk[:]), flip(src[:, h, :]), BIG, ALU.add, ALU.max))
                v(dve.tensor_copy(ends[:, 2 * d, :], out[:, :, last]))
                v(dve.tensor_reduce(ends[:, 2 * d + 1, 0:1], brk[:], X, ALU.min))
                v(dve.tensor_copy(ends[:, 2 * d + 1, 1:H], ends[:, 2 * d + 1, 0:1].to_broadcast([PI, H - 1])))
                dve.sem_inc(ends_ready, 1)
                dve.wait_ge(endsT, d + 1)
                v(dve.tensor_copy(chainT[:, 2 * d:2 * d + 2, :], pe_ends[0:H, 0:2 * P].rearrange("p (b n) -> p b n", b=2)[:, :, 0:PI]))
                to = carry[:, 0, 1:PI + 1] if d == 0 else carry[:, 1, 0:PI]
                v(dve.tensor_tensor_scan(flip(to), flip(chainT[:, 2 * d + 1, :]), flip(chainT[:, 2 * d, :]), BIG, ALU.add, ALU.max))
                dve.sem_inc(carry_ready, 1)
                dve.wait_ge(carried, d + 1)
                v(dve.tensor_copy(cin[:, d, :], pe_ends[0:PI, 256:256 + H]))
                for h in range(H):
                    v(dve.tensor_tensor_scan(flip(out[:, h, :]), flip(brk[:]), flip(src[:, h, :]), cin[:, d, h:h + 1], ALU.add, ALU.max))
            v(dve.tensor_tensor(sc[:], sc[:], bwd[:], ALU.subtract))
            dve.sem_inc(carry_ready, 1)
            n = 0
            for h in range(H):
                for q in range(0, 8, 4):
                    dve.wait_ge(back, n + 1)
                    out = g.ex[:].rearrange("p (q m) h -> p m q h", m=8)[:, q:q + 4, :, h]
                    dve.tensor_copy(out, turned[n % 2][:, :, 0:PI]).then_inc(backed, 1)
                    n += 1
            dve.wait_ge(backed, n)


def edge_sums(nc, g):
    with Scope(nc, "sums") as s:
        SLOTS = 4
        idx = s.sb("idx", [P, 2, SLOTS * S], I32)
        msg = s.sb("msg", [P, SLOTS, S, MSG])
        val = s.sb("val", [P, 2, S, OUTC])
        oh = s.sb("oh", [P, 2, S, P])
        part = [s.ps(f"part{k}", [P, 2, 512]) for k in range(2)]
        tiles = s.sb("tiles", [1, ITEMS + 4], I32)
        landed = [s.sem(f"landed{k}") for k in range(SLOTS)]
        idx_ready, val_ready, part_ready, primed, own, cleared = (
            s.sem(n) for n in ("idx_ready", "val_ready", "part_ready", "primed", "own", "cleared"))
        c = counts_scope(s, CITEMS // ROUND // 2)
        block = s.block()

        @block.sync
        def _(sp):
            sp.wait_ge(cleared, 1)
            sp.dma_start(tiles[:, 4:], g.tile0_dram[0:ITEMS].rearrange("(a n) -> a n", a=1)).then_inc(primed, 16)
            sp.wait_ge(primed, 16)
            counts_sync(sp, g, c, True)

        @block.scalar
        def _(act):
            counts_scalar_prime(act, c)
            with act.Fori(0, STEPS // BODY) as r:
                for k in range(BODY):
                    lanes_scalar(act, g, c, r, k)
                    counts_scalar(act, g, c, r, k)

        @block.gpsimd
        def _(pool):
            gathers(pool, msg, g.msg_dram, g.msg_col, idx, idx_ready, (val_ready,), landed)

        @block.tensor
        def _(pe):
            with pe.Fori(0, STEPS // 2) as r:
                for k in range(2):
                    wait(pe, val_ready, r * 2 + k + SLOTS + 1)
                    for j in range(2):
                        for h in range(2):
                            m = pe.matmul(part[k][:, j, 0:OUTC], oh[:, k, 2 * j + h, :], val[:, k, 2 * j + h, :],
                                          start=(h == 0), stop=(h == 1))
                    m.then_inc(part_ready, 1)
                    counts_tensor(pe, c, r * 2 + k, k)

        @block.vector
        def _(dve):
            def tiles_of(items):
                return nc.values_load_multi_w_load_instructions(
                    tiles[0:1, items], engines=[mybir.EngineType.DVE], min_val=0, max_val=NT - 1,
                    skip_runtime_bounds_check_because="an item's tile is a count of NT - 1 comparisons")[1]

            def add(part, at, j, before):
                if before:
                    dve.wait_ge(own, before)
                to = g.sums[:, bass.ds(at[j], 1), :].rearrange("p a c -> p (a c)")
                dve.tensor_tensor(to, to, part[:, j, 0:OUTC], ALU.add).then_inc(own, 1)

            dve.memset(tiles[:, 0:4], 0).then_inc(cleared, 1)
            dve.memset(g.sums_flat[:], 0.0)
            dve.memset(val[:, :, :, MSG:OUTC], 1.0)
            for k in range(2):
                m = dve.memset(part[k][:], 0.0)
            m.then_inc(cleared, 1)
            dve.wait_ge(cleared, 2)
            dve.wait_ge(primed, 16)
            dve.sem_inc(val_ready, SLOTS)
            dve.sem_inc(part_ready, 2)
            with dve.Fori(0, STEPS // BODY) as r:
                for k in range(BODY):
                    step = r * BODY + k
                    cols = bass.ds(step * S, S)
                    h = k % 2
                    if k % 4 == 0:
                        at = tiles_of(bass.ds((r * BODY + k) * 2, 8))
                    wait(dve, part_ready, step + 1)
                    dve.tensor_tensor(oh[:, h], g.count[:].unsqueeze(1).to_broadcast([P, S, P]),
                                      g.lane_col[:, cols].unsqueeze(2).to_broadcast([P, S, P]), ALU.is_equal)
                    at2 = at[2 * (k % 4):2 * (k % 4) + 2]
                    counts_vector(nc, dve, g, c, r, k, lambda j: add(part[h], at2, j, 2 * k + j))
                    wait(dve, landed[k % 4], r * 128 + (k // 4) * 64 + 64)
                    dve.tensor_tensor(val[:, h, :, 0:MSG].rearrange("p j (h c) -> p j h c", h=H),
                                      msg[:, k % 4].rearrange("p j (h c) -> p j h c", h=H),
                                      g.ex[:, cols, :].unsqueeze(3).to_broadcast([P, S, H, HEAD]), ALU.mult).then_inc(val_ready, 1)
                dve.wait_ge(own, 2 * BODY)
                dve.sem_clear(own)
                dve.sem_clear(c.own)
            dve.wait_ge(part_ready, STEPS + 2)
            at = tiles_of(slice(ITEMS, ITEMS + 4))
            for n in range(4):
                add(part[n // 2], at[n // 2 * 2:n // 2 * 2 + 2], n % 2, n)
            dve.wait_ge(own, 4)
            counts_vector_last(nc, dve, g, c)


def items_matrix(nc, g, tile_of, rows):
    with Scope(nc, "cmi") as q:
        bits = q.sb("bits", [CI, CC, P], I32)
        lof, hif, win, inside = (q.sb(n, [CI, CC, P]) for n in ("lof", "hif", "win", "inside"))
        turned = [q.ps(f"turned{k}", [P, 4, P]) for k in range(2)]
        own, ready, turn, copied, cleared, loaded = (q.sem(n) for n in ("own", "ready", "turn", "copied", "cleared", "loaded"))
        block = q.block()
        jobs = [lof, hif]
        windows = q.sb("windows", [1, CITEMS + ROUND], I32)
        offset = q.sb("offset", [1, CITEMS + ROUND])

        @block.sync
        def _(sp):
            sp.wait_ge(cleared, 1)
            sp.dma_start(windows[:, ROUND:], g.tile1_dram[0:CITEMS].rearrange("(a n) -> a n", a=1)).then_inc(loaded, 16)
            sp.wait_ge(loaded, 16)

        @block.vector
        def _(dve):
            v = chain(dve, own)
            dve.memset(windows[:, 0:ROUND], 0).then_inc(cleared, 1)
            for a in (g.windows, g.got, g.zeros):
                v(dve.memset(a[:].rearrange("p a b -> p (a b)") if len(a.shape) > 2 else a[:], 0.0))
            v(dve.tensor_scalar(bits[:], rows[0][:], P - 1, None, ALU.bitwise_and))
            v(dve.tensor_copy(lof[:], bits[:]))
            v(dve.tensor_scalar(lof[:], lof[:], -1.0, None, ALU.mult))
            v(dve.tensor_scalar(bits[:], rows[0][:], 7, None, ALU.logical_shift_right))
            v(dve.tensor_copy(hif[:], bits[:]))
            v(dve.tensor_scalar(tile_of[:], tile_of[:], float(WIN), None, ALU.mult))
            v(dve.tensor_copy(win[:], rows[1][:]))
            v(dve.tensor_tensor(win[:], win[:], tile_of[:].unsqueeze(2).to_broadcast([CI, CC, P]), ALU.subtract))
            v(dve.scalar_tensor_tensor(hif[:], win[:], float(NT), hif[:], ALU.mult, ALU.add))
            v(dve.tensor_scalar(inside[:], win[:], 0.0, None, ALU.is_ge))
            v(dve.scalar_tensor_tensor(inside[:], win[:], float(WIN), inside[:], ALU.is_lt, ALU.mult))
            v(dve.scalar_tensor_tensor(hif[:], hif[:], 1.0, inside[:], ALU.add, ALU.mult))
            v(dve.tensor_scalar(hif[:], hif[:], -1.0, None, ALU.add))
            dve.sem_inc(ready, 1)
            n = 0
            for col in (g.minus_lane_col, g.cell_col):
                for c in range(0, CC, 4):
                    n += 1
                    dve.wait_ge(turn, n)
                    dve.tensor_copy(col[:, c * CI:(c + 4) * CI].rearrange("p (c i) -> p c i", c=4),
                                    turned[(n - 1) % 2][:, :, 0:CI]).then_inc(copied, 1)
            dve.wait_ge(loaded, 16)
            dve.wait_ge(copied, n)
            rounds = CITEMS // ROUND + 1
            v(dve.tensor_copy(g.base[:], windows[:, ::ROUND]))
            at, off = (a[:].rearrange("a (n i) -> a n i", i=ROUND) for a in (windows, offset))
            v(dve.tensor_tensor(off, at, g.base[:].unsqueeze(2).to_broadcast([1, rounds, ROUND]), ALU.subtract))
            v(dve.tensor_tensor(off[:, 1:, 0], g.base[:, 1:], g.base[:, 0:rounds - 1], ALU.subtract))
            v(dve.tensor_scalar(g.starts[:], offset[:], float(CELLS), None, ALU.mult))

        @block.tensor
        def _(pe):
            pe.wait_ge(ready, 1)
            n = 0
            for arr in jobs:
                for c in range(0, CC, 4):
                    if n >= 2:
                        pe.wait_ge(copied, n - 1)
                    for j in range(4):
                        m = pe.transpose(turned[n % 2][:, j, 0:CI], arr[:, c + j, :], g.ident[0:CI, 0:CI])
                    m.then_inc(turn, 1)
                    n += 1


def finish_layer0(nc, g):
    with Scope(nc, "fin0") as s:
        CHUNKS = 10
        BY_VECTOR = 10
        cuts = [WINS * k // CHUNKS * WIN for k in range(CHUNKS + 1)]
        sq = s.sb("sq", [P, NT, D])
        inv, den, coef, n2, t, w1, w2, f = (s.sb(n, [P, NT, H]) for n in ("inv", "den", "coef", "n2", "t", "w1", "w2", "f"))
        a2, nrm, th = (s.sb(n, [P, NT]) for n in ("a2", "nrm", "th"))
        st = g.st
        counts = s.sb("counts", [P, CHUNKS, NT])
        deg, m, r = s.sb("deg", [P, 2, NT]), s.sb("m", [P, 2, NT]), s.sb("r", [P, 2, NT])
        junk = s.ps("junk", [P, 512])
        loaded = [s.sem(f"loaded{k}") for k in range(CHUNKS)]
        own, n2_ready, norm_ready, ratio_ready, log_ready, a2_ready, root, tanh_done, var_ready, root_ready, shrink_ready = (
            s.sem(n) for n in ("own", "n2_ready", "norm_ready", "ratio_ready", "log_ready", "a2_ready", "root",
                               "tanh_done", "var_ready", "root_ready", "shrink_ready"))
        summed, cleared, deg_ready, deg_root = (s.sem(n) for n in ("summed", "cleared", "deg_ready", "deg_root"))
        block = s.block()
        heads = g.sums[:, :, 0:MSG].rearrange("p t (h c) -> p t h c", h=H)
        h_new = heads[:, :, 0, 0:D]

        @block.sync
        def _(sp):
            for k in range(CHUNKS):
                sp.dma_start(g.matrix[:, cuts[k]:cuts[k + 1]].rearrange("p n t -> p (n t)"),
                             g.matrix_dram[:, cuts[k] // WIN:cuts[k + 1] // WIN, :].rearrange("p w c -> p (w c)")).then_inc(loaded[k], 16)
            for k in range(CHUNKS):
                sp.wait_ge(loaded[k], 16)

        @block.scalar
        def _(act):
            def add_counts(chunks):
                for k in chunks:
                    act.wait_ge(loaded[k], 16)
                    for i in range(BY_VECTOR, NT):
                        act.activation(junk[:, 0:cuts[k + 1] - cuts[k]], g.matrix[:, cuts[k]:cuts[k + 1], i], ACT.Copy,
                                       accum_out=counts[:, k, i:i + 1]).then_inc(summed, 1)
                        act.wait_ge(summed, k * (NT - BY_VECTOR) + i - BY_VECTOR + 1)

            add_counts([0, 1])
            atanh_ratio_scalar(act, n2[:], t[:], w1[:], n2_ready, norm_ready, ratio_ready, log_ready, 1)
            act.wait_ge(n2_ready, 2)
            act.activation(w1[:], n2[:], ACT.Sqrt).then_inc(shrink_ready, 1)
            add_counts([2, 3])
            act.wait_ge(a2_ready, 1)
            act.activation(nrm[:], a2[:], ACT.Sqrt).then_inc(root, 1)
            act.wait_ge(root, 1)
            act.activation(th[:], nrm[:], ACT.Tanh, scale=0.1).then_inc(tanh_done, 1)
            add_counts([4])
            layer_norm_scalar(act, st, var_ready, root_ready, 1)
            add_counts(range(5, CHUNKS))
            act.wait_ge(deg_ready, 1)
            act.activation(r[:], m[:], ACT.Sqrt).then_inc(deg_root, 1)

        @block.vector
        def _(dve):
            v = chain(dve, own)
            dve.memset(g.matrix[:, WINS * WIN:], 0.0).then_inc(cleared, 1)
            dve.wait_ge(cleared, 1)
            v(dve.tensor_scalar(inv[:], heads[:, :, :, D + 1], 0.5, None, ALU.max))
            v(dve.reciprocal(inv[:], inv[:]))
            v(dve.tensor_tensor(den[:], heads[:, :, :, D], inv[:], ALU.mult))
            v(dve.tensor_scalar(den[:], den[:], 1e-06, None, ALU.add))
            v(dve.reciprocal(coef[:], den[:]))
            v(dve.tensor_tensor(coef[:], coef[:], inv[:], ALU.mult))
            for h in range(H):
                v(dve.tensor_tensor(sq[:], heads[:, :, h, 0:D], coef[:, :, h:h + 1].to_broadcast([P, NT, D]), ALU.mult))
                v(dve.tensor_tensor(sq[:], sq[:], sq[:], ALU.mult))
                v(dve.tensor_reduce(n2[:, :, h], sq[:], X, ALU.add))
            atanh_ratio_vector(v, dve, n2[:], t[:], w1[:], w2[:], f[:], n2_ready, norm_ready, ratio_ready, log_ready, 1)
            v(dve.tensor_scalar(n2[:], n2[:], MAXNORM * MAXNORM, 1.0 / (MAXNORM * MAXNORM), ALU.max, ALU.mult))
            dve.sem_inc(n2_ready, 1)
            dve.wait_ge(shrink_ready, 1)
            v(dve.reciprocal(w2[:], w1[:]))
            v(dve.tensor_tensor(f[:], f[:], w2[:], ALU.mult))
            v(dve.scalar_tensor_tensor(coef[:], coef[:], 1.0 / H, f[:], ALU.mult, ALU.mult))
            bc = lambda a, h: a[:, :, h:h + 1].to_broadcast([P, NT, D])
            v(dve.tensor_tensor(h_new, h_new, bc(coef, 0), ALU.mult))
            for h in range(1, H):
                v(dve.tensor_tensor(sq[:], heads[:, :, h, 0:D], bc(coef, h), ALU.mult))
                v(dve.tensor_tensor(h_new, h_new, sq[:], ALU.add))
            v(dve.tensor_tensor(sq[:], h_new, h_new, ALU.mult))
            v(dve.tensor_reduce(a2[:], sq[:], X, ALU.add))
            v(dve.tensor_scalar(a2[:], a2[:], 1e-20, None, ALU.max))
            dve.sem_inc(a2_ready, 1)
            dve.wait_ge(tanh_done, 1)
            v(dve.reciprocal(a2[:], nrm[:]))
            v(dve.scalar_tensor_tensor(a2[:], a2[:], 10.0, th[:], ALU.mult, ALU.mult))
            v(dve.tensor_tensor(h_new, h_new, a2[:].unsqueeze(2).to_broadcast([P, NT, D]), ALU.mult))
            v(dve.tensor_tensor(g.x[:], g.x[:], h_new, ALU.add))
            v(dve.tensor_copy(g.deg_in[:], g.sums[:, :, MSG]))
            layer_norm_vector(v, dve, g.x[:], sq[:], st, var_ready, root_ready, 1)
            for k in range(CHUNKS):
                dve.wait_ge(loaded[k], 16)
                v(dve.tensor_reduce(counts[:, k, 0:BY_VECTOR], g.matrix[:, cuts[k]:cuts[k + 1], 0:BY_VECTOR].rearrange("p n t -> p t n"),
                                    X, ALU.add))
            dve.wait_ge(summed, CHUNKS * (NT - BY_VECTOR))
            v(dve.tensor_reduce(deg[:, 0, :], counts[:].rearrange("p k t -> p t k"), X, ALU.add))
            v(dve.tensor_copy(deg[:, 1, :], g.deg_in[:]))
            v(dve.tensor_scalar(m[:], deg[:], 1.0, None, ALU.max))
            dve.sem_inc(deg_ready, 1)
            v(dve.reciprocal(g.per_deg[:], m[:]))
            dve.wait_ge(deg_root, 1)
            v(dve.reciprocal(m[:], r[:]))
            v(dve.scalar_tensor_tensor(g.root_deg[:], deg[:], 0.0, m[:], ALU.is_gt, ALU.mult))


def graph_layer(nc, g, name, pre, reverse, scale_in, scale_out, w_dram, b_dram, relu, out=None):
    with Scope(nc, name) as s:
        has_w = w_dram is not None
        TURN = 5
        w = s.sb("w", [D, D])
        bias = s.sb("bias", [P, D])
        xT = s.sb("xT", [D, 4, P])
        feat = g.sums_flat[:, 0:NT * D].rearrange("p (t d) -> p t d", d=D)
        parts = g.sums_flat[:, NT * D:NT * D * 5 // 2].bitcast(BF16).rearrange("p (t b d) -> p t b d", b=3, d=D)
        agg = feat
        st = g.st
        flip = s.sb("flip", [P, 3, TURN, P], F16)
        px = s.ps("px", [P, 4, P])
        pw = s.ps("pw", [P, 4, D])
        pc = [s.ps(f"pc{k}", [P, 512]) for k in range(2)]
        pt = [s.ps(f"pt{k}", [P, 8, P], F16) for k in range(3)]
        loaded, own, parts_ready, summed, taken, var_ready, root_ready = (
            s.sem(n) for n in ("loaded", "own", "parts_ready", "summed", "taken", "var_ready", "root_ready"))
        if has_w:
            ready, turn, turned, multiplied = (s.sem(n) for n in ("ready", "turn", "turned", "multiplied"))
        if reverse:
            flipped, flip_turn = [s.sem(f"flipped{k}") for k in range(2)], s.sem("flip_turn")
        if out is not None:
            stored = s.sem("stored")
        block = s.block()
        bc = lambda a: a.unsqueeze(2).to_broadcast([P, NT, D])
        groups = list(range(0, NT, 4))
        jgroups = list(range(0, NT, TURN))
        steps = [(i, q) for i in range(NT) for q in jgroups]

        @block.sync
        def _(sp):
            if has_w:
                sp.dma_start(w[:], w_dram[:, :]).then_inc(loaded, 16)
                sp.dma_start(bias[:], b_dram.rearrange("(a n) -> a n", a=1).to_broadcast([P, D])).then_inc(loaded, 16)
                sp.wait_ge(loaded, 32)
            if out is not None:
                sp.wait_ge(stored, 1)
                sp.dma_start(out[0:FULL * P, :].rearrange("(t p) d -> p t d", p=P), g.x[:, 0:FULL, :]).then_inc(loaded, 16)
                sp.dma_start(out[FULL * P:N, :], g.x[0:REST, FULL, :]).then_inc(loaded, 16)
                sp.wait_ge(loaded, 32)

        @block.scalar
        def _(act):
            if reverse:
                for n in range(0, len(steps), 2):
                    k = min(TURN, NT - steps[n][1])
                    act.wait_ge(flip_turn, n + 1)
                    act.copy(flip[:, n % 3, 0:k, :], pt[n % 3][:, 0:k, :]).then_inc(flipped[0], 1)
            layer_norm_scalar(act, st, var_ready, root_ready, 1)

        def times_w_tensor(pe, src):
            pe.wait_ge(loaded, 32)
            pe.wait_ge(ready, 1)
            for n, q in enumerate(groups):
                k = min(4, NT - q)
                if n:
                    pe.wait_ge(multiplied, n)
                for i in range(k):
                    m = pe.transpose(px[0:D, i, :], src[:, q + i, :], g.ident[:])
                m.then_inc(turn, 1)
                pe.wait_ge(turned, n + 1)
                for i in range(k):
                    m = pe.matmul(pw[:, i, :], xT[:, i, :], w[:], start=True, stop=True)
                m.then_inc(turn, 1)

        def times_w_vector(dve, out):
            for n, q in enumerate(groups):
                k = min(4, NT - q)
                dve.wait_ge(turn, 2 * n + 1)
                dve.tensor_copy(xT[:, 0:k, :], px[0:D, 0:k, :]).then_inc(turned, 1)
                dve.wait_ge(turn, 2 * n + 2)
                dve.tensor_copy(out[:, q:q + k, :], pw[:, 0:k, :]).then_inc(multiplied, 1)
            dve.wait_ge(multiplied, len(groups))

        @block.tensor
        def _(pe):
            if pre:
                times_w_tensor(pe, g.x)
            pe.wait_ge(parts_ready, 1)
            n = 0
            if not reverse:
                for j in range(NT):
                    if j >= 2:
                        pe.wait_ge(taken, j - 1)
                    for i in range(NT):
                        m = pe.matmul(pc[j % 2][:, 0:3 * D], g.matrix[:, j * P:(j + 1) * P, i],
                                      parts[:, i].rearrange("p a d -> p (a d)"), start=(i == 0), stop=(i == NT - 1))
                    m.then_inc(summed, 1)
            else:
                def turn_group(n):
                    i, q = steps[n]
                    if n >= 3:
                        pe.wait_ge(flipped[(n - 3) % 2], (n - 3) // 2 + 1)
                    for j in range(q, min(q + TURN, NT)):
                        m = pe.transpose(pt[n % 3][:, j - q, :], g.matrix[:, j * P:(j + 1) * P, i], g.ident_h[:])
                    m.then_inc(flip_turn, 1)

                turn_group(0)
                turn_group(1)
                for n, (i, q) in enumerate(steps):
                    if n + 2 < len(steps):
                        turn_group(n + 2)
                    pe.wait_ge(flipped[n % 2], n // 2 + 1)
                    if q == 0 and i >= 2:
                        pe.wait_ge(taken, i - 1)
                    for j in range(q, min(q + TURN, NT)):
                        m = pe.matmul(pc[i % 2][:, 0:3 * D], flip[:, n % 3, j - q, :],
                                      parts[:, j].rearrange("p a d -> p (a d)"), start=(j == 0), stop=(j == NT - 1))
                    if q == jgroups[-1]:
                        m.then_inc(summed, 1)
            if has_w and not pre:
                times_w_tensor(pe, agg)

        @block.vector
        def _(dve):
            v = chain(dve, own)
            if pre:
                dve.sem_inc(ready, 1)
                times_w_vector(dve, feat)
                v(dve.tensor_tensor(feat, feat, bc(scale_in), ALU.mult))
            else:
                v(dve.tensor_tensor(feat, g.x[:], bc(scale_in), ALU.mult))
            for b in range(3):
                v(dve.tensor_copy(parts[:, :, b, :], feat))
                if b < 2:
                    v(dve.tensor_tensor(feat, feat, parts[:, :, b, :], ALU.subtract))
            dve.sem_inc(parts_ready, 1)
            for j in range(NT):
                if reverse:
                    for n, (i, q) in enumerate(steps):
                        if i == j and n % 2:
                            k = min(TURN, NT - q)
                            dve.wait_ge(flip_turn, n + 1)
                            dve.tensor_copy(flip[:, n % 3, 0:k, :], pt[n % 3][:, 0:k, :]).then_inc(flipped[1], 1)
                dve.wait_ge(summed, j + 1)
                dve.tensor_reduce(agg[:, j, :], pc[j % 2][:, 0:3 * D].rearrange("p (b d) -> p d b", b=3), X, ALU.add).then_inc(taken, 1)
            dve.wait_ge(taken, NT)
            v(dve.tensor_tensor(agg, agg, bc(scale_out), ALU.mult))
            if has_w and not pre:
                dve.sem_inc(ready, 1)
                times_w_vector(dve, agg)
            if has_w:
                v(dve.tensor_tensor(agg, agg, bias[:].unsqueeze(1).to_broadcast([P, NT, D]), ALU.add))
            if relu:
                v(dve.tensor_scalar(agg, agg, 0.0, None, ALU.max))
            v(dve.tensor_tensor(g.x[:], g.x[:], agg, ALU.add))
            layer_norm_vector(v, dve, g.x[:], agg, st, var_ready, root_ready, 1)
            if out is not None:
                dve.sem_inc(stored, 1)


class Shared:
    pass


def build(nc, x, src, dst, edge_type_8, rel_weight, attn_vec, rel_emb, W1, b1, W2, b2, out):
    g = Shared()
    g.x_in = x
    dram = lambda name, shape, dt=F32: nc.dram_tensor(name, shape, dt).ap()
    g.flat_src, g.flat_dst, g.flat_et = (dram(n, [EP], I32) for n in ("flat_src", "flat_dst", "flat_et"))
    g.key_dram = dram("keys", [ITEMS * PAIR + 2])
    g.node_dram = dram("node_table", [NP, NODE])
    g.msg_dram = dram("message_table", [NP * R, MSG])
    g.matrix_dram = dram("matrix", [P, WINS - 1 + ROUND, CELLS], F16)
    g.tile0_dram, g.tile1_dram = dram("tiles0", [ITEMS], I32), dram("tiles1", [CITEMS], I32)
    with Scope(nc, "g") as s:
        g.ident, g.ident_b, g.ident_h = s.sb("ident", [P, P]), s.sb("ident_b", [P, P], BF16), s.sb("ident_h", [P, P], F16)
        g.count, g.one, g.ones_b = s.sb("count", [P, P]), s.sb("one", [P, 1]), s.sb("ones_b", [P, P], BF16)
        g.count_b = s.sb("count_b", [P, 2 * P], BF16)
        g.x = s.sb("x", [P, NT, D])
        g.deg_in = s.sb("deg_in", [P, NT])
        g.per_deg, g.root_deg = s.sb("per_deg", [P, 2, NT]), s.sb("root_deg", [P, 2, NT])
        g.sums_flat = s.sb("sums", [P, NT * OUTC])
        g.sums = g.sums_flat[:].rearrange("p (t c) -> p t c", c=OUTC)
        constants(nc, g)
        stage_edges(nc, g, src, dst, edge_type_8)
        items = Scope(nc, "items")
        g.minus_lane_col, g.cell_col = items.sb("minus_lane_col", [P, CITEMS]), items.sb("cell_col", [P, CITEMS])
        g.starts, g.base = items.sb("starts", [1, CITEMS + ROUND], I32), items.sb("base", [1, CITEMS // ROUND + 1], I32)
        g.windows, g.got = items.sb("windows", [P, 2, SPAN * CELLS], F16), items.sb("got", [P, 4, STEP * CELLS], F16)
        g.zeros = items.sb("zeros", [P, ROUND * CELLS // 2])
        with Scope(nc, "l0") as l0:
            g.src_col, g.msg_col = (l0.sb(n, [P, COLS], I32) for n in ("src_col", "msg_col"))
            g.lane_col, g.et_col = l0.sb("lane_col", [P, COLS + 2 * S]), l0.sb("et_col", [P, COLS])
            g.ex = l0.sb("ex", [P, COLS, H])
            with Scope(nc, "l0n") as n0:
                g.node = n0.sb("node", [P, NT, NODE])
                with Scope(nc, "l0t") as t0:
                    xT, factor = t0.sb("xT", [D, NT, P]), t0.sb("factor", [P, NT])
                    with Scope(nc, "walks") as w:
                        tile1, tile_int1, row_int1 = walk(nc, g, w, "cmi", P, CI, CC, WIN, WINS)
                        tile0, tile_int0, row_int0 = walk(nc, g, w, "it0", PAIR, PI, PC, P, NT)
                        rows1 = [w.sb(f"{n}1", [CI, CC, P], I32) for n in ("src", "dst")]
                        rows0 = [w.sb(f"{n}0", [PI, PC, PAIR], I32) for n in ("src", "dst", "et")]
                        node_table(nc, g, attn_vec, xT, factor,
                                   [((g.flat_src, g.flat_dst), rows1, row_int1, CC, P),
                                    ((g.flat_src, g.flat_dst, g.flat_et), rows0, row_int0, PC, PAIR)],
                                   [(tile_int1, g.tile1_dram, CI), (tile_int0, g.tile0_dram, PI)])
                        items_matrix(nc, g, tile1, rows1)
                        items_layer0(nc, g, tile0, rows0)
                    message_table(nc, g, rel_weight, xT, factor)
                with Scope(nc, "l0a") as a0:
                    a = Shared()
                    a.s2, a.d2, a.gram = (a0.sb(n, [P, COLS]) for n in ("s2", "d2", "gram"))
                    a.ps, a.pd = a0.sb("ps", [P, COLS, H]), a0.sb("pd", [P, COLS, H])
                    edge_products(nc, g, a)
                    edge_weights(nc, g, a)
            edge_sums(nc, g)
        items.__exit__(None, None, None)
        clear_used_semaphores(nc)
        with Scope(nc, "m") as m:
            g.st = m.sb("st", [P, 2, NT])
            g.matrix = m.sb("matrix", [P, NP, NT], F16)
            finish_layer0(nc, g)
            deg_out, deg_in = 0, 1
            graph_layer(nc, g, "conv1", True, False, g.root_deg[:, deg_out], g.root_deg[:, deg_in], W1, b1, False)
            graph_layer(nc, g, "conv2", False, True, g.root_deg[:, deg_out], g.root_deg[:, deg_out], W2, b2, True)
            graph_layer(nc, g, "mean3", False, False, g.per_deg[:, deg_out], g.per_deg[:, deg_in], None, None, False, out)


_INS = ["x", "src", "dst", "edge_type_8", "L0_gnn_rel_weight", "L0_gnn_attn_vec", "L0_gnn_rel_emb", "L1_gnn_W",
        "L1_gnn_b", "L2_gnn_weight", "L2_gnn_bias"]


def kernel(**inputs):
    import numpy as _np
    import concourse.bacc as _bacc
    from concourse import mybir as _mybir
    from concourse.bass_utils import run_bass_kernel_spmd as _run

    nc = _bacc.Bacc("TRN2", target_bir_lowering=False, num_devices=1)
    arrays, args = {}, []
    for name in _INS:
        a = _np.ascontiguousarray(inputs[name])
        arrays[f"in_{name}"] = a
        args.append(nc.dram_tensor(f"in_{name}", a.shape, _mybir.dt.from_np(a.dtype), kind="ExternalInput").ap())
    args.append(nc.dram_tensor("out_0", (N, D), F32, kind="ExternalOutput").ap())
    build(nc, *args)
    r = _run(nc, [arrays], core_ids=[0])
    return r.results[0]["out_0"]
```
